# Optimizing a Trainium2 kernel written in Bass

```python
import numpy as np
import jax
import jax.numpy as jnp

def _softmax(x, axis=-1):
    return jax.nn.softmax(x, axis=axis)

def _gelu(x):
    return jax.nn.gelu(x, approximate=True)

def _silu(x):
    return jax.nn.silu(x)

def _sigmoid(x):
    return jax.nn.sigmoid(x)

def _layernorm(x, axis=-1, eps=1e-05):
    m = jnp.mean(x, axis=axis, keepdims=True)
    v = jnp.var(x, axis=axis, keepdims=True)
    return (x - m) / jnp.sqrt(v + eps)

def _scatter_add(tgt, idx, src, axis=0):
    return tgt.at[idx].add(src)

def _segment_sum(src, seg, n):
    return jax.ops.segment_sum(src, seg, n)
kernel_name = 'mk_seq_preln_d2_jaxref_r4_398adb'

def setup_inputs(seed: int=0):
    np.random.seed(seed)
    _w = jnp.asarray

    def _L0_attn_setup():
        import jax, jax.numpy as jnp
        import numpy as np
        B, L, D, H = (4, 1024, 256, 16)
        LN_EPS = 1e-05

        def _gated_delta_rule(q, k, v, lam, beta, d):

            def step(S, inp):
                k_t, v_t, q_t = inp
                S = lam * S
                u = beta * (v_t - jnp.einsum('kv,k->v', S, k_t))
                S = S + k_t[:, None] * u[None, :]
                o = jnp.einsum('kv,k->v', S, q_t)
                return (S, o)

            def scan_one(k_h, v_h, q_h):
                S0 = jnp.zeros((d, d), dtype=q.dtype)
                _, o = jax.lax.scan(step, S0, (k_h, v_h, q_h))
                return o
            return jax.vmap(scan_one)(k, v, q)
        key = jax.random.key(seed)
        k0, k1 = jax.random.split(key, 2)
        x = jax.random.normal(k0, (B, L, D), dtype=jnp.float32)
        W = jax.random.normal(k1, (D, D), dtype=jnp.float32) / jnp.sqrt(D).astype(jnp.float32)
        ln_gamma = jnp.ones((D,), dtype=jnp.float32)
        ln_beta = jnp.zeros((D,), dtype=jnp.float32)
        eta = jnp.asarray(0.01, dtype=jnp.float32)
        lam_logit = jnp.asarray(np.log(0.99) - np.log(0.01), dtype=jnp.float32)
        return {'x': x, 'W': W, 'ln_gamma': ln_gamma, 'ln_beta': ln_beta, 'eta': eta, 'lam_logit': lam_logit}
    _L0_attn_in = _L0_attn_setup()

    def _L0_ffn_setup():
        import jax, jax.numpy as jnp
        import numpy as np
        H = 256
        I = 128
        E = 8
        TOPK = 2
        NGROUP = 4
        TOPKG = 2
        SCALE = 1.0
        B, S = (4, 256)

        def _gate(xf, gate_weight, bias):
            T = xf.shape[0]
            logits = xf @ gate_weight.T
            scores = jax.nn.sigmoid(logits)
            scores_for_choice = scores + bias[None, :]
            gsz = E // NGROUP
            grp = scores_for_choice.reshape(T, NGROUP, gsz)
            group_scores = jax.lax.top_k(grp, 2)[0].sum(-1)
            _, group_idx = jax.lax.top_k(group_scores, TOPKG)
            rows = jnp.arange(T)[:, None]
            group_mask = jnp.zeros((T, NGROUP), xf.dtype).at[rows, group_idx].set(1.0)
            score_mask = jnp.broadcast_to(group_mask[:, :, None], (T, NGROUP, gsz)).reshape(T, E)
            tmp_scores = jnp.where(score_mask > 0, scores_for_choice, 0.0)
            _, topk_idx = jax.lax.top_k(tmp_scores, TOPK)
            topk_weight = jnp.take_along_axis(scores, topk_idx, axis=1)
            if TOPK > 1:
                topk_weight = topk_weight / (topk_weight.sum(-1, keepdims=True) + 1e-20)
            topk_weight = topk_weight * SCALE
            return (topk_idx, topk_weight)
        key = jax.random.key(seed)
        k0, k1, k2, k3, k4 = jax.random.split(key, 5)
        return {'hidden_states': jax.random.normal(k0, (B, S, H), jnp.float32), 'gate_weight': jax.random.normal(k1, (E, H), jnp.float32) * (1.0 / np.sqrt(H)), 'e_score_correction_bias': jnp.zeros((E,), jnp.float32), 'gate_proj': jax.random.normal(k2, (E, I, H), jnp.float32) * 0.02, 'up_proj': jax.random.normal(k3, (E, I, H), jnp.float32) * 0.02, 'down_proj': jax.random.normal(k4, (E, H, I), jnp.float32) * 0.02}
    _L0_ffn_in = _L0_ffn_setup()

    def _L1_attn_setup():
        import jax, jax.numpy as jnp
        import numpy as np
        B, T, E, H = (2, 512, 256, 16)
        D = E // H
        key = jax.random.key(seed)
        k = jax.random.split(key, 6)
        return {'x': jax.random.normal(k[0], (B, T, E), dtype=jnp.float32), 'w_att_val': jax.random.normal(k[1], (H, D, D), dtype=jnp.float32) * (6.0 / D) ** 0.5, 'wv_w': jax.random.normal(k[2], (E, E), dtype=jnp.float32) * E ** (-0.5), 'wv_b': jnp.zeros((E,), dtype=jnp.float32), 'out_w': jax.random.normal(k[3], (E, E), dtype=jnp.float32) * E ** (-0.5), 'out_b': jnp.zeros((E,), dtype=jnp.float32)}
    _L1_attn_in = _L1_attn_setup()

    def _L1_ffn_setup():
        import jax, jax.numpy as jnp
        import numpy as np
        DIM = 256
        HIDDEN = 768
        SCALE = 1.0 / 127.0

        def _dequant(w_int, dtype):
            return w_int.astype(dtype) * jnp.asarray(SCALE, dtype)
        key = jax.random.key(seed)
        k_x, k_g, k_u, k_d = jax.random.split(key, 4)
        x = jax.random.normal(k_x, (4, 512, DIM), dtype=jnp.float32)
        w_gate = jax.random.randint(k_g, (HIDDEN, DIM), -127, 128, dtype=jnp.int32)
        w_up = jax.random.randint(k_u, (HIDDEN, DIM), -127, 128, dtype=jnp.int32)
        w_down = jax.random.randint(k_d, (DIM, HIDDEN), -127, 128, dtype=jnp.int32)
        return {'x': x, 'w_gate': w_gate, 'w_up': w_up, 'w_down': w_down}
    _L1_ffn_in = _L1_ffn_setup()
    _d = {'L0_attn_x': _L0_attn_in['x'], 'L0_attn_W': _L0_attn_in['W'], 'L0_attn_ln_gamma': _L0_attn_in['ln_gamma'], 'L0_attn_ln_beta': _L0_attn_in['ln_beta'], 'L0_attn_eta': _L0_attn_in['eta'], 'L0_attn_lam_logit': _L0_attn_in['lam_logit'], 'L0_ffn_gate_weight': _L0_ffn_in['gate_weight'], 'L0_ffn_e_score_correction_bias': _L0_ffn_in['e_score_correction_bias'], 'L0_ffn_gate_proj': _L0_ffn_in['gate_proj'], 'L0_ffn_up_proj': _L0_ffn_in['up_proj'], 'L0_ffn_down_proj': _L0_ffn_in['down_proj'], 'L1_attn_w_att_val': _L1_attn_in['w_att_val'], 'L1_attn_wv_w': _L1_attn_in['wv_w'], 'L1_attn_wv_b': _L1_attn_in['wv_b'], 'L1_attn_out_w': _L1_attn_in['out_w'], 'L1_attn_out_b': _L1_attn_in['out_b'], 'L1_ffn_w_gate': _L1_ffn_in['w_gate'], 'L1_ffn_w_up': _L1_ffn_in['w_up'], 'L1_ffn_w_down': _L1_ffn_in['w_down']}
    _x0 = _d['L0_attn_x']
    _d['L0_attn_x'] = jax.random.normal(jax.random.fold_in(jax.random.key(seed), 1), (2, 2048, 256), dtype=_x0.dtype)
    del _x0
    return _d

def reference(L0_attn_x, L0_attn_W, L0_attn_ln_gamma, L0_attn_ln_beta, L0_attn_eta, L0_attn_lam_logit, L0_ffn_gate_weight, L0_ffn_e_score_correction_bias, L0_ffn_gate_proj, L0_ffn_up_proj, L0_ffn_down_proj, L1_attn_w_att_val, L1_attn_wv_w, L1_attn_wv_b, L1_attn_out_w, L1_attn_out_b, L1_ffn_w_gate, L1_ffn_w_up, L1_ffn_w_down):

    def _L0_attn_ref(x, W, ln_gamma, ln_beta, eta, lam_logit):
        import jax, jax.numpy as jnp
        import numpy as np
        B, L, D, H = (4, 1024, 256, 16)
        LN_EPS = 1e-05

        def _gated_delta_rule(q, k, v, lam, beta, d):

            def step(S, inp):
                k_t, v_t, q_t = inp
                S = lam * S
                u = beta * (v_t - jnp.einsum('kv,k->v', S, k_t))
                S = S + k_t[:, None] * u[None, :]
                o = jnp.einsum('kv,k->v', S, q_t)
                return (S, o)

            def scan_one(k_h, v_h, q_h):
                S0 = jnp.zeros((d, d), dtype=q.dtype)
                _, o = jax.lax.scan(step, S0, (k_h, v_h, q_h))
                return o
            return jax.vmap(scan_one)(k, v, q)
        Bx, Lx, Dx = x.shape
        d = Dx // H
        lam = jax.nn.sigmoid(lam_logit)
        beta = eta * (1.0 - lam) / d
        x_act = jnp.tanh(x)
        static_out = jnp.einsum('bld,ed->ble', x_act, W)

        def to_heads(t):
            return t.reshape(Bx, Lx, H, d).transpose(0, 2, 1, 3).reshape(Bx * H, Lx, d)
        q = to_heads(x_act)
        k = q
        v = to_heads(static_out)
        o = _gated_delta_rule(q, k, v, lam, beta, d)
        o_dyn = o.reshape(Bx, H, Lx, d).transpose(0, 2, 1, 3).reshape(Bx, Lx, Dx)
        y = static_out + o_dyn
        mu = jnp.mean(y, axis=-1, keepdims=True)
        var = jnp.mean(jnp.square(y - mu), axis=-1, keepdims=True)
        return (y - mu) * jax.lax.rsqrt(var + LN_EPS) * ln_gamma + ln_beta

    def _L0_ffn_ref(hidden_states, gate_weight, e_score_correction_bias, gate_proj, up_proj, down_proj):
        import jax, jax.numpy as jnp
        import numpy as np
        H = 256
        I = 128
        E = 8
        TOPK = 2
        NGROUP = 4
        TOPKG = 2
        SCALE = 1.0
        B, S = (4, 256)

        def _gate(xf, gate_weight, bias):
            T = xf.shape[0]
            logits = xf @ gate_weight.T
            scores = jax.nn.sigmoid(logits)
            scores_for_choice = scores + bias[None, :]
            gsz = E // NGROUP
            grp = scores_for_choice.reshape(T, NGROUP, gsz)
            group_scores = jax.lax.top_k(grp, 2)[0].sum(-1)
            _, group_idx = jax.lax.top_k(group_scores, TOPKG)
            rows = jnp.arange(T)[:, None]
            group_mask = jnp.zeros((T, NGROUP), xf.dtype).at[rows, group_idx].set(1.0)
            score_mask = jnp.broadcast_to(group_mask[:, :, None], (T, NGROUP, gsz)).reshape(T, E)
            tmp_scores = jnp.where(score_mask > 0, scores_for_choice, 0.0)
            _, topk_idx = jax.lax.top_k(tmp_scores, TOPK)
            topk_weight = jnp.take_along_axis(scores, topk_idx, axis=1)
            if TOPK > 1:
                topk_weight = topk_weight / (topk_weight.sum(-1, keepdims=True) + 1e-20)
            topk_weight = topk_weight * SCALE
            return (topk_idx, topk_weight)
        Bv, Sv, Hv = hidden_states.shape
        xf = hidden_states.reshape(-1, Hv).astype(jnp.float32)
        topk_idx, topk_weight = _gate(xf, gate_weight.astype(jnp.float32), e_score_correction_bias.astype(jnp.float32))
        y = jnp.zeros_like(xf)
        for e in range(E):
            combine_w = jnp.where(topk_idx == e, topk_weight, 0.0).sum(-1)
            g = xf @ gate_proj[e].T
            u = xf @ up_proj[e].T
            o = jax.nn.silu(g) * u @ down_proj[e].T
            y = y + combine_w[:, None] * o
        return y.reshape(Bv, Sv, Hv)

    def _L1_attn_ref(x, w_att_val, wv_w, wv_b, out_w, out_b):
        import jax, jax.numpy as jnp
        import numpy as np
        B, T, E, H = (2, 512, 256, 16)
        D = E // H
        b, t, e = x.shape
        h, d, _ = w_att_val.shape
        x_h = x.reshape(b, t, h, d).transpose(0, 2, 1, 3)
        xw = jnp.einsum('bhtd,hde->bhte', x_h, w_att_val)
        att = jnp.einsum('bhte,bhse->bhts', xw, x_h) / jnp.sqrt(jnp.asarray(d, x.dtype))
        att = jax.nn.softmax(att, axis=-1)
        vx = x @ wv_w.T + wv_b
        vx = vx.reshape(b, t, h, d).transpose(0, 2, 1, 3)
        o = jnp.einsum('bhts,bhsd->bhtd', att, vx)
        o = o.transpose(0, 2, 1, 3).reshape(b, t, e)
        return o @ out_w.T + out_b

    def _L1_ffn_ref(x, w_gate, w_up, w_down):
        import jax, jax.numpy as jnp
        import numpy as np
        DIM = 256
        HIDDEN = 768
        SCALE = 1.0 / 127.0

        def _dequant(w_int, dtype):
            return w_int.astype(dtype) * jnp.asarray(SCALE, dtype)
        wg = _dequant(w_gate, x.dtype)
        wu = _dequant(w_up, x.dtype)
        wd = _dequant(w_down, x.dtype)
        gate = jnp.einsum('bsd,hd->bsh', x, wg)
        up = jnp.einsum('bsd,hd->bsh', x, wu)
        h = jax.nn.silu(gate) * up
        return jnp.einsum('bsh,dh->bsd', h, wd)
    x = L0_attn_x
    x = x + _L0_attn_ref(_layernorm(x, axis=-1), L0_attn_W, L0_attn_ln_gamma, L0_attn_ln_beta, L0_attn_eta, L0_attn_lam_logit)
    x = x + _L0_ffn_ref(_layernorm(x, axis=-1), L0_ffn_gate_weight, L0_ffn_e_score_correction_bias, L0_ffn_gate_proj, L0_ffn_up_proj, L0_ffn_down_proj)
    x = x + _L1_attn_ref(_layernorm(x, axis=-1), L1_attn_w_att_val, L1_attn_wv_w, L1_attn_wv_b, L1_attn_out_w, L1_attn_out_b)
    x = x + _L1_ffn_ref(_layernorm(x, axis=-1), L1_ffn_w_gate, L1_ffn_w_up, L1_ffn_w_down)
    return x

_drawn_inputs = setup_inputs


def setup_inputs(seed=0):
    import zlib

    import numpy as np

    out = dict(_drawn_inputs(seed))
    spreads = {'L0_attn_ln_gamma': (1.0, 0.2),
     'L0_attn_ln_beta': (0.0, 0.1),
     'L0_ffn_e_score_correction_bias': (0.0, 0.8),
     'L1_attn_wv_b': (0.0, 0.1),
     'L1_attn_out_b': (0.0, 0.1)}
    factors = {'L0_ffn_gate_weight': 7.122,
     'L0_ffn_gate_proj': 6.071,
     'L0_ffn_up_proj': 5.973,
     'L0_ffn_down_proj': 6.006}
    for name, (base, spread) in spreads.items():
        noise = np.random.default_rng([zlib.crc32(name.encode()), seed]).standard_normal(out[name].shape)
        drawn = base * np.exp(spread * noise) if base else spread * noise
        out[name] = jnp.asarray(drawn.astype(out[name].dtype))
    for name, factor in factors.items():
        out[name] = (out[name] * factor).astype(out[name].dtype)
    return out
```

```python
import numpy as np
import concourse.bass as bass
from concourse import mybir
from contextlib import ExitStack

P = 128
ALU = mybir.AluOpType
ACT = mybir.ActivationFunctionType
AX = mybir.AxisListType
F32 = mybir.dt.float32
BF16 = mybir.dt.bfloat16
I32 = mybir.dt.int32

B, L, D, H = 2, 2048, 256, 16
d = D // H
BL = B * L
NT = BL // P
TPB = L // P
KC = D // P
GT = 4
NG = NT // GT
GTOK = GT * P
EPS = 1e-5

C = 8
VG = 4
VW = d // VG
NQ = L // (P // (B * H))
QB = NQ // C
SEG = 256
NSEG = L // SEG
QT = SEG // 4
QBLK = QT // C
SR = SEG // 4

NE, I_E = 8, 128
NGRP = 4
HID = 768
HC = HID // P
FSCALE = 1.0 / 127.0

MAGIC = float(0x5F3759DF)


class Chain:

    def __init__(self, eng, sem):
        self.eng, self.sem, self.n = eng, sem, 0

    def link(self, ins):
        self.n += 1
        ins.then_inc(self.sem, 1)
        self.eng.wait_ge(self.sem, self.n)

    def clear(self):
        self.eng.sem_clear(self.sem)
        self.n = 0


def rstd(dve, ch, mv, ve, ti, tj, t, rs, nm):
    ch.link(dve.tensor_scalar(ve, mv[:, :, 1], EPS, None, ALU.add))
    ch.link(dve.tensor_scalar(ti, ve.bitcast(I32), 1, None, ALU.arith_shift_right))
    ch.link(dve.tensor_scalar(tj, ti, -1.0, MAGIC, ALU.mult, ALU.add))
    r = tj.bitcast(F32)
    for step in range(3):
        ch.link(dve.tensor_tensor(t, r, r, ALU.mult))
        ch.link(dve.scalar_tensor_tensor(t, t, -0.5, ve, ALU.mult, ALU.mult))
        ch.link(dve.scalar_tensor_tensor(rs, t, 1.5, r, ALU.add, ALU.mult))
        r = rs
    return dve.scalar_tensor_tensor(nm, mv[:, :, 0], -1.0, rs, ALU.mult, ALU.mult)


def phase_a(nc, T, x_in, wT_in, kh, vh):
    X, ident = T["X"], T["ident"]
    with ExitStack() as c:
        sb = lambda n, s, dt=F32: c.enter_context(nc.sbuf_tensor("a_" + n, s, dt))
        sem = lambda n: c.enter_context(nc.semaphore("a_" + n))
        wT = sb("wT", [P, KC, D])
        st = sb("st", [P, NT, 6]); mv = sb("mv", [P, NT, 2])
        ve = sb("ve", [P, NT]); ti = sb("ti", [P, NT], I32); tj = sb("tj", [P, NT], I32); tt = sb("tt", [P, NT])
        rs = sb("rs", [P, NT]); nm = sb("nm", [P, NT])
        xa = sb("xa", [P, 2, GT, D]); xaT = sb("xaT", [P, 2, KC, GTOK]); vs = sb("vs", [P, 2, GT, D])
        psT = c.enter_context(nc.psum_tensor("a_psT", [P, 2, KC, GTOK], F32))
        psV = c.enter_context(nc.psum_tensor("a_psV", [P, 2, GT, D], F32))
        x_loaded = [sem(f"x_loaded{g}") for g in range(NG)]
        w_loaded = sem("w_loaded")
        chain = sem("chain"); stats = sem("stats")
        tanh_done = sem("tanh_done"); turned = sem("turned"); turned_kept = sem("turned_kept")
        v_done = sem("v_done"); v_kept = sem("v_kept")
        k_stored = [sem(f"k_stored{i}") for i in range(2)]
        v_stored = [sem(f"v_stored{i}") for i in range(2)]
        block = c.enter_context(nc.Block())

        @block.sync
        def _(sp):
            xt = x_in.rearrange("(n p) c -> p n c", p=P)
            sp.dma_start(X[:, 0:GT], xt[:, 0:GT]).then_inc(x_loaded[0], 16)
            sp.dma_start(wT[:], wT_in.rearrange("(k p) n -> p k n", p=P)).then_inc(w_loaded, 16)
            sp.dma_start(ident[:], T["ident_in"]).then_inc(w_loaded, 16)
            for g in range(1, NG):
                sp.dma_start(X[:, GT * g:GT * (g + 1)], xt[:, GT * g:GT * (g + 1)]).then_inc(x_loaded[g], 16)
            with sp.Fori(0, NG // 2) as i:
                for par in range(2):
                    g = 2 * i + par
                    sp.wait_ge(tanh_done, g * GT + GT)
                    for j in range(GT):
                        t0 = g * GTOK + j * P
                        sp.dma_start(kh[:, bass.ds(t0, P), :].rearrange("h t e -> t h e"),
                                     xa[:, par, j].rearrange("p (h e) -> p h e", h=H)).then_inc(k_stored[par], 16)
                    sp.wait_ge(v_kept, g + 1)
                    for j in range(GT):
                        t0 = g * GTOK + j * P
                        sp.dma_start(vh[:, bass.ds(t0, P), :].rearrange("h t e -> t h e"),
                                     vs[:, par, j].rearrange("p (h e) -> p h e", h=H)).then_inc(v_stored[par], 16)
            for par in range(2):
                sp.wait_ge(k_stored[par], NG // 2 * GT * 16 + GT * 16)
                sp.wait_ge(v_stored[par], NG // 2 * GT * 16 + GT * 16)

        @block.vector
        def _(dve):
            for par in range(2):
                dve.sem_inc(v_stored[par], GT * 16)
            ch = Chain(dve, chain)
            for g in range(NG):
                dve.wait_ge(x_loaded[g], 16)
                for n in range(GT * g, GT * g + GT):
                    last = nc.vector.bn_stats(st[:, n], X[:, n])
                ch.link(last)
                for n in range(GT * g, GT * g + GT):
                    last = nc.vector.bn_aggr(mv[:, n], st[:, n])
            ch.link(last)
            rstd(nc.vector, ch, mv[:], ve[:], ti[:], tj[:], tt[:], rs[:], nm[:]).then_inc(stats, 1)
            with dve.Fori(0, NG // 2) as i:
                for par in range(2):
                    g = 2 * i + par
                    dve.wait_ge(turned, g + 1)
                    nc.vector.tensor_copy(xaT[:, par], psT[:, par]).then_inc(turned_kept, 1)
                    dve.wait_ge(v_done, g + 1)
                    dve.wait_ge(v_stored[par], i * (GT * 16) + GT * 16)
                    nc.vector.tensor_copy(vs[:, par], psV[:, par]).then_inc(v_kept, 1)

        @block.scalar
        def _(act):
            for par in range(2):
                act.sem_inc(k_stored[par], GT * 16)
            act.wait_ge(stats, 1)
            with act.Fori(0, NG // 2) as i:
                for par in range(2):
                    g = 2 * i + par
                    act.wait_ge(k_stored[par], i * (GT * 16) + GT * 16)
                    act.wait_ge(turned_kept, g + 1)
                    for j in range(GT):
                        n = g * GT + j
                        nc.scalar.activation(xa[:, par, j], X[:, bass.ds(n, 1), :].rearrange("p a c -> p (a c)"), ACT.Tanh,
                                             bias=nm[:, bass.ds(n, 1)], scale=rs[:, bass.ds(n, 1)]).then_inc(tanh_done, 1)

        @block.tensor
        def _(pe):
            pe.sem_inc(turned_kept, 2)
            pe.wait_ge(w_loaded, 32)
            with pe.Fori(0, NG // 2) as i:
                for par in range(2):
                    g = 2 * i + par
                    pe.wait_ge(tanh_done, g * GT + GT)
                    pe.wait_ge(turned_kept, g + 1)
                    for k in range(KC):
                        for j in range(GT):
                            last = nc.tensor.transpose(psT[:, par, k, j * P:(j + 1) * P],
                                                       xa[:, par, j, k * P:(k + 1) * P], ident[:])
                    last.then_inc(turned, 1)
                    pe.wait_ge(turned_kept, g + 3)
                    for j in range(GT):
                        for k in range(KC):
                            last = nc.tensor.matmul(psV[:, par, j], xaT[:, par, k, j * P:(j + 1) * P], wT[:, k],
                                                    start=(k == 0), stop=(k == KC - 1))
                    last.then_inc(v_done, 1)


def head_quarters(ap, b):
    return ap[:, b * L:(b + 1) * L].rearrange("h (q t) e -> h q (t e)", q=L // NQ)


def phase_b(nc, T, eta_in, logit_in, kh, vh, kd, kt, tm, vg, w1):
    lam_c = T["lam_c"]
    with ExitStack() as c:
        sb = lambda n, s, dt=F32: c.enter_context(nc.sbuf_tensor("b_" + n, s, dt))
        sem = lambda n: c.enter_context(nc.semaphore("b_" + n))
        Kq = sb("Kq", [P, NQ, d]); Vq = sb("Vq", [P, NQ, d]); S1 = sb("S1", [P, NQ * d])
        prod = sb("prod", [P, 2, 4096])
        N = sb("N", [P, QB, C, C]); Tm = sb("Tm", [P, QB, C, C])
        ksq = sb("ksq", [P, NQ])
        s_in = sb("s_in", [P, 2]); s_t = sb("s_t", [P, 4])
        pw = sb("pw", [P, C]); pwK = sb("pwK", [P, C]); cN = sb("cN", [P, C, C])
        scal_loaded = sem("scal_loaded"); k_loaded = sem("k_loaded"); v_loaded = sem("v_loaded")
        chain = sem("chain"); pchain = sem("pchain")
        expz = sem("expz"); zeroed = sem("zeroed")
        prod_ready = sem("prod_ready"); prod_used = sem("prod_used")
        vg_ready = sem("vg_ready"); vg_stored = sem("vg_stored")
        kd_ready = sem("kd_ready"); kt_ready = sem("kt_ready"); tm_ready = sem("tm_ready"); w1_ready = sem("w1_ready")
        neg_z = sem("neg_z"); stored = sem("stored")
        block = c.enter_context(nc.Block())
        Kb = Kq[:].rearrange("p (n i) e -> p n i e", i=C)
        HB = QB // 2
        items = [(i, hf) for i in range(1, C) for hf in range(2)] + [(C, hf) for hf in range(2)]

        @block.sync
        def _(sp):
            sp.dma_start(s_in[:, 0:1], logit_in.to_broadcast([P, 1])).then_inc(scal_loaded, 16)
            sp.dma_start(s_in[:, 1:2], eta_in.to_broadcast([P, 1])).then_inc(scal_loaded, 16)
            for b in range(B):
                sp.dma_start(Kq[64 * b:64 * b + 64].rearrange("p t e -> p (t e)"), head_quarters(kh, b)).then_inc(k_loaded, 16)
            for b in range(B):
                sp.dma_start(Vq[64 * b:64 * b + 64].rearrange("p t e -> p (t e)"), head_quarters(vh, b)).then_inc(v_loaded, 16)
            sp.wait_ge(vg_ready, 1)
            for b in range(B):
                for g in range(VG):
                    dst = vg[:, g, b * L:(b + 1) * L].rearrange("h (q t) w -> h q (t w)", q=L // NQ)
                    sp.dma_start(dst, S1[64 * b:64 * b + 64, g * NQ * VW:(g + 1) * NQ * VW]).then_inc(vg_stored, 16)
            sp.wait_ge(kd_ready, 1)
            for b in range(B):
                sp.dma_start(head_quarters(kd, b), Vq[64 * b:64 * b + 64].rearrange("p t e -> p (t e)")).then_inc(stored, 16)
            sp.wait_ge(kt_ready, 1)
            for b in range(B):
                sp.dma_start(head_quarters(kt, b), S1[64 * b:64 * b + 64]).then_inc(stored, 16)
            sp.wait_ge(w1_ready, 1)
            for b in range(B):
                sp.dma_start(w1[:, b * L:(b + 1) * L].rearrange("h (q t) -> h q t", q=L // NQ), ksq[64 * b:64 * b + 64]).then_inc(stored, 16)
            sp.wait_ge(tm_ready, 1)
            for b in range(B):
                dst = tm[:, b * L // C:(b + 1) * L // C].rearrange("h (q n) m -> h q (n m)", q=L // NQ)
                sp.dma_start(dst, Tm[64 * b:64 * b + 64].rearrange("p n i j -> p (n i j)")).then_inc(stored, 16)
            sp.wait_ge(vg_stored, 16 * B * VG)
            sp.wait_ge(stored, 16 * B * 4)

        @block.scalar
        def _(act):
            act.wait_ge(scal_loaded, 32)
            nc.scalar.activation(s_t[:, 0:1], s_in[:, 0:1], ACT.Exp, scale=-1.0).then_inc(expz, 1)
            act.wait_ge(v_loaded, 32)
            nc.scalar.activation(S1[:].rearrange("p (g t w) -> p g t w", g=VG, w=VW),
                                 Vq[:].rearrange("p t (g w) -> p g t w", g=VG), ACT.Copy).then_inc(vg_ready, 1)

        @block.gpsimd
        def _(pool):
            nc.gpsimd.memset(N[:], 0.0).then_inc(pchain, 1)
            nc.gpsimd.memset(cN[:], 0.0).then_inc(pchain, 1)
            nc.gpsimd.memset(Tm[:], 0.0).then_inc(pchain, 1)
            pool.wait_ge(pchain, 3)
            nc.gpsimd.memset(Tm[:].rearrange("p n i j -> p n (i j)")[:, :, 0:C * C:C + 1], 1.0).then_inc(zeroed, 1)
            pool.wait_ge(k_loaded, 32)
            for m, (i, hf) in enumerate(items):
                if m >= 2:
                    pool.wait_ge(prod_used, m - 1)
                n0 = hf * HB
                if i < C:
                    o = prod[:, m % 2, 0:HB * i * d].rearrange("p (n j e) -> p n j e", n=HB, j=i)
                    a = Kb[:, n0:n0 + HB, i:i + 1].to_broadcast([P, HB, i, d])
                    bb = Kb[:, n0:n0 + HB, 0:i]
                else:
                    o = prod[:, m % 2].rearrange("p (n j e) -> p n j e", n=HB, j=C)
                    a = bb = Kb[:, n0:n0 + HB]
                nc.gpsimd.tensor_tensor(o, a, bb, ALU.mult).then_inc(prod_ready, 1)

        @block.vector
        def _(dve):
            v = nc.vector
            ch = Chain(dve, chain)
            dve.wait_ge(expz, 1)
            ch.link(v.tensor_scalar(s_t[:, 1:2], s_t[:, 0:1], 1.0, None, ALU.add))
            ch.link(v.reciprocal(pw[:, 0:1], s_t[:, 1:2]))
            ch.link(v.tensor_scalar(s_t[:, 2:3], pw[:, 0:1], -1.0, 1.0, ALU.mult, ALU.add))
            ch.link(v.scalar_tensor_tensor(pwK[:, C - 1:C], s_t[:, 2:3], 1.0 / d, s_in[:, 1:2], ALU.mult, ALU.mult))
            for n in range(1, C):
                v.tensor_tensor(pw[:, n:n + 1], pw[:, n - 1:n], pw[:, 0:1], ALU.mult)
                ch.link(v.tensor_tensor(pwK[:, C - 1 - n:C - n], pwK[:, C - n:C - n + 1], pw[:, 0:1], ALU.mult))
            v.tensor_scalar(s_t[:, 3:4], pwK[:, C - 1:C], -1.0, None, ALU.mult)
            ch.link(v.tensor_copy(lam_c[:], pw[:, C - 1:C]))
            dve.wait_ge(zeroed, 1)
            for i in range(1, C):
                last = v.tensor_copy(cN[:, i, 0:i], pwK[:, C - 1 - i:C - 1])
            ch.link(last)
            dve.wait_ge(k_loaded, 32)
            dve.wait_ge(vg_ready, 1)
            v.tensor_tensor(Vq[:].rearrange("p (n i) e -> p n i e", i=C), Kb,
                            pw[:].unsqueeze(1).unsqueeze(3).to_broadcast([P, QB, C, d]), ALU.mult).then_inc(kd_ready, 1)

            def sums(ms):
                for m in ms:
                    i, hf = items[m]
                    n0 = hf * HB
                    dve.wait_ge(prod_ready, m + 1)
                    if i < C:
                        src = prod[:, m % 2, 0:HB * i * d].rearrange("p (n j e) -> p n j e", n=HB, j=i)
                        dst = N[:, n0:n0 + HB, i, 0:i]
                    else:
                        src = prod[:, m % 2].rearrange("p (t e) -> p t e", e=d)
                        dst = ksq[:, n0 * C:(n0 + HB) * C]
                    v.tensor_reduce(dst, src, AX.X, ALU.add).then_inc(prod_used, 1)

            sums(range(0, 6))
            dve.wait_ge(vg_stored, 16 * B * VG)
            v.tensor_tensor(S1[:].rearrange("p (n i e) -> p n i e", i=C, e=d), Kb,
                            pwK[:].unsqueeze(1).unsqueeze(3).to_broadcast([P, QB, C, d]), ALU.mult).then_inc(kt_ready, 1)
            sums(range(6, len(items)))
            dve.wait_ge(prod_used, len(items))
            v.tensor_scalar(ksq[:], ksq[:], s_t[:, 3:4], 1.0, ALU.mult, ALU.add).then_inc(w1_ready, 1)
            ch.link(v.tensor_tensor(N[:], N[:], cN[:].unsqueeze(1).to_broadcast([P, QB, C, C]), ALU.mult))
            for i in range(1, C):
                t = prod[:, 0, 0:QB * i * i].rearrange("p (n j k) -> p n j k", n=QB, j=i)
                ch.link(v.tensor_tensor(t, N[:, :, i:i + 1, 0:i].to_broadcast([P, QB, i, i]),
                                        Tm[:, :, 0:i, 0:i].rearrange("p n k j -> p n j k"), ALU.mult))
                ins = v.tensor_reduce(Tm[:, :, i, 0:i], t, AX.X, ALU.add, negate=True)
                if i < C - 1:
                    ch.link(ins)
                else:
                    ins.then_inc(tm_ready, 1)


def phase_c(nc, T, W, kd, kt, tm, vg, vh, w1, ug, yd):
    X, ident, lam_c = T["X"], T["ident"], T["lam_c"]
    with ExitStack() as c:
        sb = lambda n, s, dt=F32: c.enter_context(nc.sbuf_tensor("c_" + n, s, dt))
        ps = lambda n, s: c.enter_context(nc.psum_tensor("c_" + n, s, F32))
        sem = lambda n: c.enter_context(nc.semaphore("c_" + n))
        kdb = sb("kdb", [P, 4, QT, d]); ktb = sb("ktb", [P, 4, QT, d]); tmb = sb("tmb", [P, 4, QBLK, C, C])
        vb = sb("vb", [P, 4, QT, VW]); ub = sb("ub", [P, 4, QT, VW])
        t1 = sb("t1", [P, C, VW, d]); pr = sb("pr", [P, C, VW]); rr = sb("rr", [P, C, VW]); t2 = sb("t2", [P, C, VW, C])
        t3 = sb("t3", [P, VW, d, C]); s3 = sb("s3", [P, VW * d]); S = sb("S", [P, VW * d])
        uR = sb("uR", [P, VG, SR, VW]); vR = sb("vR", [P, SR, d]); w1R = sb("w1R", [P, SR])
        tO = sb("tO", [P, SR, d]); yR = sb("yR", [P, SR, d])
        gam = sb("gam", [P, D]); bet = sb("bet", [P, D]); gbias = sb("gbias", [P, NE]); low = sb("low", [P, NE, NE])
        Y = sb("Y", [P, GT, D]); xn = sb("xn", [P, GT, D]); xnT = sb("xnT", [P, KC, GTOK])
        st = sb("st", [P, GT, 6]); mv = sb("mv", [P, GT, 2])
        ve = sb("ve", [P, GT]); ti = sb("ti", [P, GT], I32); tj = sb("tj", [P, GT], I32); tt = sb("tt", [P, GT])
        rs = [sb(f"rs{i}", [P, GT]) for i in range(2)]; nm = [sb(f"nm{i}", [P, GT]) for i in range(2)]
        gw = sb("gw", [P, KC, NE]); wg = sb("wg", [P, KC, NE, I_E]); wu = sb("wu", [P, KC, NE, I_E]); wd = sb("wd", [P, NE, D])
        ez = sb("ez", [P, GT, NE]); e1 = sb("e1", [P, GT, NE]); sco = sb("sco", [P, GT, NE]); sfc = sb("sfc", [P, GT, NE])
        gs = sb("gs", [P, GT, NGRP]); gsel = sb("gsel", [P, GT, NGRP]); sel = sb("sel", [P, GT, NE]); tmpc = sb("tmpc", [P, GT, NE])
        cge = sb("cge", [P, GT, NE, NE]); cgt = sb("cgt", [P, GT, NE, NE]); rank = sb("rank", [P, GT, NE])
        wsum = sb("wsum", [P, GT]); wt = sb("wt", [P, GT, NE])
        sg = sb("sg", [P, 2, GTOK]); uu = sb("uu", [P, 2, GTOK]); wb = sb("wb", [P, 2, GTOK]); hh = sb("hh", [P, 2, GTOK])
        psT = ps("psT", [P, KC, GTOK]); psGU = ps("psGU", [P, 2, GTOK]); psB = ps("psB", [P, 2, GTOK]); psY = ps("psY", [P, GT, D])

        seg_loaded = [sem(f"seg_loaded{q}") for q in range(4)]
        u_stored = [sem(f"u_stored{q}") for q in range(4)]
        w_loaded = sem("w_loaded"); quarter_done = sem("quarter_done"); chain = sem("chain"); pchain = sem("pchain")
        r_loaded = sem("r_loaded"); y_ready = sem("y_ready"); y_stored = sem("y_stored"); y_loaded = sem("y_loaded")
        moe_done = sem("moe_done")
        stats1 = sem("stats1"); normed1 = sem("normed1"); x1_done = sem("x1_done")
        stats2 = sem("stats2"); normed2 = sem("normed2"); turned = sem("turned"); turned_kept = sem("turned_kept")
        logits = sem("logits"); exp_done = sem("exp_done"); weights = sem("weights")
        gu_done = sem("gu_done"); gu_kept = sem("gu_kept"); wb_done = sem("wb_done"); wb_kept = sem("wb_kept")
        h_done = sem("h_done"); down_done = sem("down_done")
        block = c.enter_context(nc.Block())
        X4 = X[:].rearrange("p (b t) c -> p b t c", b=B)

        @block.sync
        def _(sp):
            def load_quarter(s, q):
                for b in range(B):
                    t0 = s * SEG + (b * L + q * QT)
                    n0 = s * (SEG // C) + (b * L + q * QT) // C
                    pb = slice(64 * b, 64 * b + 64)
                    for buf, src in ((kdb, kd), (ktb, kt)):
                        sp.dma_start(buf[pb, q].rearrange("p t e -> p (t e)"),
                                     src[:, bass.ds(t0, QT)].rearrange("h t e -> h (t e)").unsqueeze(1).to_broadcast([H, VG, QT * d])
                                     ).then_inc(seg_loaded[q], 16)
                    sp.dma_start(tmb[pb, q].rearrange("p n i j -> p (n i j)"),
                                 tm[:, bass.ds(n0, QBLK)].rearrange("h n m -> h (n m)").unsqueeze(1).to_broadcast([H, VG, QBLK * C * C])
                                 ).then_inc(seg_loaded[q], 16)
                    sp.dma_start(vb[pb, q].rearrange("p t w -> p (t w)"),
                                 vg[:, :, bass.ds(t0, QT)].rearrange("h g t w -> h g (t w)")).then_inc(seg_loaded[q], 16)

            def store_u(s, q):
                for b in range(B):
                    t0 = s * SEG + (b * L + q * QT)
                    sp.dma_start(ug[:, :, bass.ds(t0, QT)].rearrange("h g t w -> h g (t w)"),
                                 ub[64 * b:64 * b + 64, q].rearrange("p t w -> p (t w)")).then_inc(u_stored[q], 16)

            def output_rows(u):
                for q in range(4):
                    sp.wait_ge(u_stored[q], u * (16 * B) + 16 * B)
                sp.wait_ge(moe_done, u + 1)
                for b in range(B):
                    t0 = u * SEG + b * L
                    pb = slice(64 * b, 64 * b + 64)
                    for g in range(VG):
                        sp.dma_start(uR[pb, g].rearrange("p t w -> p (t w)"),
                                     ug[:, g, bass.ds(t0, SEG)].rearrange("h (r t) w -> h r (t w)", r=4)).then_inc(r_loaded, 16)
                    sp.dma_start(vR[pb].rearrange("p t e -> p (t e)"),
                                 vh[:, bass.ds(t0, SEG)].rearrange("h (r t) e -> h r (t e)", r=4)).then_inc(r_loaded, 16)
                    sp.dma_start(w1R[pb],
                                 w1[:, bass.ds(t0, SEG)].rearrange("h (r t) -> h r t", r=4)).then_inc(r_loaded, 16)
                sp.wait_ge(y_ready, u + 1)
                for b in range(B):
                    for r in range(4):
                        t0 = u * SEG + (b * L + r * SR)
                        sp.dma_start(yd[bass.ds(t0, SR)].rearrange("t (h e) -> h t e", h=H),
                                     yR[64 * b + r:64 * b + 64:4]).then_inc(y_stored, 16)
                sp.wait_ge(y_stored, u * (64 * B) + 64 * B)
                for b in range(B):
                    sp.dma_start(Y[:, 2 * b:2 * b + 2],
                                 yd[bass.ds(u * SEG + b * L, SEG)].rearrange("(j p) c -> p j c", p=P)).then_inc(y_loaded, 16)

            for q in range(4):
                load_quarter(0, q)
            for dst, src in ((gam, W["gamma"]), (bet, W["beta"]), (gbias, W["bias"])):
                sp.dma_start(dst[:], src.to_broadcast([P, src.shape[1]])).then_inc(w_loaded, 16)
            sp.dma_start(low[:].rearrange("p i j -> p (i j)"), W["low"].to_broadcast([P, NE * NE])).then_inc(w_loaded, 16)
            sp.dma_start(gw[:], W["gwT"].rearrange("(k p) e -> p k e", p=P)).then_inc(w_loaded, 16)
            for k in range(KC):
                sp.dma_start(wg[:, k], W["wgT"][k * P:(k + 1) * P]).then_inc(w_loaded, 16)
                sp.dma_start(wu[:, k], W["wuT"][k * P:(k + 1) * P]).then_inc(w_loaded, 16)
            sp.dma_start(wd[:], W["wdT"]).then_inc(w_loaded, 16)
            with sp.Fori(1, NSEG) as s:
                for q in range(4):
                    sp.wait_ge(quarter_done, s * 4 + (q - 3))
                    store_u(s - 1, q)
                    load_quarter(s, q)
                output_rows(s - 1)
            for q in range(4):
                sp.wait_ge(quarter_done, NSEG * 4 - 3 + q)
                store_u(NSEG - 1, q)
            output_rows(NSEG - 1)

        @block.vector
        def _(dve):
            v = nc.vector
            ch = Chain(dve, chain)
            S3 = S[:].rearrange("p (w k) -> p w k", w=VW)

            def block_step(s, q, i):
                t = slice(C * i, C * i + C)
                u = ub[:, q, t]
                ch.link(v.tensor_tensor(t1[:], kdb[:, q, t].unsqueeze(2).to_broadcast([P, C, VW, d]),
                                        S3.unsqueeze(1).to_broadcast([P, C, VW, d]), ALU.mult))
                ch.link(v.tensor_reduce(pr[:], t1[:], AX.X, ALU.add))
                ch.link(v.tensor_tensor(rr[:], vb[:, q, t], pr[:], ALU.subtract))
                ch.link(v.tensor_tensor(t2[:], tmb[:, q, i].unsqueeze(2).to_broadcast([P, C, VW, C]),
                                        rr[:].rearrange("p j w -> p w j").unsqueeze(1).to_broadcast([P, C, VW, C]), ALU.mult))
                ch.link(v.tensor_reduce(u, t2[:], AX.X, ALU.add))
                ch.link(v.tensor_tensor(t3[:], ktb[:, q, t].rearrange("p i k -> p k i").unsqueeze(1).to_broadcast([P, VW, d, C]),
                                        u.rearrange("p i w -> p w i").unsqueeze(2).to_broadcast([P, VW, d, C]), ALU.mult))
                ch.link(v.tensor_reduce(s3[:], t3[:], AX.X, ALU.add))
                new = v.scalar_tensor_tensor(S[:], S[:], lam_c[:], s3[:], ALU.mult, ALU.add)
                if i < QBLK - 1:
                    ch.link(new)
                else:
                    new.then_inc(quarter_done, 1)
                    dve.wait_ge(quarter_done, s * 4 + (q + 1))

            def stats(src, i, signal):
                for j in range(GT):
                    last = v.bn_stats(st[:, j], src(j))
                ch.link(last)
                for j in range(GT):
                    last = v.bn_aggr(mv[:, j], st[:, j])
                ch.link(last)
                rstd(v, ch, mv[:], ve[:], ti[:], tj[:], tt[:], rs[i][:], nm[i][:]).then_inc(signal, 1)

            def ranks(x, n, out):
                ge, gt = cge[:, :, 0:n, 0:n], cgt[:, :, 0:n, 0:n]
                xj = x.unsqueeze(2).to_broadcast([P, GT, n, n])
                xi = x.unsqueeze(3).to_broadcast([P, GT, n, n])
                v.tensor_tensor(ge, xj, xi, ALU.is_ge)
                ch.link(v.tensor_tensor(gt, xj, xi, ALU.is_gt))
                ch.link(v.tensor_tensor(ge, ge, gt, ALU.subtract))
                ch.link(v.tensor_tensor(ge, ge, low[:, 0:n, 0:n].unsqueeze(1).to_broadcast([P, GT, n, n]), ALU.mult))
                ch.link(v.tensor_tensor(gt, gt, ge, ALU.add))
                ch.link(v.tensor_reduce(rank[:, :, 0:n], gt, AX.X, ALU.add))
                ch.link(v.tensor_scalar(out, rank[:, :, 0:n], 1.5, None, ALU.is_lt))

            def gate():
                ch.link(v.tensor_scalar(e1[:], ez[:], 1.0, None, ALU.add))
                ch.link(v.reciprocal(sco[:], e1[:]))
                ch.link(v.tensor_tensor(sfc[:], sco[:], gbias[:].unsqueeze(1).to_broadcast([P, GT, NE]), ALU.add))
                ch.link(v.tensor_tensor(gs[:], sfc[:, :, 0::2], sfc[:, :, 1::2], ALU.add))
                ranks(gs[:], NGRP, gsel[:])
                ch.link(v.tensor_tensor(tmpc[:].rearrange("p t (g m) -> p t g m", m=2), sfc[:].rearrange("p t (g m) -> p t g m", m=2),
                                        gsel[:].unsqueeze(3).to_broadcast([P, GT, NGRP, 2]), ALU.mult))
                ranks(tmpc[:], NE, sel[:])
                ch.link(v.tensor_tensor(sel[:], sel[:], sco[:], ALU.mult))
                ch.link(v.tensor_reduce(wsum[:], sel[:], AX.X, ALU.add))
                ch.link(v.tensor_scalar(wsum[:], wsum[:], 1e-20, None, ALU.add))
                ch.link(v.reciprocal(wsum[:], wsum[:]))
                v.tensor_tensor(wt[:], sel[:], wsum[:].unsqueeze(2).to_broadcast([P, GT, NE]), ALU.mult).then_inc(weights, 1)

            def slot(u, n):
                if n == 0:
                    dve.wait_ge(y_loaded, u * (16 * B) + 16 * B)
                    stats(lambda j: Y[:, j], 0, stats1)
                if n == 1:
                    dve.wait_ge(x1_done, u + 1)
                    stats(lambda j: X4[:, j // 2, bass.ds(2 * u + j % 2, 1)].rearrange("p a c -> p (a c)"), 1, stats2)
                if n == 2:
                    dve.wait_ge(exp_done, u + 1)
                    gate()
                if n == 3:
                    dve.wait_ge(down_done, u * NE + NE)
                    xs = X4[:, :, bass.ds(2 * u, 2)]
                    v.tensor_tensor(xs, xs, psY[:].rearrange("p (b t) c -> p b t c", b=B), ALU.add).then_inc(moe_done, 1)

            def segment(s, slots):
                for q in range(4):
                    dve.wait_ge(seg_loaded[q], s * (128 * 1) + 128)
                    if slots:
                        dve.wait_ge(u_stored[q], s * (16 * B))
                    for i in range(QBLK):
                        block_step(s, q, i)
                        n = q * QBLK + i
                        if slots and n in SLOTS:
                            slot(s - 1, SLOTS.index(n))

            SLOTS = [5, 10, 14, 4 * QBLK - 1]
            dve.sem_inc(moe_done, 1)
            ch.link(v.memset(S[:], 0.0))
            dve.wait_ge(w_loaded, 16 * 10)
            segment(0, False)
            ch.clear()
            with dve.Fori(1, NSEG) as s:
                segment(s, True)
                ch.clear()
            for n in range(4):
                slot(NSEG - 1, n)

        def loops(eng, body):
            with eng.Fori(0, NSEG) as u:
                body(u)

        @block.gpsimd
        def _(pool):
            g_ = nc.gpsimd
            ch = Chain(pool, pchain)
            pool.wait_ge(w_loaded, 16 * 10)

            def group(u):
                pool.wait_ge(r_loaded, u * (16 * 12) + 16 * 12)
                ch.link(g_.tensor_tensor(tO[:].rearrange("p t (g w) -> p g t w", g=VG), uR[:],
                                         w1R[:].unsqueeze(1).unsqueeze(3).to_broadcast([P, VG, SR, VW]), ALU.mult))
                ch.link(g_.tensor_tensor(tO[:], vR[:], tO[:], ALU.subtract))
                g_.tensor_tensor(yR[:], vR[:], tO[:], ALU.add).then_inc(y_ready, 1)
                pool.wait_ge(normed1, u + 1)
                ch.link(g_.tensor_tensor(Y[:], Y[:], gam[:].unsqueeze(1).to_broadcast([P, GT, D]), ALU.mult))
                ch.link(g_.tensor_tensor(Y[:], Y[:], bet[:].unsqueeze(1).to_broadcast([P, GT, D]), ALU.add))
                xs = X4[:, :, bass.ds(2 * u, 2)]
                g_.tensor_tensor(xs, xs, Y[:].rearrange("p (b t) c -> p b t c", b=B), ALU.add).then_inc(x1_done, 1)
                for e in range(NE):
                    pool.wait_ge(wb_kept, u * NE + (e + 1))
                    ch.link(g_.tensor_tensor(sg[:, e % 2], sg[:, e % 2], wb[:, e % 2], ALU.mult))
                    if e >= 2:
                        pool.wait_ge(down_done, u * NE + (e - 1))
                    g_.tensor_tensor(hh[:, e % 2], sg[:, e % 2], uu[:, e % 2], ALU.mult).then_inc(h_done, 1)
                ch.clear()

            loops(pool, group)

        @block.scalar
        def _(act):
            a = nc.scalar

            def group(u):
                act.wait_ge(stats1, u + 1)
                for j in range(GT):
                    last = a.activation(Y[:, j], Y[:, j], ACT.Identity, bias=nm[0][:, j:j + 1], scale=rs[0][:, j:j + 1])
                last.then_inc(normed1, 1)
                act.wait_ge(stats2, u + 1)
                for j in range(GT):
                    xj = X4[:, j // 2, bass.ds(2 * u + j % 2, 1)].rearrange("p a c -> p (a c)")
                    last = a.activation(xn[:, j], xj, ACT.Identity, bias=nm[1][:, j:j + 1], scale=rs[1][:, j:j + 1])
                last.then_inc(normed2, 1)
                act.wait_ge(turned, u + 1)
                a.activation(xnT[:], psT[:], ACT.Copy).then_inc(turned_kept, 1)
                act.wait_ge(logits, u + 1)
                a.activation(ez[:], psT[:, 0, 0:GT * NE].rearrange("p (t e) -> p t e", e=NE), ACT.Exp, scale=-1.0).then_inc(exp_done, 1)
                for e in range(NE):
                    act.wait_ge(gu_done, u * NE + (e + 1))
                    if e >= 2:
                        act.wait_ge(h_done, u * NE + (e - 1))
                    a.activation(sg[:, e % 2], psGU[:, 0], ACT.Silu)
                    a.activation(uu[:, e % 2], psGU[:, 1], ACT.Copy).then_inc(gu_kept, 1)
                    act.wait_ge(wb_done, u * NE + (e + 1))
                    a.activation(wb[:, e % 2], psB[:, e % 2], ACT.Copy).then_inc(wb_kept, 1)

            loops(act, group)

        @block.tensor
        def _(pe):
            t = nc.tensor
            pe.wait_ge(w_loaded, 16 * 10)

            def group(u):
                pe.wait_ge(normed2, u + 1)
                pe.wait_ge(moe_done, u + 1)
                for k in range(KC):
                    for j in range(GT):
                        last = t.transpose(psT[:, k, j * P:(j + 1) * P], xn[:, j, k * P:(k + 1) * P], ident[:])
                last.then_inc(turned, 1)
                pe.wait_ge(turned_kept, u + 1)
                for j in range(GT):
                    for k in range(KC):
                        last = t.matmul(psT[:, 0, j * NE:(j + 1) * NE], xnT[:, k, j * P:(j + 1) * P], gw[:, k],
                                        start=(k == 0), stop=(k == KC - 1))
                last.then_inc(logits, 1)

                def gate_up(e):
                    if e >= 1:
                        pe.wait_ge(gu_kept, u * NE + e)
                    for i, w in enumerate((wg, wu)):
                        for k in range(KC):
                            last = t.matmul(psGU[:, i], w[:, k, e], xnT[:, k], start=(k == 0), stop=(k == KC - 1))
                    last.then_inc(gu_done, 1)

                def spread(e):
                    if e == 0:
                        pe.wait_ge(weights, u + 1)
                    if e >= 2:
                        pe.wait_ge(wb_kept, u * NE + (e - 1))
                    for j in range(GT):
                        last = t.matmul(psB[:, e % 2, j * P:(j + 1) * P], wt[:, j, e:e + 1].to_broadcast([P, P]), ident[:],
                                        start=True, stop=True)
                    last.then_inc(wb_done, 1)

                def down(e):
                    pe.wait_ge(h_done, u * NE + (e + 1))
                    for j in range(GT):
                        last = t.matmul(psY[:, j], hh[:, e % 2, j * P:(j + 1) * P], wd[:, e],
                                        start=(e == 0 and j % 2 == 0), stop=(e == NE - 1), skip_group_check=True)
                    last.then_inc(down_done, 1)

                for e in range(NE):
                    gate_up(e)
                    spread(e)
                    if e >= 1:
                        down(e - 1)
                down(NE - 1)

            loops(pe, group)


NH = B * H
KR = 6 * d
SPLIT_Q = (0, 0, 0, 1, 1, 2)
SPLIT_X = (0, 1, 2, 0, 1, 0)
RING = 4
KT = L // P
QC = 512
NQC = L // QC
LEAD = 3


def phase_d(nc, T, W, xp, qp, vx):
    X, ident = T["X"], T["ident"]
    with ExitStack() as c:
        sb = lambda n, s, dt=F32: c.enter_context(nc.sbuf_tensor("d_" + n, s, dt))
        ps = lambda n, s: c.enter_context(nc.psum_tensor("d_" + n, s, F32))
        sem = lambda n: c.enter_context(nc.semaphore("d_" + n))
        st = sb("st", [P, NT, 6]); mv = sb("mv", [P, NT, 2])
        ve = sb("ve", [P, NT]); ti = sb("ti", [P, NT], I32); tj = sb("tj", [P, NT], I32); tt = sb("tt", [P, NT])
        rs = sb("rs", [P, NT]); nm = sb("nm", [P, NT])
        wv = sb("wv", [P, KC, D]); wa = sb("wa", [P, KC, P]); vbias = sb("vbias", [P, D])
        xn = sb("xn", [P, 2, GT, D]); xnT = sb("xnT", [P, 2, KC, GTOK])
        part = sb("part", [P, 2, 2, 3, KC, GTOK], BF16)
        r1 = sb("r1", [P, 2, KC, GTOK])
        vst = sb("vst", [P, 2, H, GT, 32])
        psT = ps("psT", [P, 2, KC, GTOK]); psV = ps("psV", [P, GT, D]); psW = ps("psW", [P, KC, GTOK])
        w_loaded = sem("w_loaded"); chain = sem("chain"); stats = sem("stats"); normed = sem("normed")
        turned = sem("turned"); hi_kept = sem("hi_kept"); v_done = sem("v_done"); q_done = sem("q_done"); qhi_kept = sem("qhi_kept")
        parts_done = sem("parts_done"); v_kept = sem("v_kept"); zeroed = sem("zeroed")
        stored = [sem(f"stored{i}") for i in range(2)]
        block = c.enter_context(nc.Block())
        GB = NG // B
        SHARE = 16 * (2 * 3 * KC + 1)

        @block.sync
        def _(sp):
            sp.dma_start(wv[:], W["wvT"].rearrange("(k p) n -> p k n", p=P)).then_inc(w_loaded, 16)
            sp.dma_start(wa[:], W["wa"].rearrange("(k p) n -> p k n", p=P)).then_inc(w_loaded, 16)
            sp.dma_start(vbias[:], W["wv_b"].to_broadcast([P, D])).then_inc(w_loaded, 16)
            for b in range(B):
                with sp.Fori(0, GB // 2) as i:
                    for par in range(2):
                        gi = 2 * i + par
                        sp.wait_ge(parts_done, gi * 2 + (b * GB * 2 + 2))
                        for a, dst in enumerate((xp, qp)):
                            for m in range(3):
                                for k in range(KC):
                                    sp.dma_start(dst[m, b, k * P:(k + 1) * P, bass.ds(gi * GTOK, GTOK)],
                                                 part[:, par, a, m, k]).then_inc(stored[par], 16)
                        sp.wait_ge(v_kept, gi + (b * GB + 1))
                        sp.dma_start(vx[b * H:(b + 1) * H, :, bass.ds(gi * GT, GT)].rearrange("h p k e -> p h (k e)"),
                                     vst[:, par].rearrange("p h k e -> p h (k e)")).then_inc(stored[par], 16)
            for par in range(2):
                sp.wait_ge(stored[par], (NG // 2 + 1) * SHARE)

        def groups(eng, body):
            for b in range(B):
                with eng.Fori(0, GB // 2) as i:
                    for par in range(2):
                        body(2 * i + (b * GB + par), par, i + b * GB // 2)

        @block.vector
        def _(dve):
            v = nc.vector
            ch = Chain(dve, chain)
            for par in range(2):
                dve.sem_inc(stored[par], SHARE)
            for n in range(NT):
                last = v.bn_stats(st[:, n], X[:, n])
            ch.link(last)
            for n in range(NT):
                last = v.bn_aggr(mv[:, n], st[:, n])
            ch.link(last)
            rstd(v, ch, mv[:], ve[:], ti[:], tj[:], tt[:], rs[:], nm[:]).then_inc(stats, 1)
            ch.clear()
            dve.wait_ge(w_loaded, 48)
            dve.wait_ge(zeroed, 2)

            def group(g, par, i):
                def split(a, src, signal):
                    ch.link(v.tensor_tensor(r1[:, a], src, part[:, par, a, 0], ALU.subtract))
                    ch.link(v.tensor_copy(part[:, par, a, 1], r1[:, a]))
                    v.tensor_tensor(part[:, par, a, 2], r1[:, a], part[:, par, a, 1], ALU.subtract).then_inc(signal, 1)

                dve.wait_ge(stored[par], i * SHARE + SHARE)
                dve.wait_ge(hi_kept, g + 1)
                split(0, psT[:, par], parts_done)
                dve.wait_ge(v_done, g + 1)
                v.tensor_tensor(vst[:, par, :, :, 0:d].rearrange("p h t e -> p t h e"),
                                psV[:].rearrange("p t (h e) -> p t h e", h=H),
                                vbias[:].rearrange("p (h e) -> p h e", h=H).unsqueeze(1).to_broadcast([P, GT, H, d]),
                                ALU.add).then_inc(v_kept, 1)
                dve.wait_ge(qhi_kept, g + 1)
                dve.wait_ge(parts_done, g * 2 + 1)
                split(1, psW[:], parts_done)
                ch.clear()

            groups(dve, group)

        @block.gpsimd
        def _(pool):
            nc.gpsimd.memset(vst[:], 0.0).then_inc(zeroed, 1)
            pool.wait_ge(zeroed, 1)
            nc.gpsimd.memset(vst[:, :, :, :, d:d + 1], 1.0).then_inc(zeroed, 1)

        @block.scalar
        def _(act):
            a = nc.scalar
            act.wait_ge(stats, 1)

            def group(g, par, i):
                for j in range(GT):
                    n = g * GT + j
                    last = a.activation(xn[:, par, j], X[:, bass.ds(n, 1)].rearrange("p a c -> p (a c)"), ACT.Identity,
                                        bias=nm[:, bass.ds(n, 1)], scale=rs[:, bass.ds(n, 1)])
                last.then_inc(normed, 1)
                act.wait_ge(turned, g + 1)
                a.activation(xnT[:, par], psT[:, par], ACT.Copy)
                act.wait_ge(stored[par], i * SHARE + SHARE)
                a.activation(part[:, par, 0, 0], psT[:, par], ACT.Copy).then_inc(hi_kept, 1)
                act.wait_ge(q_done, g + 1)
                a.activation(part[:, par, 1, 0], psW[:], ACT.Copy).then_inc(qhi_kept, 1)

            groups(act, group)

        @block.tensor
        def _(pe):
            t = nc.tensor
            pe.wait_ge(w_loaded, 48)

            def group(g, par, i):
                pe.wait_ge(normed, g + 1)
                for k in range(KC):
                    for j in range(GT):
                        last = t.transpose(psT[:, par, k, j * P:(j + 1) * P], xn[:, par, j, k * P:(k + 1) * P], ident[:])
                last.then_inc(turned, 1)
                pe.wait_ge(hi_kept, g + 1)
                pe.wait_ge(parts_done, g * 2 + 1)
                for j in range(GT):
                    for k in range(KC):
                        last = t.matmul(psV[:, j], xnT[:, par, k, j * P:(j + 1) * P], wv[:, k], start=(k == 0), stop=(k == KC - 1))
                last.then_inc(v_done, 1)
                for k in range(KC):
                    last = t.matmul(psW[:, k], wa[:, k], xnT[:, par, k], start=True, stop=True)
                last.then_inc(q_done, 1)

            groups(pe, group)


def phase_e(nc, T, xp, qp, vx):
    ident, O2 = T["ident"], T["O2"]
    with ExitStack() as c:
        sb = lambda n, s, dt=F32: c.enter_context(nc.sbuf_tensor("e_" + n, s, dt))
        ps = lambda n, s: c.enter_context(nc.psum_tensor("e_" + n, s, F32))
        sem = lambda n: c.enter_context(nc.semaphore("e_" + n))
        XS = [sb(f"XS{i}", [P, L], BF16) for i in range(RING)]
        QS = [sb(f"QS{i}", [P, L], BF16) for i in range(RING)]
        Vh = [sb(f"Vh{i}", [P, KT, 32]) for i in range(2)]
        Pt = [sb(f"Pt{i}", [P, L]) for i in range(2)]
        oT = [sb(f"oT{i}", [P, QC]) for i in range(2)]
        mx = [sb(f"mx{i}", [P, KT, NQC]) for i in range(2)]
        mneg = sb("mneg", [P, KT]); mr = sb("mr", [P, KT]); M3 = sb("M3", [P, 3, 32], BF16)
        MT = [sb(f"MT{i}", [P, 3, 32], BF16) for i in range(2)]
        rden = sb("rden", [P, NQC, NQC])
        psS = [ps(f"psS{i}", [P, 2, QC]) for i in range(2)]
        psM = [ps(f"psM{i}", [P, QC]) for i in range(2)]
        psO = ps("psO", [P, QC]); psX = ps("psX", [P, QC])
        stacks = sem("stacks"); v_loaded = sem("v_loaded"); ones = sem("ones")
        max_ready = sem("max_ready"); max_used = sem("max_used"); m_ready = sem("m_ready"); m_loaded = sem("m_loaded")
        scores = sem("scores"); exp_done = sem("exp_done"); av_done = sem("av_done")
        o_kept = sem("o_kept"); o_turned = sem("o_turned"); normed = sem("normed"); chain = sem("chain")
        block = c.enter_context(nc.Block())
        SHARE = 16 * 12
        MT_OF = KT * NQC

        def heads(body):
            def run(eng):
                body(0, 0)
                with eng.Fori(0, NH // RING - 1) as i:
                    for k in range(RING):
                        body(i * RING + (1 + k), (1 + k) % RING)
                for n in range(NH - RING + 1, NH):
                    body(n, n % RING)
            return run

        def is_there(n):
            return not isinstance(n, int) or 0 <= n < NH

        @block.sync
        def _(sp):
            def load_stacks(n, r):
                for row, (mq, mk) in enumerate(zip(SPLIT_Q, SPLIT_X)):
                    rows = slice(row * d, row * d + d)
                    sp.dma_start(QS[r % RING][rows], qp[mq].rearrange("b c t -> (b c) t")[bass.ds(n * d, d)]).then_inc(stacks, 16)
                    sp.dma_start(XS[r % RING][rows], xp[mk].rearrange("b c t -> (b c) t")[bass.ds(n * d, d)]).then_inc(stacks, 16)

            def load_values(n, r):
                sp.dma_start(Vh[r % 2][:].rearrange("p k e -> p (k e)"),
                             vx[bass.ds(n, 1)].rearrange("n p k e -> (n p) (k e)")).then_inc(v_loaded, 16)

            def load_max(n, r):
                sp.wait_ge(m_ready, n + 1)
                for m in range(3):
                    for q4 in range(4):
                        dst = QS[r % RING][KR + m:KR + m + 1].rearrange("p (t q c) -> p q t c", q=4, c=32)[:, q4]
                        sp.dma_start(dst, MT[r % 2][32 * q4:32 * q4 + KT, m]).then_inc(m_loaded, 16)

            load_stacks(0, 0)
            sp.wait_ge(stacks, SHARE)
            load_stacks(1, 1)
            load_values(0, 0)
            load_max(0, 0)

            def head(n, r):
                if not isinstance(n, int) or n > 0:
                    sp.wait_ge(av_done, n * KT)
                if is_there(n + 2):
                    sp.wait_ge(stacks, n * SHARE + 2 * SHARE)
                    load_stacks(n + 2, r + 2)
                if is_there(n + 1):
                    sp.wait_ge(v_loaded, n * 16 + 16)
                    load_values(n + 1, r + 1)
                    load_max(n + 1, r + 1)

            heads(head)(sp)

        @block.vector
        def _(dve):
            v = nc.vector
            ch = Chain(dve, chain)
            ch.link(v.memset(M3[:], 0.0))
            for i in range(RING):
                last = v.memset(XS[i][KR:KR + 3], 1.0)
            last.then_inc(ones, 1)

            def tile_max(n, r, t):
                for q in range(NQC):
                    dve.wait_ge(max_ready, n * MT_OF + (t * NQC + q + 1))
                    v.reduce_max(mx[r % 2][:, t, q:q + 1], psM[q % 2][:], AX.X).then_inc(max_used, 1)
                if t == KT - 1:
                    dve.wait_ge(max_used, n * MT_OF + MT_OF)
                    ch.link(v.tensor_reduce(mneg[:], mx[r % 2][:], AX.X, ALU.max, negate=True))
                    ch.link(v.tensor_copy(M3[:, 0, 0:KT], mneg[:]))
                    ch.link(v.tensor_tensor(mr[:], mneg[:], M3[:, 0, 0:KT], ALU.subtract))
                    ch.link(v.tensor_copy(M3[:, 1, 0:KT], mr[:]))
                    ch.link(v.tensor_tensor(M3[:, 2, 0:KT], mr[:], M3[:, 1, 0:KT], ALU.subtract))
                    if not isinstance(n, int) or n >= 2:
                        dve.wait_ge(m_loaded, n * SHARE - SHARE)
                    v.transpose(MT[r % 2][:].rearrange("p m c -> p (m c)"), M3[:].rearrange("p m c -> p (m c)")).then_inc(m_ready, 1)
                    dve.wait_ge(m_ready, n + 1)

            def norm(n):
                dve.wait_ge(o_turned, n + 1)
                x = psX[:].rearrange("p (c j e) -> p j c e", c=NQC, e=32)
                ch.link(v.reciprocal(rden[:], x[:, :, :, d]))
                o = O2[:, bass.ds(n, 1)].rearrange("p a (j c) e -> p (a j) c e", j=NQC)
                v.tensor_tensor(o, x[:, :, :, 0:d], rden[:].unsqueeze(3).to_broadcast([P, NQC, NQC, d]), ALU.mult).then_inc(normed, 1)
                dve.wait_ge(normed, n + 1)

            for t in range(KT):
                tile_max(0, 0, t)
            for t in range(LEAD):
                tile_max(1, 1, t)
            ch.clear()

            def head(n, r):
                for kt in range(KT):
                    ahead, t = 1 + (kt + LEAD) // KT, (kt + LEAD) % KT
                    if is_there(n + ahead):
                        tile_max(n + ahead, r + ahead, t)
                    if kt == 3 and is_there(n - 1):
                        norm(n - 1)
                ch.clear()

            heads(head)(dve)
            norm(NH - 1)

        @block.scalar
        def _(act):
            a = nc.scalar

            def keep_output(n, r):
                act.wait_ge(av_done, n * KT + KT)
                a.activation(oT[r % 2][:], psO[:], ACT.Copy).then_inc(o_kept, 1)

            def head(n, r):
                for kt in range(KT):
                    if not isinstance(n, int) or n * KT + kt >= 2:
                        act.wait_ge(av_done, n * KT + (kt - 1))
                    for half in range(2):
                        act.wait_ge(scores, n * (2 * KT) + (2 * kt + half + 1))
                        a.activation(Pt[kt % 2][:, half * 2 * QC:(half + 1) * 2 * QC], psS[half][:].rearrange("p a c -> p (a c)"),
                                     ACT.Exp, scale=float(d) ** -0.5).then_inc(exp_done, 1)
                    if kt == 0 and is_there(n - 1):
                        keep_output(n - 1, r + 1)

            heads(head)(act)
            keep_output(NH - 1, NH - 1)

        @block.tensor
        def _(pe):
            t_ = nc.tensor

            def for_max(n, r, t, q):
                if t == 0 and q == 0:
                    pe.wait_ge(stacks, n * SHARE + SHARE)
                if not isinstance(n, int) or n * MT_OF + t * NQC + q >= 2:
                    pe.wait_ge(max_used, n * MT_OF + (t * NQC + q - 1))
                t_.matmul(psM[q % 2][:], QS[r % RING][0:KR, t * P:(t + 1) * P], XS[r % RING][0:KR, q * QC:(q + 1) * QC],
                          start=True, stop=True).then_inc(max_ready, 1)

            def for_exp(n, r, kt, half, wait):
                if wait is not None:
                    pe.wait_ge(exp_done, wait)
                for q in range(2):
                    q0 = (half * 2 + q) * QC
                    last = t_.matmul(psS[half][:, q], XS[r % RING][0:KR + 3, kt * P:(kt + 1) * P], QS[r % RING][0:KR + 3, q0:q0 + QC],
                                     start=True, stop=True)
                last.then_inc(scores, 1)

            def times_values(n, r, kt):
                if kt == 0:
                    pe.wait_ge(v_loaded, n * 16 + 16)
                    if is_there(n - 1):
                        pe.wait_ge(o_kept, n)
                for j in range(NQC):
                    last = t_.matmul(psO[32 * j:32 * j + 32], Vh[r % 2][:, kt], Pt[kt % 2][:, j * QC:(j + 1) * QC],
                                     start=(kt == 0), stop=(kt == KT - 1))
                last.then_inc(av_done, 1)

            def turn_output(n, r):
                pe.wait_ge(o_kept, n + 1)
                for cc in range(NQC):
                    last = t_.transpose(psX[:, cc * P:(cc + 1) * P], oT[r % 2][:, cc * P:(cc + 1) * P], ident[:])
                last.then_inc(o_turned, 1)

            for t in range(KT):
                for q in range(NQC):
                    for_max(0, 0, t, q)
            for t in range(LEAD):
                for q in range(NQC):
                    for_max(1, 1, t, q)
            pe.wait_ge(ones, 1)
            pe.wait_ge(m_loaded, SHARE)
            for half in range(2):
                for_exp(0, 0, 0, half, None)

            def head(n, r):
                for kt in range(KT):
                    k = n * (2 * KT) + 2 * kt
                    ahead, t = 1 + (kt + LEAD) // KT, (kt + LEAD) % KT
                    nn, nr, nk = (n, r, kt + 1) if kt < KT - 1 else (n + 1, r + 1, 0)
                    if kt == KT - 1 and is_there(nn):
                        pe.wait_ge(m_loaded, n * SHARE + 2 * SHARE)
                    for half in range(2):
                        if is_there(nn):
                            for_exp(nn, nr, nk, half, k + (half + 1))
                        if is_there(n + ahead):
                            for_max(n + ahead, r + ahead, t, half)
                    if not is_there(nn):
                        pe.wait_ge(exp_done, k + 2)
                    times_values(n, r, kt)
                    for q in range(2, NQC):
                        if is_there(n + ahead):
                            for_max(n + ahead, r + ahead, t, q)
                    if kt == 2 and is_there(n - 1):
                        turn_output(n - 1, r + 1)

            heads(head)(pe)
            pe.wait_ge(normed, NH - 1)
            turn_output(NH - 1, NH - 1)


def phase_f(nc, T, W, out):
    X, ident, O2 = T["X"], T["ident"], T["O2"]
    F32R = mybir.dt.float32r
    with ExitStack() as c:
        sb = lambda n, s, dt=F32: c.enter_context(nc.sbuf_tensor("f_" + n, s, dt))
        ps = lambda n, s: c.enter_context(nc.psum_tensor("f_" + n, s, F32))
        sem = lambda n: c.enter_context(nc.semaphore("f_" + n))
        ow = sb("ow", [P, KC, D]); obias = sb("obias", [P, D])
        wi = sb("wi", [P, KC * HID], I32)
        wg = sb("wg", [P, KC, HID], F32R); wu = sb("wu", [P, KC, HID], F32R); wd = sb("wd", [P, HC, D], F32R)
        ot = sb("ot", [P, GT, D]); otT = sb("otT", [P, KC, GTOK]); xn = sb("xn", [P, GT, D])
        xh = sb("xh", [P, 2, KC, GTOK], F32R)
        st = sb("st", [P, GT, 6]); mv = sb("mv", [P, GT, 2])
        ve = sb("ve", [P, GT]); ti = sb("ti", [P, GT], I32); tj = sb("tj", [P, GT], I32); tt = sb("tt", [P, GT])
        rs = sb("rs", [P, GT]); nm = sb("nm", [P, GT])
        sg = sb("sg", [P, 2, GTOK]); hf = sb("hf", [P, 2, GTOK]); hp = sb("hp", [P, 2, 2, GTOK], F32R)
        yo = sb("yo", [P, GT, D])
        psT = ps("psT", [P, KC, GTOK]); psG = ps("psG", [P, GTOK]); psU = ps("psU", [P, GTOK])
        psP = ps("psP", [P, GT, D]); psY = ps("psY", [P, GT, D])
        w_loaded = sem("w_loaded"); wi_loaded = sem("wi_loaded"); wi_used = sem("wi_used")
        chain = sem("chain"); pchain = sem("pchain")
        gathered = sem("gathered"); turned_o = sem("turned_o"); kept_o = sem("kept_o"); biased = sem("biased"); projected = sem("projected")
        stats = sem("stats"); normed = sem("normed"); turned = sem("turned"); high = sem("high"); low = sem("low")
        g_done = sem("g_done"); silu_done = sem("silu_done"); h_done = sem("h_done"); hh_done = sem("hh_done"); hl_done = sem("hl_done")
        down_done = sem("down_done"); y_done = sem("y_done"); stored = sem("stored")
        block = c.enter_context(nc.Block())
        X3 = X[:].rearrange("p n c -> p n c")

        @block.sync
        def _(sp):
            sp.dma_start(ow[:], W["owT"].rearrange("(k p) n -> p k n", p=P)).then_inc(w_loaded, 16)
            sp.dma_start(obias[:], W["out_b"].to_broadcast([P, D])).then_inc(w_loaded, 16)
            for i, (src, k) in enumerate(((W["fgT"], KC), (W["fuT"], KC), (W["fdT"], HC))):
                if i:
                    sp.wait_ge(wi_used, i)
                sp.dma_start(wi[:].rearrange("p (k n) -> p k n", k=k), src.rearrange("(k p) n -> p k n", p=P)).then_inc(wi_loaded, 16)
            with sp.Fori(0, NG) as g:
                sp.wait_ge(y_done, g + 1)
                sp.dma_start(out[bass.ds(g * GTOK, GTOK)].rearrange("(j p) c -> p j c", p=P), yo[:]).then_inc(stored, 16)
            sp.wait_ge(stored, NG * 16 + 16)

        def loops(eng, body):
            for b in range(B):
                with eng.Fori(0, NG // B) as i:
                    body(i + b * (NG // B), O2[:, b * H:(b + 1) * H, bass.ds(i * GT, GT), :])

        @block.gpsimd
        def _(pool):
            pool.wait_ge(w_loaded, 32)

            def group(g, _):
                xs = X[:, bass.ds(g * GT, GT)]
                nc.gpsimd.tensor_tensor(xs, xs, obias[:].unsqueeze(1).to_broadcast([P, GT, D]), ALU.add).then_inc(biased, 1)

            loops(pool, group)

        @block.scalar
        def _(act):
            a = nc.scalar
            for i, w in enumerate((wg, wu, wd)):
                act.wait_ge(wi_loaded, 16 * (i + 1))
                a.activation(w[:].rearrange("p k n -> p (k n)"), wi[:], ACT.Copy).then_inc(wi_used, 1)

            def group(g, o2):
                a.activation(ot[:].rearrange("p t (h e) -> p t h e", h=H), o2.rearrange("p h t e -> p t h e"), ACT.Copy).then_inc(gathered, 1)
                act.wait_ge(turned_o, g + 1)
                a.activation(otT[:], psT[:], ACT.Copy).then_inc(kept_o, 1)
                act.wait_ge(stats, g + 1)
                for j in range(GT):
                    last = a.activation(xn[:, j], X[:, bass.ds(g * GT + j, 1)].rearrange("p a c -> p (a c)"), ACT.Identity,
                                        bias=nm[:, j:j + 1], scale=rs[:, j:j + 1])
                last.then_inc(normed, 1)
                act.wait_ge(turned, g + 1)
                a.activation(xh[:, 0], psT[:], ACT.Copy).then_inc(high, 1)
                for m in range(HC):
                    act.wait_ge(g_done, g * HC + (m + 1))
                    a.activation(sg[:, m % 2], psG[:], ACT.Silu, scale=FSCALE).then_inc(silu_done, 1)
                    act.wait_ge(h_done, g * HC + (m + 1))
                    if m >= 2:
                        act.wait_ge(down_done, g * HC + (m - 1))
                    a.activation(hp[:, m % 2, 0], hf[:, m % 2], ACT.Copy).then_inc(hh_done, 1)

            loops(act, group)

        @block.vector
        def _(dve):
            v = nc.vector
            ch = Chain(dve, chain)
            dve.sem_inc(stored, 16)

            def group(g, _):
                xs = X[:, bass.ds(g * GT, GT)]
                dve.wait_ge(biased, g + 1)
                dve.wait_ge(projected, g + 1)
                ch.link(v.tensor_tensor(xs, xs, psP[:], ALU.add))
                for j in range(GT):
                    last = v.bn_stats(st[:, j], X[:, bass.ds(g * GT + j, 1)].rearrange("p a c -> p (a c)"))
                ch.link(last)
                for j in range(GT):
                    last = v.bn_aggr(mv[:, j], st[:, j])
                ch.link(last)
                rstd(v, ch, mv[:], ve[:], ti[:], tj[:], tt[:], rs[:], nm[:]).then_inc(stats, 1)
                dve.wait_ge(high, g + 1)
                v.tensor_tensor(xh[:, 1], psT[:], xh[:, 0], ALU.subtract).then_inc(low, 1)
                for m in range(HC):
                    dve.wait_ge(silu_done, g * HC + (m + 1))
                    v.tensor_tensor(hf[:, m % 2], psU[:], sg[:, m % 2], ALU.mult).then_inc(h_done, 1)
                    dve.wait_ge(hh_done, g * HC + (m + 1))
                    v.tensor_tensor(hp[:, m % 2, 1], hf[:, m % 2], hp[:, m % 2, 0], ALU.subtract).then_inc(hl_done, 1)
                dve.wait_ge(down_done, g * HC + HC)
                dve.wait_ge(stored, g * 16 + 16)
                v.scalar_tensor_tensor(yo[:].rearrange("p t c -> p (t c)"), psY[:].rearrange("p t c -> p (t c)"), FSCALE * FSCALE,
                                       xs.rearrange("p t c -> p (t c)"), ALU.mult, ALU.add).then_inc(y_done, 1)
                ch.clear()

            loops(dve, group)

        @block.tensor
        def _(pe):
            t = nc.tensor
            pe.wait_ge(w_loaded, 32)
            pe.wait_ge(wi_used, 3)

            def group(g, _):
                pe.wait_ge(gathered, g + 1)
                for k in range(KC):
                    for j in range(GT):
                        last = t.transpose(psT[:, k, j * P:(j + 1) * P], ot[:, j, k * P:(k + 1) * P], ident[:])
                last.then_inc(turned_o, 1)
                pe.wait_ge(kept_o, g + 1)
                for j in range(GT):
                    for k in range(KC):
                        last = t.matmul(psP[:, j], otT[:, k, j * P:(j + 1) * P], ow[:, k], start=(k == 0), stop=(k == KC - 1))
                last.then_inc(projected, 1)
                pe.wait_ge(normed, g + 1)
                for k in range(KC):
                    for j in range(GT):
                        last = t.transpose(psT[:, k, j * P:(j + 1) * P], xn[:, j, k * P:(k + 1) * P], ident[:])
                last.then_inc(turned, 1)

                def up(m):
                    if m >= 1:
                        pe.wait_ge(h_done, g * HC + m)
                    for w, o in ((wg, psG), (wu, psU)):
                        n = 0
                        for k in range(KC):
                            for part in range(2):
                                last = t.matmul(o[:], w[:, k, m * P:(m + 1) * P], xh[:, part, k], start=(n == 0), stop=(n == 2 * KC - 1))
                                n += 1
                    last.then_inc(g_done, 1)

                def down(m):
                    pe.wait_ge(hl_done, g * HC + (m + 1))
                    for j in range(GT):
                        for part in range(2):
                            last = t.matmul(psY[:, j], hp[:, m % 2, part, j * P:(j + 1) * P], wd[:, m],
                                            start=(m == 0 and j % 2 == 0 and part == 0), stop=(m == HC - 1 and part == 1),
                                            skip_group_check=True)
                    last.then_inc(down_done, 1)

                pe.wait_ge(low, g + 1)
                for m in range(HC):
                    up(m)
                    if m >= 1:
                        down(m - 1)
                down(HC - 1)

            loops(pe, group)


def build(nc, a, out):
    scratch = lambda n, s, dt=F32: nc.dram_tensor(n, s, dt, kind="Internal").ap()
    with ExitStack() as c:
        sb = lambda n, s, dt=F32: c.enter_context(nc.sbuf_tensor(n, s, dt))
        T = {"ident_in": a["ident"]}
        T["X"] = sb("X", [P, NT, D])
        T["ident"] = sb("ident", [P, P])
        T["lam_c"] = sb("lam_c", [P, 1])
        kh = scratch("kh", (H, BL, d)); vh = scratch("vh", (H, BL, d))
        kd = scratch("kd", (H, BL, d)); kt = scratch("kt", (H, BL, d))
        tm = scratch("tm", (H, BL // C, C * C)); vg = scratch("vg", (H, VG, BL, VW)); w1 = scratch("w1", (H, BL))
        ug = scratch("ug", (H, VG, BL, VW)); yd = scratch("yd", (BL, D))
        xp = scratch("xp", (3, B, D, L), BF16); qp = scratch("qp", (3, B, D, L), BF16); vx = scratch("vx", (NH, P, KT, 32))
        phase_a(nc, T, a["x"], a["wT"], kh, vh)
        phase_b(nc, T, a["eta"], a["lam_logit"], kh, vh, kd, kt, tm, vg, w1)
        phase_c(nc, T, a, kd, kt, tm, vg, vh, w1, ug, yd)
        phase_d(nc, T, a, xp, qp, vx)
        T["O2"] = sb("O2", [P, NH, KT, d])
        phase_e(nc, T, xp, qp, vx)
        phase_f(nc, T, a, out)


def laid_out(i):
    wa = np.zeros((D, P), np.float32)
    for h in range(H):
        hh = h % (P // d)
        wa[h * d:(h + 1) * d, hh * d:(hh + 1) * d] = i["L1_attn_w_att_val"][h]
    return {
        "x": i["L0_attn_x"].reshape(BL, D),
        "wT": i["L0_attn_W"].T,
        "gamma": i["L0_attn_ln_gamma"].reshape(1, D),
        "beta": i["L0_attn_ln_beta"].reshape(1, D),
        "eta": i["L0_attn_eta"].reshape(1, 1),
        "lam_logit": i["L0_attn_lam_logit"].reshape(1, 1),
        "gwT": i["L0_ffn_gate_weight"].T,
        "bias": i["L0_ffn_e_score_correction_bias"].reshape(1, NE),
        "wgT": i["L0_ffn_gate_proj"].transpose(2, 0, 1),
        "wuT": i["L0_ffn_up_proj"].transpose(2, 0, 1),
        "wdT": i["L0_ffn_down_proj"].transpose(2, 0, 1),
        "wa": wa,
        "wvT": i["L1_attn_wv_w"].T,
        "wv_b": i["L1_attn_wv_b"].reshape(1, D),
        "owT": i["L1_attn_out_w"].T,
        "out_b": i["L1_attn_out_b"].reshape(1, D),
        "fgT": i["L1_ffn_w_gate"].T,
        "fuT": i["L1_ffn_w_up"].T,
        "fdT": i["L1_ffn_w_down"].T,
        "ident": np.eye(P, dtype=np.float32),
        "low": np.tril(np.ones((NE, NE), np.float32), -1).reshape(1, NE * NE),
    }


def kernel(**inputs):
    import concourse.bacc as _bacc
    from concourse.bass_utils import run_bass_kernel_spmd as _run

    nc = _bacc.Bacc("TRN2", target_bir_lowering=False, num_devices=1)
    arrays = {f"in_{n}": np.ascontiguousarray(v) for n, v in laid_out({n: np.asarray(v) for n, v in inputs.items()}).items()}
    args = {n[3:]: nc.dram_tensor(n, v.shape, mybir.dt.from_np(v.dtype), kind="ExternalInput").ap() for n, v in arrays.items()}
    out = nc.dram_tensor("out", (BL, D), F32, kind="ExternalOutput").ap()
    build(nc, args, out)
    r = _run(nc, [arrays], core_ids=[0])
    return r.results[0]["out"].reshape(B, L, D)
```

```python
import numpy as np
import concourse.bass as bass
from concourse import mybir
from contextlib import ExitStack

P = 128
ALU = mybir.AluOpType
ACT = mybir.ActivationFunctionType
AX = mybir.AxisListType
F32 = mybir.dt.float32
BF16 = mybir.dt.bfloat16
I32 = mybir.dt.int32
F32R = mybir.dt.float32r

B, L, D, H = 2, 2048, 256, 16
d = D // H
BL = B * L
NT = BL // P
TPB = L // P
KC = D // P
GT = 4
NG = NT // GT
GTOK = GT * P
EPS = 1e-5

C = 8
VG = 4
VW = d // VG
NQ = L // (P // (B * H))
QB = NQ // C
SEG = 256
NSEG = L // SEG
QT = SEG // 4
QBLK = QT // C
SR = SEG // 4

NE, I_E = 8, 128
NGRP = 4
HID = 768
HC = HID // P
FSCALE = 1.0 / 127.0

MAGIC = float(0x5F3759DF)


class Chain:

    def __init__(self, eng, sem):
        self.eng, self.sem, self.n = eng, sem, 0

    def link(self, ins):
        self.n += 1
        ins.then_inc(self.sem, 1)
        self.eng.wait_ge(self.sem, self.n)

    def clear(self):
        self.eng.sem_clear(self.sem)
        self.n = 0


def rstd(dve, ch, mv, ve, ti, tj, t, rs, nm):
    ch.link(dve.tensor_scalar(ve, mv[:, :, 1], EPS, None, ALU.add))
    ch.link(dve.tensor_scalar(ti, ve.bitcast(I32), 1, None, ALU.arith_shift_right))
    ch.link(dve.tensor_scalar(tj, ti, -1.0, MAGIC, ALU.mult, ALU.add))
    r = tj.bitcast(F32)
    for step in range(3):
        ch.link(dve.tensor_tensor(t, r, r, ALU.mult))
        ch.link(dve.scalar_tensor_tensor(t, t, -0.5, ve, ALU.mult, ALU.mult))
        ch.link(dve.scalar_tensor_tensor(rs, t, 1.5, r, ALU.add, ALU.mult))
        r = rs
    return dve.scalar_tensor_tensor(nm, mv[:, :, 0], -1.0, rs, ALU.mult, ALU.mult)


def phase_a(nc, T, x_in, wT_in, kh, vh):
    X, ident = T["X"], T["ident"]
    with ExitStack() as c:
        sb = lambda n, s, dt=F32: c.enter_context(nc.sbuf_tensor("a_" + n, s, dt))
        sem = lambda n: c.enter_context(nc.semaphore("a_" + n))
        wT = sb("wT", [P, KC, D])
        st = sb("st", [P, NT, 6]); mv = sb("mv", [P, NT, 2])
        ve = sb("ve", [P, NT]); ti = sb("ti", [P, NT], I32); tj = sb("tj", [P, NT], I32); tt = sb("tt", [P, NT])
        rs = sb("rs", [P, NT]); nm = sb("nm", [P, NT])
        xa = sb("xa", [P, 2, GT, D]); xaT = sb("xaT", [P, 2, KC, GTOK]); vs = sb("vs", [P, 2, GT, D])
        psT = c.enter_context(nc.psum_tensor("a_psT", [P, 2, KC, GTOK], F32))
        psV = c.enter_context(nc.psum_tensor("a_psV", [P, 2, GT, D], F32))
        x_loaded = [sem(f"x_loaded{g}") for g in range(NG)]
        w_loaded = sem("w_loaded")
        chain = sem("chain"); stats = sem("stats")
        tanh_done = sem("tanh_done"); turned = sem("turned"); turned_kept = sem("turned_kept")
        v_done = sem("v_done"); v_kept = sem("v_kept")
        k_stored = [sem(f"k_stored{i}") for i in range(2)]
        v_stored = [sem(f"v_stored{i}") for i in range(2)]
        block = c.enter_context(nc.Block())

        @block.sync
        def _(sp):
            xt = x_in.rearrange("(n p) c -> p n c", p=P)
            sp.dma_start(X[:, 0:GT], xt[:, 0:GT]).then_inc(x_loaded[0], 16)
            sp.dma_start(wT[:], wT_in.rearrange("(k p) n -> p k n", p=P)).then_inc(w_loaded, 16)
            sp.dma_start(ident[:], T["ident_in"]).then_inc(w_loaded, 16)
            for g in range(1, NG):
                sp.dma_start(X[:, GT * g:GT * (g + 1)], xt[:, GT * g:GT * (g + 1)]).then_inc(x_loaded[g], 16)
            with sp.Fori(0, NG // 2) as i:
                for par in range(2):
                    g = 2 * i + par
                    sp.wait_ge(tanh_done, g * GT + GT)
                    for j in range(GT):
                        t0 = g * GTOK + j * P
                        sp.dma_start(kh[:, bass.ds(t0, P), :].rearrange("h t e -> t h e"),
                                     xa[:, par, j].rearrange("p (h e) -> p h e", h=H)).then_inc(k_stored[par], 16)
                    sp.wait_ge(v_kept, g + 1)
                    for j in range(GT):
                        t0 = g * GTOK + j * P
                        sp.dma_start(vh[:, bass.ds(t0, P), :].rearrange("h t e -> t h e"),
                                     vs[:, par, j].rearrange("p (h e) -> p h e", h=H)).then_inc(v_stored[par], 16)
            for par in range(2):
                sp.wait_ge(k_stored[par], NG // 2 * GT * 16 + GT * 16)
                sp.wait_ge(v_stored[par], NG // 2 * GT * 16 + GT * 16)

        @block.vector
        def _(dve):
            for par in range(2):
                dve.sem_inc(v_stored[par], GT * 16)
            ch = Chain(dve, chain)
            for g in range(NG):
                dve.wait_ge(x_loaded[g], 16)
                for n in range(GT * g, GT * g + GT):
                    last = nc.vector.bn_stats(st[:, n], X[:, n])
                ch.link(last)
                for n in range(GT * g, GT * g + GT):
                    last = nc.vector.bn_aggr(mv[:, n], st[:, n])
            ch.link(last)
            rstd(nc.vector, ch, mv[:], ve[:], ti[:], tj[:], tt[:], rs[:], nm[:]).then_inc(stats, 1)
            with dve.Fori(0, NG // 2) as i:
                for par in range(2):
                    g = 2 * i + par
                    dve.wait_ge(turned, g + 1)
                    nc.vector.tensor_copy(xaT[:, par], psT[:, par]).then_inc(turned_kept, 1)
                    dve.wait_ge(v_done, g + 1)
                    dve.wait_ge(v_stored[par], i * (GT * 16) + GT * 16)
                    nc.vector.tensor_copy(vs[:, par], psV[:, par]).then_inc(v_kept, 1)

        @block.scalar
        def _(act):
            for par in range(2):
                act.sem_inc(k_stored[par], GT * 16)
            act.wait_ge(stats, 1)
            with act.Fori(0, NG // 2) as i:
                for par in range(2):
                    g = 2 * i + par
                    act.wait_ge(k_stored[par], i * (GT * 16) + GT * 16)
                    act.wait_ge(turned_kept, g + 1)
                    for j in range(GT):
                        n = g * GT + j
                        nc.scalar.activation(xa[:, par, j], X[:, bass.ds(n, 1), :].rearrange("p a c -> p (a c)"), ACT.Tanh,
                                             bias=nm[:, bass.ds(n, 1)], scale=rs[:, bass.ds(n, 1)]).then_inc(tanh_done, 1)

        @block.tensor
        def _(pe):
            pe.sem_inc(turned_kept, 2)
            pe.wait_ge(w_loaded, 32)
            with pe.Fori(0, NG // 2) as i:
                for par in range(2):
                    g = 2 * i + par
                    pe.wait_ge(tanh_done, g * GT + GT)
                    pe.wait_ge(turned_kept, g + 1)
                    for k in range(KC):
                        for j in range(GT):
                            last = nc.tensor.transpose(psT[:, par, k, j * P:(j + 1) * P],
                                                       xa[:, par, j, k * P:(k + 1) * P], ident[:])
                    last.then_inc(turned, 1)
                    pe.wait_ge(turned_kept, g + 3)
                    for j in range(GT):
                        for k in range(KC):
                            last = nc.tensor.matmul(psV[:, par, j], xaT[:, par, k, j * P:(j + 1) * P], wT[:, k],
                                                    start=(k == 0), stop=(k == KC - 1))
                    last.then_inc(v_done, 1)


def head_quarters(ap, b):
    return ap[:, b * L:(b + 1) * L].rearrange("h (q t) e -> h q (t e)", q=L // NQ)


def phase_b(nc, T, eta_in, logit_in, kh, vh, kd, kt, tm, vg, w1):
    lam_c = T["lam_c"]
    with ExitStack() as c:
        sb = lambda n, s, dt=F32: c.enter_context(nc.sbuf_tensor("b_" + n, s, dt))
        sem = lambda n: c.enter_context(nc.semaphore("b_" + n))
        Kq = sb("Kq", [P, NQ, d]); Vq = sb("Vq", [P, NQ, d]); S1 = sb("S1", [P, NQ * d])
        prod = sb("prod", [P, 2, 4096])
        N = sb("N", [P, QB, C, C]); Tm = sb("Tm", [P, QB, C, C])
        ksq = sb("ksq", [P, NQ])
        s_in = sb("s_in", [P, 2]); s_t = sb("s_t", [P, 4])
        pw = sb("pw", [P, C]); pwK = sb("pwK", [P, C]); cN = sb("cN", [P, C, C])
        scal_loaded = sem("scal_loaded"); k_loaded = sem("k_loaded"); v_loaded = sem("v_loaded")
        chain = sem("chain"); pchain = sem("pchain")
        expz = sem("expz"); zeroed = sem("zeroed")
        prod_ready = sem("prod_ready"); prod_used = sem("prod_used")
        vg_ready = sem("vg_ready"); vg_stored = sem("vg_stored")
        kd_ready = sem("kd_ready"); kt_ready = sem("kt_ready"); tm_ready = sem("tm_ready"); w1_ready = sem("w1_ready")
        neg_z = sem("neg_z"); stored = sem("stored")
        block = c.enter_context(nc.Block())
        Kb = Kq[:].rearrange("p (n i) e -> p n i e", i=C)
        HB = QB // 2
        items = [(i, hf) for i in range(1, C) for hf in range(2)] + [(C, hf) for hf in range(2)]

        @block.sync
        def _(sp):
            sp.dma_start(s_in[:, 0:1], logit_in.to_broadcast([P, 1])).then_inc(scal_loaded, 16)
            sp.dma_start(s_in[:, 1:2], eta_in.to_broadcast([P, 1])).then_inc(scal_loaded, 16)
            for b in range(B):
                sp.dma_start(Kq[64 * b:64 * b + 64].rearrange("p t e -> p (t e)"), head_quarters(kh, b)).then_inc(k_loaded, 16)
            for b in range(B):
                sp.dma_start(Vq[64 * b:64 * b + 64].rearrange("p t e -> p (t e)"), head_quarters(vh, b)).then_inc(v_loaded, 16)
            sp.wait_ge(vg_ready, 1)
            for b in range(B):
                for g in range(VG):
                    dst = vg[:, g, b * L:(b + 1) * L].rearrange("h (q t) w -> h q (t w)", q=L // NQ)
                    sp.dma_start(dst, S1[64 * b:64 * b + 64, g * NQ * VW:(g + 1) * NQ * VW]).then_inc(vg_stored, 16)
            sp.wait_ge(kd_ready, 1)
            for b in range(B):
                sp.dma_start(head_quarters(kd, b), Vq[64 * b:64 * b + 64].rearrange("p t e -> p (t e)")).then_inc(stored, 16)
            sp.wait_ge(kt_ready, 1)
            for b in range(B):
                sp.dma_start(head_quarters(kt, b), S1[64 * b:64 * b + 64]).then_inc(stored, 16)
            sp.wait_ge(w1_ready, 1)
            for b in range(B):
                sp.dma_start(w1[:, b * L:(b + 1) * L].rearrange("h (q t) -> h q t", q=L // NQ), ksq[64 * b:64 * b + 64]).then_inc(stored, 16)
            sp.wait_ge(tm_ready, 1)
            for b in range(B):
                dst = tm[:, b * L // C:(b + 1) * L // C].rearrange("h (q n) m -> h q (n m)", q=L // NQ)
                sp.dma_start(dst, Tm[64 * b:64 * b + 64].rearrange("p n i j -> p (n i j)")).then_inc(stored, 16)
            sp.wait_ge(vg_stored, 16 * B * VG)
            sp.wait_ge(stored, 16 * B * 4)

        @block.scalar
        def _(act):
            act.wait_ge(scal_loaded, 32)
            nc.scalar.activation(s_t[:, 0:1], s_in[:, 0:1], ACT.Exp, scale=-1.0).then_inc(expz, 1)
            act.wait_ge(v_loaded, 32)
            nc.scalar.activation(S1[:].rearrange("p (g t w) -> p g t w", g=VG, w=VW),
                                 Vq[:].rearrange("p t (g w) -> p g t w", g=VG), ACT.Copy).then_inc(vg_ready, 1)

        @block.gpsimd
        def _(pool):
            nc.gpsimd.memset(N[:], 0.0).then_inc(pchain, 1)
            nc.gpsimd.memset(cN[:], 0.0).then_inc(pchain, 1)
            nc.gpsimd.memset(Tm[:], 0.0).then_inc(pchain, 1)
            pool.wait_ge(pchain, 3)
            nc.gpsimd.memset(Tm[:].rearrange("p n i j -> p n (i j)")[:, :, 0:C * C:C + 1], 1.0).then_inc(zeroed, 1)
            pool.wait_ge(k_loaded, 32)
            for m, (i, hf) in enumerate(items):
                if m >= 2:
                    pool.wait_ge(prod_used, m - 1)
                n0 = hf * HB
                if i < C:
                    o = prod[:, m % 2, 0:HB * i * d].rearrange("p (n j e) -> p n j e", n=HB, j=i)
                    a = Kb[:, n0:n0 + HB, i:i + 1].to_broadcast([P, HB, i, d])
                    bb = Kb[:, n0:n0 + HB, 0:i]
                else:
                    o = prod[:, m % 2].rearrange("p (n j e) -> p n j e", n=HB, j=C)
                    a = bb = Kb[:, n0:n0 + HB]
                nc.gpsimd.tensor_tensor(o, a, bb, ALU.mult).then_inc(prod_ready, 1)

        @block.vector
        def _(dve):
            v = nc.vector
            ch = Chain(dve, chain)
            dve.wait_ge(expz, 1)
            ch.link(v.tensor_scalar(s_t[:, 1:2], s_t[:, 0:1], 1.0, None, ALU.add))
            ch.link(v.reciprocal(pw[:, 0:1], s_t[:, 1:2]))
            ch.link(v.tensor_scalar(s_t[:, 2:3], pw[:, 0:1], -1.0, 1.0, ALU.mult, ALU.add))
            ch.link(v.scalar_tensor_tensor(pwK[:, C - 1:C], s_t[:, 2:3], 1.0 / d, s_in[:, 1:2], ALU.mult, ALU.mult))
            for n in range(1, C):
                v.tensor_tensor(pw[:, n:n + 1], pw[:, n - 1:n], pw[:, 0:1], ALU.mult)
                ch.link(v.tensor_tensor(pwK[:, C - 1 - n:C - n], pwK[:, C - n:C - n + 1], pw[:, 0:1], ALU.mult))
            v.tensor_scalar(s_t[:, 3:4], pwK[:, C - 1:C], -1.0, None, ALU.mult)
            ch.link(v.tensor_copy(lam_c[:], pw[:, C - 1:C]))
            dve.wait_ge(zeroed, 1)
            for i in range(1, C):
                last = v.tensor_copy(cN[:, i, 0:i], pwK[:, C - 1 - i:C - 1])
            ch.link(last)
            dve.wait_ge(k_loaded, 32)
            dve.wait_ge(vg_ready, 1)
            v.tensor_tensor(Vq[:].rearrange("p (n i) e -> p n i e", i=C), Kb,
                            pw[:].unsqueeze(1).unsqueeze(3).to_broadcast([P, QB, C, d]), ALU.mult).then_inc(kd_ready, 1)

            def sums(ms):
                for m in ms:
                    i, hf = items[m]
                    n0 = hf * HB
                    dve.wait_ge(prod_ready, m + 1)
                    if i < C:
                        src = prod[:, m % 2, 0:HB * i * d].rearrange("p (n j e) -> p n j e", n=HB, j=i)
                        dst = N[:, n0:n0 + HB, i, 0:i]
                    else:
                        src = prod[:, m % 2].rearrange("p (t e) -> p t e", e=d)
                        dst = ksq[:, n0 * C:(n0 + HB) * C]
                    v.tensor_reduce(dst, src, AX.X, ALU.add).then_inc(prod_used, 1)

            sums(range(0, 6))
            dve.wait_ge(vg_stored, 16 * B * VG)
            v.tensor_tensor(S1[:].rearrange("p (n i e) -> p n i e", i=C, e=d), Kb,
                            pwK[:].unsqueeze(1).unsqueeze(3).to_broadcast([P, QB, C, d]), ALU.mult).then_inc(kt_ready, 1)
            sums(range(6, len(items)))
            dve.wait_ge(prod_used, len(items))
            v.tensor_scalar(ksq[:], ksq[:], s_t[:, 3:4], 1.0, ALU.mult, ALU.add).then_inc(w1_ready, 1)
            ch.link(v.tensor_tensor(N[:], N[:], cN[:].unsqueeze(1).to_broadcast([P, QB, C, C]), ALU.mult))
            for i in range(1, C):
                t = prod[:, 0, 0:QB * i * i].rearrange("p (n j k) -> p n j k", n=QB, j=i)
                ch.link(v.tensor_tensor(t, N[:, :, i:i + 1, 0:i].to_broadcast([P, QB, i, i]),
                                        Tm[:, :, 0:i, 0:i].rearrange("p n k j -> p n j k"), ALU.mult))
                ins = v.tensor_reduce(Tm[:, :, i, 0:i], t, AX.X, ALU.add, negate=True)
                if i < C - 1:
                    ch.link(ins)
                else:
                    ins.then_inc(tm_ready, 1)


def phase_c(nc, T, W, kd, kt, tm, vg, vh, w1, ug, yd, xp, qp, vx):
    X, ident, lam_c = T["X"], T["ident"], T["lam_c"]
    with ExitStack() as c:
        sb = lambda n, s, dt=F32: c.enter_context(nc.sbuf_tensor("c_" + n, s, dt))
        ps = lambda n, s: c.enter_context(nc.psum_tensor("c_" + n, s, F32))
        sem = lambda n: c.enter_context(nc.semaphore("c_" + n))
        kdb = sb("kdb", [P, 4, QT, d]); ktb = sb("ktb", [P, 4, QT, d]); tmb = sb("tmb", [P, 4, QBLK, C, C])
        vb = sb("vb", [P, 4, QT, VW]); ub = sb("ub", [P, 4, QT, VW])
        t1 = sb("t1", [P, C, VW, d]); pr = sb("pr", [P, C, VW]); rr = sb("rr", [P, C, VW]); t2 = sb("t2", [P, C, VW, C])
        t3 = sb("t3", [P, VW, d, C]); s3 = sb("s3", [P, VW * d]); S = sb("S", [P, VW * d])
        uR = sb("uR", [P, VG, SR, VW]); vR = sb("vR", [P, SR, d]); w1R = sb("w1R", [P, SR])
        tO = sb("tO", [P, SR, d]); yR = sb("yR", [P, SR, d])
        gam = sb("gam", [P, D]); bet = sb("bet", [P, D]); gbias = sb("gbias", [P, NE]); low = sb("low", [P, NE, NE])
        Y = sb("Y", [P, GT, D]); xn = sb("xn", [P, GT, D]); xnT = sb("xnT", [P, KC, GTOK])
        st = sb("st", [P, GT, 6]); mv = sb("mv", [P, GT, 2])
        ve = sb("ve", [P, GT]); ti = sb("ti", [P, GT], I32); tj = sb("tj", [P, GT], I32); tt = sb("tt", [P, GT])
        rs = [sb(f"rs{i}", [P, GT]) for i in range(3)]; nm = [sb(f"nm{i}", [P, GT]) for i in range(3)]
        gw = sb("gw", [P, KC, NE]); wg = sb("wg", [P, KC, NE, I_E]); wu = sb("wu", [P, KC, NE, I_E]); wd = sb("wd", [P, NE, D])
        ez = sb("ez", [P, GT, NE]); e1 = sb("e1", [P, GT, NE]); sco = sb("sco", [P, GT, NE]); sfc = sb("sfc", [P, GT, NE])
        gs = sb("gs", [P, GT, NGRP]); gsel = sb("gsel", [P, GT, NGRP]); sel = sb("sel", [P, GT, NE]); tmpc = sb("tmpc", [P, GT, NE])
        cge = sb("cge", [P, GT, NE, NE]); cgt = sb("cgt", [P, GT, NE, NE]); rank = sb("rank", [P, GT, NE])
        wsum = sb("wsum", [P, GT]); wt = sb("wt", [P, GT, NE])
        sg = sb("sg", [P, 2, GTOK]); uu = sb("uu", [P, 2, GTOK]); wb = sb("wb", [P, 2, GTOK]); hh = sb("hh", [P, 2, GTOK])
        wv = sb("wv", [P, KC, D]); wa = sb("wa", [P, KC, P]); vbias = sb("vbias", [1, D]); ones = sb("ones", [1, P])
        part = sb("part", [P, 2, 3, KC, GTOK], BF16); rest = sb("rest", [P, 2, KC, GTOK]); qf = sb("qf", [P, KC, GTOK])
        vst = sb("vst", [P, H, GT, 32])
        psT = ps("psT", [P, KC, GTOK]); psGU = ps("psGU", [P, 2, GTOK]); psB = ps("psB", [P, 2, GTOK]); psY = ps("psY", [P, GT, D])

        seg_loaded = [sem(f"seg_loaded{q}") for q in range(4)]
        u_stored = [sem(f"u_stored{q}") for q in range(4)]
        w_loaded = sem("w_loaded"); quarter_done = sem("quarter_done"); chain = sem("chain"); pchain = sem("pchain")
        r_loaded = sem("r_loaded"); y_ready = sem("y_ready"); y_stored = sem("y_stored"); y_loaded = sem("y_loaded")
        moe_done = sem("moe_done")
        stats1 = sem("stats1"); normed1 = sem("normed1"); x1_done = sem("x1_done")
        stats2 = sem("stats2"); normed2 = sem("normed2"); turned = sem("turned"); turned_kept = sem("turned_kept")
        logits = sem("logits"); exp_done = sem("exp_done"); weights = sem("weights")
        gu_done = sem("gu_done"); gu_kept = sem("gu_kept"); wb_done = sem("wb_done"); wb_kept = sem("wb_kept")
        h_done = sem("h_done"); down_done = sem("down_done")
        stats3 = sem("stats3"); stats3_seen = sem("stats3_seen"); x2_seen = sem("x2_seen"); normed3 = sem("normed3"); turned3 = sem("turned3"); turned3_kept = sem("turned3_kept")
        q_done = sem("q_done"); v_done = sem("v_done"); v_kept = sem("v_kept"); staged = sem("staged")
        high = sem("high"); rested = sem("rested"); mid = sem("mid"); low_done = sem("low_done"); d_stored = sem("d_stored")
        WLOADS = 16 * 13
        D_SHARE = 16 * 7 * B
        block = c.enter_context(nc.Block())
        X4 = X[:].rearrange("p (b t) c -> p b t c", b=B)

        @block.sync
        def _(sp):
            def load_quarter(s, q):
                for b in range(B):
                    t0 = s * SEG + (b * L + q * QT)
                    n0 = s * (SEG // C) + (b * L + q * QT) // C
                    pb = slice(64 * b, 64 * b + 64)
                    for buf, src in ((kdb, kd), (ktb, kt)):
                        sp.dma_start(buf[pb, q].rearrange("p t e -> p (t e)"),
                                     src[:, bass.ds(t0, QT)].rearrange("h t e -> h (t e)").unsqueeze(1).to_broadcast([H, VG, QT * d])
                                     ).then_inc(seg_loaded[q], 16)
                    sp.dma_start(tmb[pb, q].rearrange("p n i j -> p (n i j)"),
                                 tm[:, bass.ds(n0, QBLK)].rearrange("h n m -> h (n m)").unsqueeze(1).to_broadcast([H, VG, QBLK * C * C])
                                 ).then_inc(seg_loaded[q], 16)
                    sp.dma_start(vb[pb, q].rearrange("p t w -> p (t w)"),
                                 vg[:, :, bass.ds(t0, QT)].rearrange("h g t w -> h g (t w)")).then_inc(seg_loaded[q], 16)

            def store_u(s, q):
                for b in range(B):
                    t0 = s * SEG + (b * L + q * QT)
                    sp.dma_start(ug[:, :, bass.ds(t0, QT)].rearrange("h g t w -> h g (t w)"),
                                 ub[64 * b:64 * b + 64, q].rearrange("p t w -> p (t w)")).then_inc(u_stored[q], 16)

            def output_rows(u):
                for q in range(4):
                    sp.wait_ge(u_stored[q], u * (16 * B) + 16 * B)
                sp.wait_ge(moe_done, u + 1)
                for b in range(B):
                    t0 = u * SEG + b * L
                    pb = slice(64 * b, 64 * b + 64)
                    for g in range(VG):
                        sp.dma_start(uR[pb, g].rearrange("p t w -> p (t w)"),
                                     ug[:, g, bass.ds(t0, SEG)].rearrange("h (r t) w -> h r (t w)", r=4)).then_inc(r_loaded, 16)
                    sp.dma_start(vR[pb].rearrange("p t e -> p (t e)"),
                                 vh[:, bass.ds(t0, SEG)].rearrange("h (r t) e -> h r (t e)", r=4)).then_inc(r_loaded, 16)
                    sp.dma_start(w1R[pb],
                                 w1[:, bass.ds(t0, SEG)].rearrange("h (r t) -> h r t", r=4)).then_inc(r_loaded, 16)
                sp.wait_ge(y_ready, u + 1)
                for b in range(B):
                    for r in range(4):
                        t0 = u * SEG + (b * L + r * SR)
                        sp.dma_start(yd[bass.ds(t0, SR)].rearrange("t (h e) -> h t e", h=H),
                                     yR[64 * b + r:64 * b + 64:4]).then_inc(y_stored, 16)
                sp.wait_ge(y_stored, u * (64 * B) + 64 * B)
                for b in range(B):
                    sp.dma_start(Y[:, 2 * b:2 * b + 2],
                                 yd[bass.ds(u * SEG + b * L, SEG)].rearrange("(j p) c -> p j c", p=P)).then_inc(y_loaded, 16)

            def store_operands(u):
                sp.wait_ge(v_kept, u + 1)
                sp.wait_ge(low_done, u + 1)
                for b in range(B):
                    for a, dst in enumerate((xp, qp)):
                        for m in range(3):
                            sp.dma_start(dst[m, b].rearrange("(k p) t -> p k t", p=P)[:, :, bass.ds(u * SEG, SEG)],
                                         part[:, a, m, :, b * SEG:(b + 1) * SEG]).then_inc(d_stored, 16)
                    sp.dma_start(vx[b * H:(b + 1) * H, :, bass.ds(u * (GT // B), GT // B)].rearrange("h p k e -> p h (k e)"),
                                 vst[:, :, b * (GT // B):(b + 1) * (GT // B)].rearrange("p h k e -> p h (k e)")).then_inc(d_stored, 16)

            def after_segment(s):
                for q in range(4):
                    sp.wait_ge(quarter_done, s * 4 + (q - 3))
                    store_u(s - 1, q)
                    load_quarter(s, q)
                output_rows(s - 1)

            for q in range(4):
                load_quarter(0, q)
            for dst, src in ((gam, W["gamma"]), (bet, W["beta"]), (gbias, W["bias"])):
                sp.dma_start(dst[:], src.to_broadcast([P, src.shape[1]])).then_inc(w_loaded, 16)
            sp.dma_start(low[:].rearrange("p i j -> p (i j)"), W["low"].to_broadcast([P, NE * NE])).then_inc(w_loaded, 16)
            sp.dma_start(gw[:], W["gwT"].rearrange("(k p) e -> p k e", p=P)).then_inc(w_loaded, 16)
            for k in range(KC):
                sp.dma_start(wg[:, k], W["wgT"][k * P:(k + 1) * P]).then_inc(w_loaded, 16)
                sp.dma_start(wu[:, k], W["wuT"][k * P:(k + 1) * P]).then_inc(w_loaded, 16)
            sp.dma_start(wd[:], W["wdT"]).then_inc(w_loaded, 16)
            sp.dma_start(wv[:], W["wvT"].rearrange("(k p) n -> p k n", p=P)).then_inc(w_loaded, 16)
            sp.dma_start(wa[:], W["wa"].rearrange("(k p) n -> p k n", p=P)).then_inc(w_loaded, 16)
            sp.dma_start(vbias[:], W["wv_b"]).then_inc(w_loaded, 16)
            after_segment(1)
            with sp.Fori(2, NSEG) as s:
                after_segment(s)
                store_operands(s - 2)
            for q in range(4):
                sp.wait_ge(quarter_done, NSEG * 4 - 3 + q)
                store_u(NSEG - 1, q)
            output_rows(NSEG - 1)
            store_operands(NSEG - 2)
            store_operands(NSEG - 1)
            sp.wait_ge(d_stored, NSEG * D_SHARE + D_SHARE)

        @block.vector
        def _(dve):
            v = nc.vector
            ch = Chain(dve, chain)
            S3 = S[:].rearrange("p (w k) -> p w k", w=VW)

            def block_step(s, q, i):
                t = slice(C * i, C * i + C)
                u = ub[:, q, t]
                ch.link(v.tensor_tensor(t1[:], kdb[:, q, t].unsqueeze(2).to_broadcast([P, C, VW, d]),
                                        S3.unsqueeze(1).to_broadcast([P, C, VW, d]), ALU.mult))
                ch.link(v.tensor_reduce(pr[:], t1[:], AX.X, ALU.add))
                ch.link(v.tensor_tensor(rr[:], vb[:, q, t], pr[:], ALU.subtract))
                ch.link(v.tensor_tensor(t2[:], tmb[:, q, i].unsqueeze(2).to_broadcast([P, C, VW, C]),
                                        rr[:].rearrange("p j w -> p w j").unsqueeze(1).to_broadcast([P, C, VW, C]), ALU.mult))
                ch.link(v.tensor_reduce(u, t2[:], AX.X, ALU.add))
                ch.link(v.tensor_tensor(t3[:], ktb[:, q, t].rearrange("p i k -> p k i").unsqueeze(1).to_broadcast([P, VW, d, C]),
                                        u.rearrange("p i w -> p w i").unsqueeze(2).to_broadcast([P, VW, d, C]), ALU.mult))
                ch.link(v.tensor_reduce(s3[:], t3[:], AX.X, ALU.add))
                new = v.scalar_tensor_tensor(S[:], S[:], lam_c[:], s3[:], ALU.mult, ALU.add)
                if i < QBLK - 1:
                    ch.link(new)
                else:
                    new.then_inc(quarter_done, 1)
                    dve.wait_ge(quarter_done, s * 4 + (q + 1))

            def stats(src, i, signal):
                for j in range(GT):
                    last = v.bn_stats(st[:, j], src(j))
                ch.link(last)
                for j in range(GT):
                    last = v.bn_aggr(mv[:, j], st[:, j])
                ch.link(last)
                rstd(v, ch, mv[:], ve[:], ti[:], tj[:], tt[:], rs[i][:], nm[i][:]).then_inc(signal, 1)

            def ranks(x, n, out):
                ge, gt = cge[:, :, 0:n, 0:n], cgt[:, :, 0:n, 0:n]
                xj = x.unsqueeze(2).to_broadcast([P, GT, n, n])
                xi = x.unsqueeze(3).to_broadcast([P, GT, n, n])
                v.tensor_tensor(ge, xj, xi, ALU.is_ge)
                ch.link(v.tensor_tensor(gt, xj, xi, ALU.is_gt))
                ch.link(v.tensor_tensor(ge, ge, gt, ALU.subtract))
                ch.link(v.tensor_tensor(ge, ge, low[:, 0:n, 0:n].unsqueeze(1).to_broadcast([P, GT, n, n]), ALU.mult))
                ch.link(v.tensor_tensor(gt, gt, ge, ALU.add))
                ch.link(v.tensor_reduce(rank[:, :, 0:n], gt, AX.X, ALU.add))
                ch.link(v.tensor_scalar(out, rank[:, :, 0:n], 1.5, None, ALU.is_lt))

            def gate():
                ch.link(v.tensor_scalar(e1[:], ez[:], 1.0, None, ALU.add))
                ch.link(v.reciprocal(sco[:], e1[:]))
                ch.link(v.tensor_tensor(sfc[:], sco[:], gbias[:].unsqueeze(1).to_broadcast([P, GT, NE]), ALU.add))
                ch.link(v.tensor_tensor(gs[:], sfc[:, :, 0::2], sfc[:, :, 1::2], ALU.add))
                ranks(gs[:], NGRP, gsel[:])
                ch.link(v.tensor_tensor(tmpc[:].rearrange("p t (g m) -> p t g m", m=2), sfc[:].rearrange("p t (g m) -> p t g m", m=2),
                                        gsel[:].unsqueeze(3).to_broadcast([P, GT, NGRP, 2]), ALU.mult))
                ranks(tmpc[:], NE, sel[:])
                ch.link(v.tensor_tensor(sel[:], sel[:], sco[:], ALU.mult))
                ch.link(v.tensor_reduce(wsum[:], sel[:], AX.X, ALU.add))
                ch.link(v.tensor_scalar(wsum[:], wsum[:], 1e-20, None, ALU.add))
                ch.link(v.reciprocal(wsum[:], wsum[:]))
                v.tensor_tensor(wt[:], sel[:], wsum[:].unsqueeze(2).to_broadcast([P, GT, NE]), ALU.mult).then_inc(weights, 1)

            def slot(u, n):
                if n == 0:
                    dve.wait_ge(y_loaded, u * (16 * B) + 16 * B)
                    stats(lambda j: Y[:, j], 0, stats1)
                if n == 1:
                    dve.wait_ge(x1_done, u + 1)
                    stats(lambda j: X4[:, j // 2, bass.ds(2 * u + j % 2, 1)].rearrange("p a c -> p (a c)"), 1, stats2)
                if n == 2:
                    dve.wait_ge(exp_done, u + 1)
                    gate()
                if n == 3:
                    dve.wait_ge(down_done, u * NE + NE)
                    xs = X4[:, :, bass.ds(2 * u, 2)]
                    v.tensor_tensor(xs, xs, psY[:].rearrange("p (b t) c -> p b t c", b=B), ALU.add).then_inc(moe_done, 1)
                    dve.wait_ge(moe_done, u + 2)
                    dve.sem_inc(x2_seen, 1)
                    stats(lambda j: X4[:, j // 2, bass.ds(2 * u + j % 2, 1)].rearrange("p a c -> p (a c)"), 2, stats3)

            def segment(s, slots):
                for q in range(4):
                    dve.wait_ge(seg_loaded[q], s * (128 * 1) + 128)
                    if slots:
                        dve.wait_ge(u_stored[q], s * (16 * B))
                    for i in range(QBLK):
                        block_step(s, q, i)
                        n = q * QBLK + i
                        if slots and n in SLOTS:
                            slot(s - 1, SLOTS.index(n))

            SLOTS = [7, 12, 16, 31]
            ch.link(v.memset(ones[:], 1.0))
            dve.sem_inc(moe_done, 1)
            ch.link(v.memset(S[:], 0.0))
            dve.wait_ge(w_loaded, WLOADS)
            segment(0, False)
            with dve.Fori(1, NSEG) as s:
                dve.wait_ge(w_loaded, WLOADS)
                ch.clear()
                segment(s, True)
            dve.wait_ge(w_loaded, WLOADS)
            ch.clear()
            for n in range(4):
                slot(NSEG - 1, n)

        def loops(eng, body):
            with eng.Fori(0, NSEG) as u:
                body(u)

        @block.gpsimd
        def _(pool):
            g_ = nc.gpsimd
            ch = Chain(pool, pchain)
            ch.link(g_.memset(vst[:], 0.0))
            g_.memset(vst[:, :, :, d:d + 1], 1.0).then_inc(staged, 1)
            ch.clear()
            pool.wait_ge(w_loaded, WLOADS)

            def operands(u):
                for i, whole in enumerate((xnT, qf)):
                    pool.wait_ge(high, u * 2 + (i + 1))
                    g_.tensor_tensor(rest[:, i], whole[:], part[:, i, 0], ALU.subtract).then_inc(rested, 1)
                for i in range(2):
                    pool.wait_ge(mid, u * 2 + (i + 1))
                    last = g_.tensor_tensor(part[:, i, 2], rest[:, i], part[:, i, 1], ALU.subtract)
                last.then_inc(low_done, 1)

            def group(u):
                pool.wait_ge(r_loaded, u * (16 * 12) + 16 * 12)
                ch.link(g_.tensor_tensor(tO[:].rearrange("p t (g w) -> p g t w", g=VG), uR[:],
                                         w1R[:].unsqueeze(1).unsqueeze(3).to_broadcast([P, VG, SR, VW]), ALU.mult))
                ch.link(g_.tensor_tensor(tO[:], vR[:], tO[:], ALU.subtract))
                g_.tensor_tensor(yR[:], vR[:], tO[:], ALU.add).then_inc(y_ready, 1)
                pool.wait_ge(normed1, u + 1)
                ch.link(g_.tensor_tensor(Y[:], Y[:], gam[:].unsqueeze(1).to_broadcast([P, GT, D]), ALU.mult))
                ch.link(g_.tensor_tensor(Y[:], Y[:], bet[:].unsqueeze(1).to_broadcast([P, GT, D]), ALU.add))
                xs = X4[:, :, bass.ds(2 * u, 2)]
                g_.tensor_tensor(xs, xs, Y[:].rearrange("p (b t) c -> p b t c", b=B), ALU.add).then_inc(x1_done, 1)
                for e in range(NE):
                    pool.wait_ge(wb_kept, u * NE + (e + 1))
                    ch.link(g_.tensor_tensor(sg[:, e % 2], sg[:, e % 2], wb[:, e % 2], ALU.mult))
                    if e >= 2:
                        pool.wait_ge(down_done, u * NE + (e - 1))
                    g_.tensor_tensor(hh[:, e % 2], sg[:, e % 2], uu[:, e % 2], ALU.mult).then_inc(h_done, 1)
                ch.clear()
                operands(u)

            loops(pool, group)

        @block.scalar
        def _(act):
            a = nc.scalar
            act.sem_inc(d_stored, D_SHARE)
            act.wait_ge(staged, 1)

            def operands(u):
                act.wait_ge(stats3, u + 1)
                act.sem_inc(stats3_seen, 1)
                for j in range(GT):
                    xj = X4[:, j // 2, bass.ds(2 * u + j % 2, 1)].rearrange("p a c -> p (a c)")
                    last = a.activation(xn[:, j], xj, ACT.Identity, bias=nm[2][:, j:j + 1], scale=rs[2][:, j:j + 1])
                last.then_inc(normed3, 1)
                act.wait_ge(turned3, u + 1)
                a.activation(xnT[:], psT[:], ACT.Copy).then_inc(turned3_kept, 1)
                act.wait_ge(d_stored, u * D_SHARE + D_SHARE)
                a.activation(part[:, 0, 0], psT[:], ACT.Copy).then_inc(high, 1)
                act.wait_ge(q_done, u + 1)
                a.activation(qf[:], psGU[:], ACT.Copy)
                a.activation(part[:, 1, 0], psGU[:], ACT.Copy).then_inc(high, 1)
                for i in range(2):
                    act.wait_ge(rested, u * 2 + (i + 1))
                    a.activation(part[:, i, 1], rest[:, i], ACT.Copy).then_inc(mid, 1)
                act.wait_ge(v_done, u + 1)
                a.activation(vst[:, :, :, 0:d].rearrange("p h t e -> p t h e"),
                             psB[:].rearrange("p a (j h e) -> p (a j) h e", h=H, e=d), ACT.Copy).then_inc(v_kept, 1)

            def group(u):
                act.wait_ge(stats1, u + 1)
                for j in range(GT):
                    last = a.activation(Y[:, j], Y[:, j], ACT.Identity, bias=nm[0][:, j:j + 1], scale=rs[0][:, j:j + 1])
                last.then_inc(normed1, 1)
                act.wait_ge(stats2, u + 1)
                for j in range(GT):
                    xj = X4[:, j // 2, bass.ds(2 * u + j % 2, 1)].rearrange("p a c -> p (a c)")
                    last = a.activation(xn[:, j], xj, ACT.Identity, bias=nm[1][:, j:j + 1], scale=rs[1][:, j:j + 1])
                last.then_inc(normed2, 1)
                act.wait_ge(turned, u + 1)
                a.activation(xnT[:], psT[:], ACT.Copy).then_inc(turned_kept, 1)
                act.wait_ge(logits, u + 1)
                a.activation(ez[:], psT[:, 0, 0:GT * NE].rearrange("p (t e) -> p t e", e=NE), ACT.Exp, scale=-1.0).then_inc(exp_done, 1)
                for e in range(NE):
                    act.wait_ge(gu_done, u * NE + (e + 1))
                    if e >= 2:
                        act.wait_ge(h_done, u * NE + (e - 1))
                    a.activation(sg[:, e % 2], psGU[:, 0], ACT.Silu)
                    a.activation(uu[:, e % 2], psGU[:, 1], ACT.Copy).then_inc(gu_kept, 1)
                    act.wait_ge(wb_done, u * NE + (e + 1))
                    a.activation(wb[:, e % 2], psB[:, e % 2], ACT.Copy).then_inc(wb_kept, 1)
                operands(u)

            loops(act, group)

        @block.tensor
        def _(pe):
            t = nc.tensor
            pe.wait_ge(w_loaded, WLOADS)
            psV = psB[:].rearrange("p a (j c) -> p (a j) c", c=D)

            def operands(u):
                pe.wait_ge(normed3, u + 1)
                for k in range(KC):
                    for j in range(GT):
                        last = t.transpose(psT[:, k, j * P:(j + 1) * P], xn[:, j, k * P:(k + 1) * P], ident[:])
                last.then_inc(turned3, 1)
                pe.wait_ge(turned3_kept, u + 1)
                for k in range(KC):
                    last = t.matmul(psGU[:, k], wa[:, k], xnT[:, k], start=True, stop=True)
                last.then_inc(q_done, 1)
                for j in range(GT):
                    for k in range(KC):
                        t.matmul(psV[:, j], xnT[:, k, j * P:(j + 1) * P], wv[:, k], start=(k == 0), stop=False)
                    last = t.matmul(psV[:, j], ones[:], vbias[:], start=False, stop=True)
                last.then_inc(v_done, 1)

            def group(u):
                pe.wait_ge(normed2, u + 1)
                pe.wait_ge(moe_done, u + 1)
                for k in range(KC):
                    for j in range(GT):
                        last = t.transpose(psT[:, k, j * P:(j + 1) * P], xn[:, j, k * P:(k + 1) * P], ident[:])
                last.then_inc(turned, 1)
                pe.wait_ge(turned_kept, u + 1)
                for j in range(GT):
                    for k in range(KC):
                        last = t.matmul(psT[:, 0, j * NE:(j + 1) * NE], xnT[:, k, j * P:(j + 1) * P], gw[:, k],
                                        start=(k == 0), stop=(k == KC - 1))
                last.then_inc(logits, 1)

                def gate_up(e):
                    if e >= 1:
                        pe.wait_ge(gu_kept, u * NE + e)
                    for i, w in enumerate((wg, wu)):
                        for k in range(KC):
                            last = t.matmul(psGU[:, i], w[:, k, e], xnT[:, k], start=(k == 0), stop=(k == KC - 1))
                    last.then_inc(gu_done, 1)

                def spread(e):
                    if e == 0:
                        pe.wait_ge(weights, u + 1)
                    if e >= 2:
                        pe.wait_ge(wb_kept, u * NE + (e - 1))
                    for j in range(GT):
                        last = t.matmul(psB[:, e % 2, j * P:(j + 1) * P], wt[:, j, e:e + 1].to_broadcast([P, P]), ident[:],
                                        start=True, stop=True)
                    last.then_inc(wb_done, 1)

                def down(e):
                    pe.wait_ge(h_done, u * NE + (e + 1))
                    for j in range(GT):
                        last = t.matmul(psY[:, j], hh[:, e % 2, j * P:(j + 1) * P], wd[:, e],
                                        start=(e == 0 and j % 2 == 0), stop=(e == NE - 1), skip_group_check=True)
                    last.then_inc(down_done, 1)

                for e in range(NE):
                    gate_up(e)
                    spread(e)
                    if e >= 1:
                        down(e - 1)
                down(NE - 1)
                operands(u)

            loops(pe, group)


NH = B * H
KR = 6 * d
SPLIT_Q = (0, 0, 0, 1, 1, 2)
SPLIT_X = (0, 1, 2, 0, 1, 0)
RING = 4
KT = L // P
QC = 512
NQC = L // QC
MB = 3
LEAD = 8


def phase_e(nc, T, W, xp, qp, vx):
    ident, O2 = T["ident"], T["O2"]
    with ExitStack() as c:
        sb = lambda n, s, dt=F32: c.enter_context(nc.sbuf_tensor("e_" + n, s, dt))
        ps = lambda n, s: c.enter_context(nc.psum_tensor("e_" + n, s, F32))
        sem = lambda n: c.enter_context(nc.semaphore("e_" + n))
        wi = sb("wi", [P, 3, KC * HID], I32)
        XS = [sb(f"XS{i}", [P, L], BF16) for i in range(RING)]
        QS = [sb(f"QS{i}", [P, L], BF16) for i in range(RING)]
        Vh = [sb(f"Vh{i}", [P, KT, 32]) for i in range(2)]
        Pt = [sb(f"Pt{i}", [P, L]) for i in range(2)]
        oT = [sb(f"oT{i}", [P, QC]) for i in range(2)]
        mx = [sb(f"mx{i}", [P, KT, NQC]) for i in range(2)]
        one = sb("one", [P, KT]); mneg = sb("mneg", [P, KT]); mr = sb("mr", [P, KT]); M3 = sb("M3", [P, 3, 32], BF16)
        MT = [sb(f"MT{i}", [P, 3, 32], BF16) for i in range(2)]
        rden = sb("rden", [P, NQC, NQC])
        psS = [ps(f"psS{i}", [P, 2, QC]) for i in range(2)]
        psM = [ps(f"psM{i}", [P, QC]) for i in range(MB)]
        psO = ps("psO", [P, QC])
        stacks = sem("stacks"); v_loaded = sem("v_loaded"); ones = sem("ones")
        max_ready = sem("max_ready"); max_used = sem("max_used"); m_ready = sem("m_ready"); m_loaded = sem("m_loaded")
        wi_loaded = sem("wi_loaded"); m_whole = sem("m_whole"); m_split = sem("m_split"); pchain = sem("pchain")
        scores = sem("scores"); exp_done = sem("exp_done"); av_done = sem("av_done")
        o_kept = sem("o_kept"); o_turned = sem("o_turned"); normed = sem("normed"); chain = sem("chain")
        block = c.enter_context(nc.Block())
        SHARE = 16 * 12
        MT_OF = KT * NQC
        TURN_KT = 2
        TURN_AT = (TURN_KT + LEAD + 1) * NQC

        def place(c):
            return c if c < TURN_AT else c + 1

        def heads(body):
            def run(eng):
                body(0, 0)
                with eng.Fori(0, NH // RING - 1) as i:
                    for k in range(RING):
                        body(i * RING + (1 + k), (1 + k) % RING)
                for n in range(NH - RING + 1, NH):
                    body(n, n % RING)
            return run

        def is_there(n):
            return not isinstance(n, int) or 0 <= n < NH

        @block.sync
        def _(sp):
            def load_stacks(n, r):
                for row, (mq, mk) in enumerate(zip(SPLIT_Q, SPLIT_X)):
                    rows = slice(row * d, row * d + d)
                    sp.dma_start(QS[r % RING][rows], qp[mq].rearrange("b c t -> (b c) t")[bass.ds(n * d, d)]).then_inc(stacks, 16)
                    sp.dma_start(XS[r % RING][rows], xp[mk].rearrange("b c t -> (b c) t")[bass.ds(n * d, d)]).then_inc(stacks, 16)

            def load_values(n, r):
                sp.dma_start(Vh[r % 2][:].rearrange("p k e -> p (k e)"),
                             vx[bass.ds(n, 1)].rearrange("n p k e -> (n p) (k e)")).then_inc(v_loaded, 16)

            def load_max(n, r):
                sp.wait_ge(ones, 1)
                sp.wait_ge(m_ready, n + 1)
                for m in range(3):
                    for q4 in range(4):
                        dst = QS[r % RING][KR + m:KR + m + 1].rearrange("p (t q c) -> p q t c", q=4, c=32)[:, q4]
                        sp.dma_start(dst, MT[r % 2][32 * q4:32 * q4 + KT, m]).then_inc(m_loaded, 16)

            load_stacks(0, 0)
            sp.wait_ge(stacks, SHARE)
            load_stacks(1, 1)
            load_values(0, 0)
            load_max(0, 0)
            for i, (src, k) in enumerate(((W["fgT"], KC), (W["fuT"], KC), (W["fdT"], HC))):
                sp.dma_start(wi[:, i].rearrange("p (k n) -> p k n", k=k), src.rearrange("(k p) n -> p k n", p=P)).then_inc(wi_loaded, 16)

            def head(n, r):
                if not isinstance(n, int) or n > 0:
                    sp.wait_ge(av_done, n * KT)
                if is_there(n + 2):
                    sp.wait_ge(stacks, n * SHARE + 2 * SHARE)
                    load_stacks(n + 2, r + 2)
                if is_there(n + 1):
                    sp.wait_ge(v_loaded, n * 16 + 16)
                    load_values(n + 1, r + 1)
                    load_max(n + 1, r + 1)

            heads(head)(sp)

        @block.vector
        def _(dve):
            v = nc.vector
            ch = Chain(dve, chain)
            v.memset(M3[:], 0.0)
            v.memset(one[:], 1.0)
            for i in range(RING):
                v.memset(QS[i][KR:P], 0.0)
                last = v.memset(XS[i][KR:P], 0.0)
            ch.link(last)
            for i in range(RING):
                last = v.memset(XS[i][KR:KR + 3], 1.0)
            last.then_inc(ones, 1)

            def tile_max(n, r, t):
                for q in range(NQC):
                    dve.wait_ge(max_ready, n * MT_OF + (t * NQC + q + 1))
                    v.reduce_max(mx[r % 2][:, t, q:q + 1], psM[place(t * NQC + q) % MB][:], AX.X).then_inc(max_used, 1)
                if t == KT - 1:
                    dve.wait_ge(max_used, n * MT_OF + MT_OF)
                    if is_there(n - 1):
                        dve.wait_ge(m_split, n)
                    v.tensor_reduce(mneg[:], mx[r % 2][:], AX.X, ALU.max, negate=True).then_inc(m_whole, 1)

            def turn_max(n, r):
                dve.wait_ge(m_split, n + 1)
                if not isinstance(n, int) or n >= 2:
                    dve.wait_ge(m_loaded, n * SHARE - SHARE)
                v.transpose(MT[r % 2][:].rearrange("p m c -> p (m c)"), M3[:].rearrange("p m c -> p (m c)")).then_inc(m_ready, 1)

            def norm(n):
                dve.wait_ge(o_turned, n + 1)
                x = psM[TURN_AT % MB][:].rearrange("p (c j e) -> p j c e", c=NQC, e=32)
                ch.link(v.reciprocal(rden[:], x[:, :, :, d]))
                o = O2[:, bass.ds(n, 1)].rearrange("p a (j c) e -> p (a j) c e", j=NQC)
                v.tensor_tensor(o, x[:, :, :, 0:d], rden[:].unsqueeze(3).to_broadcast([P, NQC, NQC, d]), ALU.mult).then_inc(normed, 1)
                dve.wait_ge(normed, n + 1)

            for t in range(KT):
                tile_max(0, 0, t)
            for t in range(LEAD):
                tile_max(1, 1, t)
                if t == 0:
                    turn_max(0, 0)
            ch.clear()

            def head(n, r):
                for kt in range(KT):
                    ahead, t = 1 + (kt + LEAD) // KT, (kt + LEAD) % KT
                    if is_there(n + ahead):
                        tile_max(n + ahead, r + ahead, t)
                    if t == 0 and is_there(n + 1):
                        turn_max(n + 1, r + 1)
                    if kt == TURN_KT and is_there(n - 1):
                        norm(n - 1)
                ch.clear()

            heads(head)(dve)
            norm(NH - 1)

        @block.gpsimd
        def _(pool):
            g_ = nc.gpsimd
            ch = Chain(pool, pchain)
            pool.wait_ge(ones, 1)

            def convert_weights():
                pool.wait_ge(wi_loaded, 48)
                for i, w in enumerate((T["wg"], T["wu"], T["wd"])):
                    g_.tensor_copy(w[:].rearrange("p k n -> p (k n)"), wi[:, i])

            def head(n, r):
                pool.wait_ge(m_whole, n + 1)
                if is_there(n - 1):
                    pool.wait_ge(m_ready, n)
                ch.link(g_.tensor_tensor(M3[:, 0, 0:KT], mneg[:], one[:], ALU.mult))
                ch.link(g_.tensor_tensor(mr[:], mneg[:], M3[:, 0, 0:KT], ALU.subtract))
                ch.link(g_.tensor_tensor(M3[:, 1, 0:KT], mr[:], one[:], ALU.mult))
                g_.tensor_tensor(M3[:, 2, 0:KT], mr[:], M3[:, 1, 0:KT], ALU.subtract).then_inc(m_split, 1)
                ch.clear()
                if isinstance(n, int) and n == 0:
                    convert_weights()

            heads(head)(pool)

        @block.scalar
        def _(act):
            a = nc.scalar

            def keep_output(n, r):
                act.wait_ge(av_done, n * KT + KT)
                a.activation(oT[r % 2][:], psO[:], ACT.Copy).then_inc(o_kept, 1)

            def head(n, r):
                for kt in range(KT):
                    if not isinstance(n, int) or n * KT + kt >= 2:
                        act.wait_ge(av_done, n * KT + (kt - 1))
                    for half in range(2):
                        act.wait_ge(scores, n * (2 * KT) + (2 * kt + half + 1))
                        a.activation(Pt[kt % 2][:, half * 2 * QC:(half + 1) * 2 * QC], psS[half][:].rearrange("p a c -> p (a c)"),
                                     ACT.Exp, scale=float(d) ** -0.5).then_inc(exp_done, 1)
                    if kt == 0 and is_there(n - 1):
                        keep_output(n - 1, r + 1)

            heads(head)(act)
            keep_output(NH - 1, NH - 1)

        @block.tensor
        def _(pe):
            t_ = nc.tensor

            def for_max(n, r, t, q):
                if t == 0 and q == 0:
                    pe.wait_ge(stacks, n * SHARE + SHARE)
                at = place(t * NQC + q)
                if at - MB == TURN_AT:
                    if not isinstance(n, int) or n >= 2:
                        pe.wait_ge(normed, n - 1)
                elif at >= MB:
                    pe.wait_ge(max_used, n * MT_OF + (at - MB if at - MB < TURN_AT else at - MB - 1) + 1)
                elif is_there(n - 1):
                    past = [p for p in range(MT_OF + 1) if p % MB == at][-1]
                    pe.wait_ge(max_used, n * MT_OF + (past - MT_OF))
                t_.matmul(psM[at % MB][:], QS[r % RING][0:KR, t * P:(t + 1) * P], XS[r % RING][0:KR, q * QC:(q + 1) * QC],
                          start=True, stop=True).then_inc(max_ready, 1)

            def for_exp(n, r, kt, half, wait):
                if wait is not None:
                    pe.wait_ge(exp_done, wait)
                for q in range(2):
                    q0 = (half * 2 + q) * QC
                    last = t_.matmul(psS[half][:, q], XS[r % RING][:, kt * P:(kt + 1) * P], QS[r % RING][:, q0:q0 + QC],
                                     start=True, stop=True)
                last.then_inc(scores, 1)

            def times_values(n, r, kt):
                if kt == 0:
                    pe.wait_ge(v_loaded, n * 16 + 16)
                    if is_there(n - 1):
                        pe.wait_ge(o_kept, n)
                for j in range(NQC):
                    last = t_.matmul(psO[32 * j:32 * j + 32], Vh[r % 2][:, kt], Pt[kt % 2][:, j * QC:(j + 1) * QC],
                                     start=(kt == 0), stop=(kt == KT - 1))
                last.then_inc(av_done, 1)

            def turn_output(n, r):
                pe.wait_ge(o_kept, n + 1)
                if isinstance(n, int) and n >= NH - 2:
                    pe.wait_ge(max_used, NH * MT_OF)
                else:
                    pe.wait_ge(max_used, n * MT_OF + (2 * MT_OF + TURN_AT - MB + 1))
                for cc in range(NQC):
                    last = t_.transpose(psM[TURN_AT % MB][:, cc * P:(cc + 1) * P], oT[r % 2][:, cc * P:(cc + 1) * P], ident[:])
                last.then_inc(o_turned, 1)

            for t in range(KT):
                for q in range(NQC):
                    for_max(0, 0, t, q)
            for t in range(LEAD):
                for q in range(NQC):
                    for_max(1, 1, t, q)
            pe.wait_ge(ones, 1)
            pe.wait_ge(m_loaded, SHARE)
            for half in range(2):
                for_exp(0, 0, 0, half, None)

            def head(n, r):
                for kt in range(KT):
                    k = n * (2 * KT) + 2 * kt
                    ahead, t = 1 + (kt + LEAD) // KT, (kt + LEAD) % KT
                    nn, nr, nk = (n, r, kt + 1) if kt < KT - 1 else (n + 1, r + 1, 0)
                    if kt == KT - 1 and is_there(nn):
                        pe.wait_ge(m_loaded, n * SHARE + 2 * SHARE)
                    for half in range(2):
                        if is_there(nn):
                            for_exp(nn, nr, nk, half, k + (half + 1))
                        if is_there(n + ahead):
                            for_max(n + ahead, r + ahead, t, half)
                    if is_there(n + ahead):
                        for_max(n + ahead, r + ahead, t, 2)
                    if not is_there(nn):
                        pe.wait_ge(exp_done, k + 2)
                    times_values(n, r, kt)
                    if is_there(n + ahead):
                        for_max(n + ahead, r + ahead, t, 3)
                    if kt == TURN_KT and is_there(n - 1):
                        turn_output(n - 1, r + 1)

            heads(head)(pe)
            pe.wait_ge(normed, NH - 1)
            turn_output(NH - 1, NH - 1)


def phase_f(nc, T, W, out):
    X, ident, O2, wg, wu, wd = T["X"], T["ident"], T["O2"], T["wg"], T["wu"], T["wd"]
    with ExitStack() as c:
        sb = lambda n, s, dt=F32: c.enter_context(nc.sbuf_tensor("f_" + n, s, dt))
        ps = lambda n, s: c.enter_context(nc.psum_tensor("f_" + n, s, F32))
        sem = lambda n: c.enter_context(nc.semaphore("f_" + n))
        ow = sb("ow", [P, KC, D]); obias = sb("obias", [P, D])
        ot = sb("ot", [P, GT, D]); otT = sb("otT", [P, KC, GTOK]); xn = sb("xn", [P, GT, D])
        xh = sb("xh", [P, 2, KC, GTOK], F32R)
        st = sb("st", [P, GT, 6]); mv = sb("mv", [P, GT, 2])
        ve = sb("ve", [P, GT]); ti = sb("ti", [P, GT], I32); tj = sb("tj", [P, GT], I32); tt = sb("tt", [P, GT])
        rs = sb("rs", [P, GT]); nm = sb("nm", [P, GT])
        sg = sb("sg", [P, 2, GTOK]); hf = sb("hf", [P, 2, GTOK]); hp = sb("hp", [P, 2, 2, GTOK], F32R)
        yo = sb("yo", [P, GT, D])
        psT = ps("psT", [P, KC, GTOK]); psY = ps("psY", [P, GT, D])
        psG = [ps(f"psG{i}", [P, GTOK]) for i in range(2)]; psU = [ps(f"psU{i}", [P, GTOK]) for i in range(2)]
        psP = psT[:].rearrange("p k (j c) -> p (k j) c", c=D)
        w_loaded = sem("w_loaded"); chain = sem("chain")
        gathered = sem("gathered"); turned_o = sem("turned_o"); kept_o = sem("kept_o"); biased = sem("biased"); projected = sem("projected")
        stats = sem("stats"); normed = sem("normed"); turned = sem("turned"); high = sem("high"); low = sem("low")
        g_done = sem("g_done"); silu_done = sem("silu_done"); h_done = sem("h_done"); hh_done = sem("hh_done"); hl_done = sem("hl_done")
        down_done = sem("down_done"); y_done = sem("y_done"); stored = sem("stored")
        block = c.enter_context(nc.Block())
        GB = NG // B

        def groups(eng, first, step):
            o2 = lambda b, i: O2[:, b * H:(b + 1) * H, bass.ds(i * GT, GT), :]
            first(0, o2(0, 0))
            for b in range(B):
                with eng.Fori(0, GB - 1) as i:
                    step(i + b * GB, (i + (b * GB + 1), o2(b, i + 1)))
                step(b * GB + GB - 1, ((b + 1) * GB, o2(b + 1, 0)) if b < B - 1 else None)

        @block.sync
        def _(sp):
            sp.dma_start(ow[:], W["owT"].rearrange("(k p) n -> p k n", p=P)).then_inc(w_loaded, 16)
            sp.dma_start(obias[:], W["out_b"].to_broadcast([P, D])).then_inc(w_loaded, 16)
            with sp.Fori(0, NG) as g:
                sp.wait_ge(y_done, g + 2)
                sp.dma_start(out[bass.ds(g * GTOK, GTOK)].rearrange("(j p) c -> p j c", p=P), yo[:]).then_inc(stored, 16)
            sp.wait_ge(stored, NG * 16 + 16)

        @block.gpsimd
        def _(pool):
            pool.wait_ge(w_loaded, 32)
            with pool.Fori(0, NG) as g:
                xs = X[:, bass.ds(g * GT, GT)]
                nc.gpsimd.tensor_tensor(xs, xs, obias[:].unsqueeze(1).to_broadcast([P, GT, D]), ALU.add).then_inc(biased, 1)

        @block.scalar
        def _(act):
            a = nc.scalar

            def gather(g, o2):
                a.activation(ot[:].rearrange("p t (h e) -> p t h e", h=H), o2.rearrange("p h t e -> p t h e"), ACT.Copy).then_inc(gathered, 1)

            def keep(g):
                act.wait_ge(turned_o, g + 1)
                a.activation(otT[:], psT[:], ACT.Copy).then_inc(kept_o, 1)

            def norm(g):
                act.wait_ge(stats, g + 1)
                for j in range(GT):
                    last = a.activation(xn[:, j], X[:, bass.ds(g * GT + j, 1)].rearrange("p a c -> p (a c)"), ACT.Identity,
                                        bias=nm[:, j:j + 1], scale=rs[:, j:j + 1])
                last.then_inc(normed, 1)

            def round_high(g):
                act.wait_ge(turned, g + 1)
                a.activation(xh[:, 0], psT[:], ACT.Copy).then_inc(high, 1)

            def first(g, o2):
                gather(g, o2)
                keep(g)
                norm(g)
                round_high(g)

            def step(g, after):
                for m in range(HC):
                    act.wait_ge(g_done, g * HC + (m + 1))
                    a.activation(sg[:, m % 2], psG[m % 2][:], ACT.Silu, scale=FSCALE).then_inc(silu_done, 1)
                    if after and m == HC - 1:
                        round_high(after[0])
                    act.wait_ge(h_done, g * HC + (m + 3))
                    act.wait_ge(down_done, g * HC + (m + 1))
                    a.activation(hp[:, m % 2, 0], hf[:, m % 2], ACT.Copy).then_inc(hh_done, 1)
                    if after and m == 0:
                        gather(*after)
                    if after and m == 1:
                        keep(after[0])
                    if after and m == 3:
                        norm(after[0])

            groups(act, first, step)

        @block.vector
        def _(dve):
            v = nc.vector
            ch = Chain(dve, chain)
            dve.sem_inc(stored, 16)
            dve.sem_inc(y_done, 1)
            dve.sem_inc(h_done, 2)

            def residual(g):
                xs = X[:, bass.ds(g * GT, GT)]
                dve.wait_ge(biased, g + 1)
                dve.wait_ge(projected, g + 1)
                ch.link(v.tensor_tensor(xs, xs, psP, ALU.add))
                for j in range(GT):
                    last = v.bn_stats(st[:, j], X[:, bass.ds(g * GT + j, 1)].rearrange("p a c -> p (a c)"))
                return last

            def moments(g, after_stats):
                ch.link(after_stats)
                for j in range(GT):
                    last = v.bn_aggr(mv[:, j], st[:, j])
                ch.link(last)
                rstd(v, ch, mv[:], ve[:], ti[:], tj[:], tt[:], rs[:], nm[:]).then_inc(stats, 1)

            def round_low(g):
                dve.wait_ge(high, g + 1)
                v.tensor_tensor(xh[:, 1], psT[:], xh[:, 0], ALU.subtract).then_inc(low, 1)

            def first(g, o2):
                moments(g, residual(g))
                round_low(g)
                ch.clear()

            def step(g, after):
                for m in range(HC):
                    dve.wait_ge(silu_done, g * HC + (m + 1))
                    v.tensor_tensor(hf[:, m % 2], psU[m % 2][:], sg[:, m % 2], ALU.mult).then_inc(h_done, 1)
                    if after and m == HC - 1:
                        round_low(after[0])
                    dve.wait_ge(hh_done, g * HC + (m + 1))
                    v.tensor_tensor(hp[:, m % 2, 1], hf[:, m % 2], hp[:, m % 2, 0], ALU.subtract).then_inc(hl_done, 1)
                    if after and m == 2:
                        moments(after[0], residual(after[0]))
                dve.wait_ge(down_done, g * HC + (HC + 2))
                dve.wait_ge(stored, g * 16 + 16)
                v.scalar_tensor_tensor(yo[:].rearrange("p t c -> p (t c)"), psY[:].rearrange("p t c -> p (t c)"), FSCALE * FSCALE,
                                       X[:, bass.ds(g * GT, GT)].rearrange("p t c -> p (t c)"), ALU.mult, ALU.add).then_inc(y_done, 1)
                ch.clear()

            groups(dve, first, step)

        @block.tensor
        def _(pe):
            t = nc.tensor
            pe.wait_ge(w_loaded, 32)
            pe.sem_inc(down_done, 2)

            def turn(src, signal):
                for k in range(KC):
                    for j in range(GT):
                        last = t.transpose(psT[:, k, j * P:(j + 1) * P], src[:, j, k * P:(k + 1) * P], ident[:])
                last.then_inc(signal, 1)

            def turn_output(g):
                pe.wait_ge(gathered, g + 1)
                turn(ot, turned_o)

            def project(g):
                pe.wait_ge(kept_o, g + 1)
                for j in range(GT):
                    for k in range(KC):
                        last = t.matmul(psP[:, j], otT[:, k, j * P:(j + 1) * P], ow[:, k], start=(k == 0), stop=(k == KC - 1))
                last.then_inc(projected, 1)

            def turn_normed(g):
                pe.wait_ge(normed, g + 1)
                turn(xn, turned)

            def first(g, o2):
                turn_output(g)
                project(g)
                turn_normed(g)

            def step(g, after):
                def up(m):
                    pe.wait_ge(h_done, g * HC + (m + 1))
                    for w, o in ((wg, psG[m % 2]), (wu, psU[m % 2])):
                        n = 0
                        for k in range(KC):
                            for part in range(2):
                                last = t.matmul(o[:], w[:, k, m * P:(m + 1) * P], xh[:, part, k], start=(n == 0), stop=(n == 2 * KC - 1))
                                n += 1
                    last.then_inc(g_done, 1)

                def down(m):
                    pe.wait_ge(hl_done, g * HC + (m + 1))
                    if m == 0:
                        pe.wait_ge(y_done, g + 1)
                    for j in range(GT):
                        for part in range(2):
                            last = t.matmul(psY[:, j], hp[:, m % 2, part, j * P:(j + 1) * P], wd[:, m],
                                            start=(m == 0 and j % 2 == 0 and part == 0), stop=(m == HC - 1 and part == 1),
                                            skip_group_check=True)
                    last.then_inc(down_done, 1)

                pe.wait_ge(low, g + 1)
                for m in range(HC):
                    up(m)
                    if after and m == HC - 1:
                        turn_normed(after[0])
                    if m >= 1:
                        down(m - 1)
                    if after and m == 1:
                        turn_output(after[0])
                    if after and m == 2:
                        project(after[0])
                down(HC - 1)

            groups(pe, first, step)


def build(nc, a, out):
    scratch = lambda n, s, dt=F32: nc.dram_tensor(n, s, dt, kind="Internal").ap()
    with ExitStack() as c:
        sb = lambda n, s, dt=F32: c.enter_context(nc.sbuf_tensor(n, s, dt))
        T = {"ident_in": a["ident"]}
        T["X"] = sb("X", [P, NT, D])
        T["ident"] = sb("ident", [P, P])
        T["lam_c"] = sb("lam_c", [P, 1])
        kh = scratch("kh", (H, BL, d)); vh = scratch("vh", (H, BL, d))
        kd = scratch("kd", (H, BL, d)); kt = scratch("kt", (H, BL, d))
        tm = scratch("tm", (H, BL // C, C * C)); vg = scratch("vg", (H, VG, BL, VW)); w1 = scratch("w1", (H, BL))
        ug = scratch("ug", (H, VG, BL, VW)); yd = scratch("yd", (BL, D))
        xp = scratch("xp", (3, B, D, L), BF16); qp = scratch("qp", (3, B, D, L), BF16); vx = scratch("vx", (NH, P, KT, 32))
        phase_a(nc, T, a["x"], a["wT"], kh, vh)
        phase_b(nc, T, a["eta"], a["lam_logit"], kh, vh, kd, kt, tm, vg, w1)
        phase_c(nc, T, a, kd, kt, tm, vg, vh, w1, ug, yd, xp, qp, vx)
        T["O2"] = sb("O2", [P, NH, KT, d])
        T["wg"] = sb("wg", [P, KC, HID], F32R); T["wu"] = sb("wu", [P, KC, HID], F32R); T["wd"] = sb("wd", [P, HC, D], F32R)
        phase_e(nc, T, a, xp, qp, vx)
        phase_f(nc, T, a, out)


def laid_out(i):
    wa = np.zeros((D, P), np.float32)
    for h in range(H):
        hh = h % (P // d)
        wa[h * d:(h + 1) * d, hh * d:(hh + 1) * d] = i["L1_attn_w_att_val"][h]
    return {
        "x": i["L0_attn_x"].reshape(BL, D),
        "wT": i["L0_attn_W"].T,
        "gamma": i["L0_attn_ln_gamma"].reshape(1, D),
        "beta": i["L0_attn_ln_beta"].reshape(1, D),
        "eta": i["L0_attn_eta"].reshape(1, 1),
        "lam_logit": i["L0_attn_lam_logit"].reshape(1, 1),
        "gwT": i["L0_ffn_gate_weight"].T,
        "bias": i["L0_ffn_e_score_correction_bias"].reshape(1, NE),
        "wgT": i["L0_ffn_gate_proj"].transpose(2, 0, 1),
        "wuT": i["L0_ffn_up_proj"].transpose(2, 0, 1),
        "wdT": i["L0_ffn_down_proj"].transpose(2, 0, 1),
        "wa": wa,
        "wvT": i["L1_attn_wv_w"].T,
        "wv_b": i["L1_attn_wv_b"].reshape(1, D),
        "owT": i["L1_attn_out_w"].T,
        "out_b": i["L1_attn_out_b"].reshape(1, D),
        "fgT": i["L1_ffn_w_gate"].T,
        "fuT": i["L1_ffn_w_up"].T,
        "fdT": i["L1_ffn_w_down"].T,
        "ident": np.eye(P, dtype=np.float32),
        "low": np.tril(np.ones((NE, NE), np.float32), -1).reshape(1, NE * NE),
    }


def kernel(**inputs):
    import concourse.bacc as _bacc
    from concourse.bass_utils import run_bass_kernel_spmd as _run

    nc = _bacc.Bacc("TRN2", target_bir_lowering=False, num_devices=1)
    arrays = {f"in_{n}": np.ascontiguousarray(v) for n, v in laid_out({n: np.asarray(v) for n, v in inputs.items()}).items()}
    args = {n[3:]: nc.dram_tensor(n, v.shape, mybir.dt.from_np(v.dtype), kind="ExternalInput").ap() for n, v in arrays.items()}
    out = nc.dram_tensor("out", (BL, D), F32, kind="ExternalOutput").ap()
    build(nc, args, out)
    r = _run(nc, [arrays], core_ids=[0])
    return r.results[0]["out"].reshape(B, L, D)
```

```python
import numpy as np
import concourse.bass as bass
from concourse import mybir
from contextlib import ExitStack

P = 128
ALU = mybir.AluOpType
ACT = mybir.ActivationFunctionType
AX = mybir.AxisListType
F32 = mybir.dt.float32
BF16 = mybir.dt.bfloat16
I32 = mybir.dt.int32
F32R = mybir.dt.float32r

B, L, D, H = 2, 2048, 256, 16
d = D // H
BL = B * L
NT = BL // P
TPB = L // P
KC = D // P
GT = 4
NG = NT // GT
GTOK = GT * P
EPS = 1e-5

C = 8
VG = 4
VW = d // VG
NQ = L // (P // (B * H))
QB = NQ // C
SEG = 256
NSEG = L // SEG
QT = SEG // 4
QBLK = QT // C
SR = SEG // 4

NE, I_E = 8, 128
NGRP = 4
HID = 768
HC = HID // P
FSCALE = 1.0 / 127.0

MAGIC = float(0x5F3759DF)


class Chain:

    def __init__(self, eng, sem):
        self.eng, self.sem, self.n = eng, sem, 0

    def link(self, ins):
        self.n += 1
        ins.then_inc(self.sem, 1)
        self.eng.wait_ge(self.sem, self.n)

    def clear(self):
        self.eng.sem_clear(self.sem)
        self.n = 0


def rstd(dve, ch, mv, ve, ti, tj, t, rs, nm):
    ch.link(dve.tensor_scalar(ve, mv[:, :, 1], EPS, None, ALU.add))
    ch.link(dve.tensor_scalar(ti, ve.bitcast(I32), 1, None, ALU.arith_shift_right))
    ch.link(dve.tensor_scalar(tj, ti, -1.0, MAGIC, ALU.mult, ALU.add))
    r = tj.bitcast(F32)
    for step in range(3):
        ch.link(dve.tensor_tensor(t, r, r, ALU.mult))
        ch.link(dve.scalar_tensor_tensor(t, t, -0.5, ve, ALU.mult, ALU.mult))
        ch.link(dve.scalar_tensor_tensor(rs, t, 1.5, r, ALU.add, ALU.mult))
        r = rs
    return dve.scalar_tensor_tensor(nm, mv[:, :, 0], -1.0, rs, ALU.mult, ALU.mult)


def phase_a(nc, T, x_in, wT_in, kh, vh):
    X, ident = T["X"], T["ident"]
    with ExitStack() as c:
        sb = lambda n, s, dt=F32: c.enter_context(nc.sbuf_tensor("a_" + n, s, dt))
        sem = lambda n: c.enter_context(nc.semaphore("a_" + n))
        wT = sb("wT", [P, KC, D])
        st = sb("st", [P, GT, 6]); mv = sb("mv", [P, GT, 2])
        ve = sb("ve", [P, GT]); ti = sb("ti", [P, GT], I32); tj = sb("tj", [P, GT], I32); tt = sb("tt", [P, GT])
        rs = [sb(f"rs{i}", [P, GT]) for i in range(2)]; nm = [sb(f"nm{i}", [P, GT]) for i in range(2)]
        xa = sb("xa", [P, 2, GT, D]); xaT = sb("xaT", [P, 2, KC, GTOK]); vs = sb("vs", [P, 2, GT, D])
        psT = c.enter_context(nc.psum_tensor("a_psT", [P, 2, KC, GTOK], F32))
        psV = c.enter_context(nc.psum_tensor("a_psV", [P, 2, GT, D], F32))
        x_loaded = [sem(f"x_loaded{i}") for i in range(2)]
        w_loaded = sem("w_loaded")
        chain = sem("chain"); stats = sem("stats")
        tanh_done = sem("tanh_done"); turned = sem("turned"); turned_kept = sem("turned_kept")
        v_done = sem("v_done"); v_kept = sem("v_kept")
        k_stored = [sem(f"k_stored{i}") for i in range(2)]
        v_stored = [sem(f"v_stored{i}") for i in range(2)]
        block = c.enter_context(nc.Block())

        @block.sync
        def _(sp):
            xt = x_in.rearrange("(n p) c -> p n c", p=P)
            for g in range(2):
                sp.dma_start(X[:, GT * g:GT * (g + 1)], xt[:, GT * g:GT * (g + 1)]).then_inc(x_loaded[g], 16)
            sp.dma_start(wT[:], wT_in.rearrange("(k p) n -> p k n", p=P)).then_inc(w_loaded, 16)
            sp.dma_start(ident[:], T["ident_in"]).then_inc(w_loaded, 16)
            for g in range(2, NG):
                sp.wait_ge(x_loaded[g % 2], g // 2 * 16)
                sp.dma_start(X[:, GT * g:GT * (g + 1)], xt[:, GT * g:GT * (g + 1)]).then_inc(x_loaded[g % 2], 16)
            with sp.Fori(0, NG // 2) as i:
                for par in range(2):
                    g = 2 * i + par
                    sp.wait_ge(tanh_done, g * GT + GT)
                    for j in range(GT):
                        t0 = g * GTOK + j * P
                        sp.dma_start(kh[:, bass.ds(t0, P), :].rearrange("h t e -> t h e"),
                                     xa[:, par, j].rearrange("p (h e) -> p h e", h=H)).then_inc(k_stored[par], 16)
                    sp.wait_ge(v_kept, g + 1)
                    for j in range(GT):
                        t0 = g * GTOK + j * P
                        sp.dma_start(vh[:, bass.ds(t0, P), :].rearrange("h t e -> t h e"),
                                     vs[:, par, j].rearrange("p (h e) -> p h e", h=H)).then_inc(v_stored[par], 16)
            for par in range(2):
                sp.wait_ge(k_stored[par], NG // 2 * GT * 16 + GT * 16)
                sp.wait_ge(v_stored[par], NG // 2 * GT * 16 + GT * 16)

        @block.vector
        def _(dve):
            v = nc.vector
            ch = Chain(dve, chain)

            def moments(g, par, i):
                dve.wait_ge(x_loaded[par], i * 16 + 16)
                for j in range(GT):
                    last = v.bn_stats(st[:, j], X[:, bass.ds(g * GT + j, 1)].rearrange("p a c -> p (a c)"))
                ch.link(last)
                for j in range(GT):
                    last = v.bn_aggr(mv[:, j], st[:, j])
                ch.link(last)
                rstd(v, ch, mv[:], ve[:], ti[:], tj[:], tt[:], rs[par][:], nm[par][:]).then_inc(stats, 1)

            def pair(i, more):
                for par in range(2):
                    g = 2 * i + par
                    dve.wait_ge(turned, g + 1)
                    v.tensor_copy(xaT[:, par], psT[:, par]).then_inc(turned_kept, 1)
                    if more:
                        moments(g + 2, par, i + 1)
                ch.clear()

            for par in range(2):
                moments(par, par, 0)
            ch.clear()
            with dve.Fori(0, NG // 2 - 1) as i:
                pair(i, True)
            pair(NG // 2 - 1, False)

        @block.scalar
        def _(act):
            a = nc.scalar
            for par in range(2):
                act.sem_inc(k_stored[par], GT * 16)
                act.sem_inc(v_stored[par], GT * 16)

            def keys(g, par, i):
                act.wait_ge(stats, g + 1)
                act.wait_ge(k_stored[par], i * (GT * 16) + GT * 16)
                act.wait_ge(turned_kept, g + 1)
                for j in range(GT):
                    a.activation(xa[:, par, j], X[:, bass.ds(g * GT + j, 1), :].rearrange("p a c -> p (a c)"), ACT.Tanh,
                                 bias=nm[par][:, j:j + 1], scale=rs[par][:, j:j + 1]).then_inc(tanh_done, 1)

            def values(g, par, i):
                act.wait_ge(v_done, g + 1)
                act.wait_ge(v_stored[par], i * (GT * 16) + GT * 16)
                a.activation(vs[:, par], psV[:, par], ACT.Copy).then_inc(v_kept, 1)

            keys(0, 0, 0)
            with act.Fori(0, NG // 2 - 1) as i:
                keys(2 * i + 1, 1, i)
                values(2 * i, 0, i)
                keys(2 * i + 2, 0, i + 1)
                values(2 * i + 1, 1, i)
            i = NG // 2 - 1
            keys(2 * i + 1, 1, i)
            values(2 * i, 0, i)
            values(2 * i + 1, 1, i)

        @block.tensor
        def _(pe):
            pe.sem_inc(turned_kept, 2)
            pe.wait_ge(w_loaded, 32)
            with pe.Fori(0, NG // 2) as i:
                for par in range(2):
                    g = 2 * i + par
                    pe.wait_ge(tanh_done, g * GT + GT)
                    pe.wait_ge(turned_kept, g + 1)
                    for k in range(KC):
                        for j in range(GT):
                            last = nc.tensor.transpose(psT[:, par, k, j * P:(j + 1) * P],
                                                       xa[:, par, j, k * P:(k + 1) * P], ident[:])
                    last.then_inc(turned, 1)
                    pe.wait_ge(turned_kept, g + 3)
                    for j in range(GT):
                        for k in range(KC):
                            last = nc.tensor.matmul(psV[:, par, j], xaT[:, par, k, j * P:(j + 1) * P], wT[:, k],
                                                    start=(k == 0), stop=(k == KC - 1))
                    last.then_inc(v_done, 1)


def head_quarters(ap, b):
    return ap[:, b * L:(b + 1) * L].rearrange("h (q t) e -> h q (t e)", q=L // NQ)


def phase_b(nc, T, eta_in, logit_in, kh, vh, kd, kt, tm, vg, w1):
    lam_c = T["lam_c"]
    with ExitStack() as c:
        sb = lambda n, s, dt=F32: c.enter_context(nc.sbuf_tensor("b_" + n, s, dt))
        sem = lambda n: c.enter_context(nc.semaphore("b_" + n))
        HB = QB // 2
        HQ = NQ // 2
        SQ = NQ // 8
        OWN = (2, 4)
        rows = [i for i in range(1, C) if i not in OWN]
        Kq = sb("Kq", [P, NQ, d]); Vq = sb("Vq", [P, NQ, d]); S1 = sb("S1", [P, NQ * d])
        prod = sb("prod", [P, 2, HB * (C - 1) * d]); own = sb("own", [P, HB * max(OWN) * d])
        sq = sb("sq", [P, 2, SQ, d])
        N = sb("N", [P, QB, C, C]); Tm = sb("Tm", [P, QB, C, C])
        ksq = sb("ksq", [P, NQ])
        s_in = sb("s_in", [P, 2]); s_t = sb("s_t", [P, 4])
        pw = sb("pw", [P, C]); pwK = sb("pwK", [P, C]); cN = sb("cN", [P, C, C])
        scal_loaded = sem("scal_loaded"); k_loaded = [sem(f"k_loaded{hf}") for hf in range(2)]; v_loaded = sem("v_loaded")
        chain = sem("chain"); pchain = sem("pchain")
        expz = sem("expz"); zeroed = sem("zeroed"); powers = sem("powers")
        prod_ready = sem("prod_ready"); prod_used = sem("prod_used"); sq_ready = sem("sq_ready"); sq_used = sem("sq_used")
        vg_ready = sem("vg_ready"); vg_stored = sem("vg_stored")
        kd_ready = sem("kd_ready"); kt_ready = sem("kt_ready"); tm_ready = sem("tm_ready"); w1_ready = sem("w1_ready")
        stored = sem("stored")
        block = c.enter_context(nc.Block())
        Kb = Kq[:].rearrange("p (n i) e -> p n i e", i=C)

        def pairs(ap, hf, i):
            return ap[:, 0:HB * i * d].rearrange("p (n j e) -> p n j e", n=HB, j=i)

        def multiply(eng, o, hf, i):
            n0 = hf * HB
            return eng.tensor_tensor(o, Kb[:, n0:n0 + HB, i:i + 1].to_broadcast([P, HB, i, d]), Kb[:, n0:n0 + HB, 0:i], ALU.mult)

        @block.sync
        def _(sp):
            sp.dma_start(s_in[:, 0:1], logit_in.to_broadcast([P, 1])).then_inc(scal_loaded, 16)
            sp.dma_start(s_in[:, 1:2], eta_in.to_broadcast([P, 1])).then_inc(scal_loaded, 16)
            for hf in range(2):
                for b in range(B):
                    sp.dma_start(Kq[64 * b:64 * b + 64, hf * HQ:(hf + 1) * HQ].rearrange("p t e -> p (t e)"),
                                 head_quarters(kh, b)[:, :, hf * HQ * d:(hf + 1) * HQ * d]).then_inc(k_loaded[hf], 16)
            for b in range(B):
                sp.dma_start(Vq[64 * b:64 * b + 64].rearrange("p t e -> p (t e)"), head_quarters(vh, b)).then_inc(v_loaded, 16)
            sp.wait_ge(vg_ready, 1)
            for b in range(B):
                for g in range(VG):
                    dst = vg[:, g, b * L:(b + 1) * L].rearrange("h (q t) w -> h q (t w)", q=L // NQ)
                    sp.dma_start(dst, S1[64 * b:64 * b + 64, g * NQ * VW:(g + 1) * NQ * VW]).then_inc(vg_stored, 16)
            sp.wait_ge(kd_ready, 1)
            for b in range(B):
                sp.dma_start(head_quarters(kd, b), Vq[64 * b:64 * b + 64].rearrange("p t e -> p (t e)")).then_inc(stored, 16)
            sp.wait_ge(kt_ready, 1)
            for b in range(B):
                sp.dma_start(head_quarters(kt, b), S1[64 * b:64 * b + 64]).then_inc(stored, 16)
            for hf in range(2):
                sp.wait_ge(tm_ready, hf + 1)
                for b in range(B):
                    dst = tm[:, b * L // C:(b + 1) * L // C].rearrange("h (q n) m -> h q (n m)", q=L // NQ)
                    sp.dma_start(dst[:, :, hf * HB * C * C:(hf + 1) * HB * C * C],
                                 Tm[64 * b:64 * b + 64, hf * HB:(hf + 1) * HB].rearrange("p n i j -> p (n i j)")).then_inc(stored, 16)
            sp.wait_ge(w1_ready, 1)
            for b in range(B):
                sp.dma_start(w1[:, b * L:(b + 1) * L].rearrange("h (q t) -> h q t", q=L // NQ), ksq[64 * b:64 * b + 64]).then_inc(stored, 16)
            sp.wait_ge(vg_stored, 16 * B * VG)
            sp.wait_ge(stored, 16 * B * 5)

        @block.scalar
        def _(act):
            a = nc.scalar
            act.wait_ge(scal_loaded, 32)
            a.activation(s_t[:, 0:1], s_in[:, 0:1], ACT.Exp, scale=-1.0).then_inc(expz, 1)
            act.wait_ge(v_loaded, 32)
            a.activation(S1[:].rearrange("p (g t w) -> p g t w", g=VG, w=VW),
                         Vq[:].rearrange("p t (g w) -> p g t w", g=VG), ACT.Copy).then_inc(vg_ready, 1)
            act.wait_ge(k_loaded[1], 32)
            act.wait_ge(powers, 1)
            act.wait_ge(vg_ready, 1)
            for i in range(C):
                last = a.activation(Vq[:].rearrange("p (n i) e -> p n i e", i=C)[:, :, i], Kb[:, :, i], ACT.Copy, scale=pw[:, i:i + 1])
            last.then_inc(kd_ready, 1)
            for i in range(NQ // SQ):
                if i >= 2:
                    act.wait_ge(sq_used, i - 1)
                a.activation(sq[:, i % 2], Kq[:, i * SQ:(i + 1) * SQ], ACT.Square).then_inc(sq_ready, 1)
            act.wait_ge(vg_stored, 16 * B * VG)
            for i in range(C):
                last = a.activation(S1[:].rearrange("p (n i e) -> p n i e", i=C, e=d)[:, :, i], Kb[:, :, i], ACT.Copy, scale=pwK[:, i:i + 1])
            last.then_inc(kt_ready, 1)

        @block.gpsimd
        def _(pool):
            g_ = nc.gpsimd
            g_.memset(N[:], 0.0).then_inc(pchain, 1)
            g_.memset(cN[:], 0.0).then_inc(pchain, 1)
            g_.memset(Tm[:], 0.0).then_inc(pchain, 1)
            pool.wait_ge(pchain, 3)
            g_.memset(Tm[:].rearrange("p n i j -> p n (i j)")[:, :, 0:C * C:C + 1], 1.0).then_inc(zeroed, 1)
            m = 0
            for hf in range(2):
                pool.wait_ge(k_loaded[hf], 32)
                for i in rows:
                    if m >= 2:
                        pool.wait_ge(prod_used, m - 1)
                    multiply(g_, pairs(prod[:, m % 2], hf, i), hf, i).then_inc(prod_ready, 1)
                    m += 1

        @block.vector
        def _(dve):
            v = nc.vector
            ch = Chain(dve, chain)
            dve.wait_ge(expz, 1)
            ch.link(v.tensor_scalar(s_t[:, 1:2], s_t[:, 0:1], 1.0, None, ALU.add))
            ch.link(v.reciprocal(pw[:, 0:1], s_t[:, 1:2]))
            ch.link(v.tensor_scalar(s_t[:, 2:3], pw[:, 0:1], -1.0, 1.0, ALU.mult, ALU.add))
            ch.link(v.scalar_tensor_tensor(pwK[:, C - 1:C], s_t[:, 2:3], 1.0 / d, s_in[:, 1:2], ALU.mult, ALU.mult))
            for n in range(1, C):
                v.tensor_tensor(pw[:, n:n + 1], pw[:, n - 1:n], pw[:, 0:1], ALU.mult)
                ch.link(v.tensor_tensor(pwK[:, C - 1 - n:C - n], pwK[:, C - n:C - n + 1], pw[:, 0:1], ALU.mult))
            v.tensor_scalar(s_t[:, 3:4], pwK[:, C - 1:C], -1.0, None, ALU.mult).then_inc(powers, 1)
            ch.link(v.tensor_copy(lam_c[:], pw[:, C - 1:C]))
            dve.wait_ge(zeroed, 1)
            for i in range(1, C):
                last = v.tensor_copy(cN[:, i, 0:i], pwK[:, C - 1 - i:C - 1])
            ch.link(last)

            def row_sums(hf, i, src):
                return v.tensor_reduce(N[:, hf * HB:(hf + 1) * HB, i, 0:i], src, AX.X, ALU.add)

            def squares(n):
                for i in range(2 * n, 2 * n + 2):
                    dve.wait_ge(sq_ready, i + 1)
                    v.tensor_reduce(ksq[:, i * SQ:(i + 1) * SQ], sq[:, i % 2], AX.X, ALU.add).then_inc(sq_used, 1)

            for hf in range(2):
                n0 = hf * HB
                nb = slice(n0, n0 + HB)
                dve.wait_ge(k_loaded[hf], 32)
                for i in OWN:
                    ch.link(multiply(v, pairs(own[:], hf, i), hf, i))
                    ch.link(row_sums(hf, i, pairs(own[:], hf, i)))
                for m, i in enumerate(rows, hf * len(rows)):
                    dve.wait_ge(prod_ready, m + 1)
                    row_sums(hf, i, pairs(prod[:, m % 2], hf, i)).then_inc(prod_used, 1)
                    if hf and m < len(rows) + 4:
                        squares(m - len(rows))
                dve.wait_ge(prod_used, (hf + 1) * len(rows))
                ch.link(v.tensor_tensor(N[:, nb], N[:, nb], cN[:].unsqueeze(1).to_broadcast([P, HB, C, C]), ALU.mult))
                for i in range(1, C):
                    t = own[:, 0:HB * i * i].rearrange("p (n j k) -> p n j k", n=HB, j=i)
                    ch.link(v.tensor_tensor(t, N[:, nb, i:i + 1, 0:i].to_broadcast([P, HB, i, i]),
                                            Tm[:, nb, 0:i, 0:i].rearrange("p n k j -> p n j k"), ALU.mult))
                    ins = v.tensor_reduce(Tm[:, nb, i, 0:i], t, AX.X, ALU.add, negate=True)
                    if i < C - 1:
                        ch.link(ins)
                    else:
                        ins.then_inc(tm_ready, 1)
                        dve.wait_ge(tm_ready, hf + 1)
            dve.wait_ge(sq_used, NQ // SQ)
            v.tensor_scalar(ksq[:], ksq[:], s_t[:, 3:4], 1.0, ALU.mult, ALU.add).then_inc(w1_ready, 1)


def phase_c(nc, T, W, kd, kt, tm, vg, vh, w1, ug, yd, xp, qp, vx):
    X, ident, lam_c = T["X"], T["ident"], T["lam_c"]
    with ExitStack() as c:
        sb = lambda n, s, dt=F32: c.enter_context(nc.sbuf_tensor("c_" + n, s, dt))
        ps = lambda n, s: c.enter_context(nc.psum_tensor("c_" + n, s, F32))
        sem = lambda n: c.enter_context(nc.semaphore("c_" + n))
        kdb = sb("kdb", [P, 4, QT, d]); ktb = sb("ktb", [P, 4, QT, d]); tmb = sb("tmb", [P, 4, QBLK, C, C])
        vb = sb("vb", [P, 4, QT, VW]); ub = sb("ub", [P, 4, QT, VW])
        t1 = sb("t1", [P, C, VW, d]); pr = sb("pr", [P, C, VW]); rr = sb("rr", [P, C, VW]); t2 = sb("t2", [P, C, VW, C])
        t3 = sb("t3", [P, VW, d, C]); s3 = sb("s3", [P, VW * d]); S = sb("S", [P, VW * d])
        uR = sb("uR", [P, VG, SR, VW]); vR = sb("vR", [P, SR, d]); w1R = sb("w1R", [P, SR])
        tO = sb("tO", [P, SR, d]); yR = sb("yR", [P, SR, d])
        gam = sb("gam", [P, D]); bet = sb("bet", [P, D]); gbias = sb("gbias", [P, NE]); low = sb("low", [P, NE, NE])
        Y = sb("Y", [P, GT, D]); xn = sb("xn", [P, GT, D]); xnT = sb("xnT", [P, KC, GTOK])
        st = sb("st", [P, GT, 6]); mv = sb("mv", [P, GT, 2])
        ve = [sb(f"ve{i}", [P, GT]) for i in range(3)]; tj = [sb(f"tj{i}", [P, GT], I32) for i in range(3)]
        mneg = [sb(f"mneg{i}", [P, GT]) for i in range(3)]; ti = sb("ti", [P, GT], I32); tt = sb("tt", [P, GT])
        rs = [sb(f"rs{i}", [P, GT]) for i in range(3)]; nm = [sb(f"nm{i}", [P, GT]) for i in range(3)]
        gw = sb("gw", [P, KC, NE]); wg = sb("wg", [P, KC, NE, I_E]); wu = sb("wu", [P, KC, NE, I_E]); wd = sb("wd", [P, NE, D])
        ez = sb("ez", [P, GT, NE]); e1 = sb("e1", [P, GT, NE]); sco = sb("sco", [P, GT, NE]); sfc = sb("sfc", [P, GT, NE])
        gs = sb("gs", [P, GT, NGRP]); gsel = sb("gsel", [P, GT, NGRP]); sel = sb("sel", [P, GT, NE]); tmpc = sb("tmpc", [P, GT, NE])
        ceq = sb("ceq", [P, GT, NE, NE]); cgt = sb("cgt", [P, GT, NE, NE]); rank = sb("rank", [P, GT, NE])
        wsum = sb("wsum", [P, GT]); wt = sb("wt", [P, GT, NE])
        sg = sb("sg", [P, 2, GTOK]); uu = sb("uu", [P, 2, GTOK]); wb = sb("wb", [P, 2, GTOK]); hh = sb("hh", [P, 2, GTOK])
        wv = sb("wv", [P, KC, D]); wa = sb("wa", [P, KC, P]); vbias = sb("vbias", [1, D]); ones = sb("ones", [1, P])
        part = sb("part", [P, 2, 3, KC, GTOK], BF16); rest = sb("rest", [P, 2, KC, GTOK]); qf = sb("qf", [P, KC, GTOK])
        vst = sb("vst", [P, H, GT, 32])
        psT = ps("psT", [P, KC, GTOK]); psGU = ps("psGU", [P, 2, GTOK]); psB = ps("psB", [P, 2, GTOK]); psY = ps("psY", [P, GT, D])

        seg_loaded = [sem(f"seg_loaded{q}") for q in range(4)]
        u_stored = [sem(f"u_stored{q}") for q in range(4)]
        w_loaded = sem("w_loaded"); quarter_done = sem("quarter_done"); chain = sem("chain"); pchain = sem("pchain")
        r_loaded = sem("r_loaded"); y_ready = sem("y_ready"); v_doubled = sem("v_doubled"); y_stored = sem("y_stored"); y_loaded = sem("y_loaded")
        moe_done = sem("moe_done")
        stats1 = sem("stats1"); normed1 = sem("normed1"); x1_done = sem("x1_done")
        stats2 = sem("stats2"); normed2 = sem("normed2"); turned = sem("turned"); turned_kept = sem("turned_kept")
        logits = sem("logits"); exp_done = sem("exp_done"); weights = sem("weights")
        gu_done = sem("gu_done"); gu_kept = sem("gu_kept"); wb_done = sem("wb_done"); wb_kept = sem("wb_kept")
        h_done = sem("h_done"); down_done = sem("down_done")
        stats3 = sem("stats3"); started = [sem(f"started{i}") for i in range(3)]; stats3_seen = sem("stats3_seen"); x2_seen = sem("x2_seen"); normed3 = sem("normed3"); turned3 = sem("turned3"); turned3_kept = sem("turned3_kept")
        q_done = sem("q_done"); v_done = sem("v_done"); v_kept = sem("v_kept"); staged = sem("staged")
        high = sem("high"); rested = sem("rested"); mid = sem("mid"); low_done = sem("low_done"); d_stored = sem("d_stored")
        WLOADS = 16 * 13
        SEG_LOADS = 16 * 4 * B
        D_SHARE = 16 * 7 * B
        block = c.enter_context(nc.Block())
        X4 = X[:].rearrange("p (b t) c -> p b t c", b=B)

        @block.sync
        def _(sp):
            def load_quarter(s, q):
                for b in range(B):
                    t0 = s * SEG + (b * L + q * QT)
                    n0 = s * (SEG // C) + (b * L + q * QT) // C
                    pb = slice(64 * b, 64 * b + 64)
                    for buf, src in ((kdb, kd), (ktb, kt)):
                        sp.dma_start(buf[pb, q].rearrange("p t e -> p (t e)"),
                                     src[:, bass.ds(t0, QT)].rearrange("h t e -> h (t e)").unsqueeze(1).to_broadcast([H, VG, QT * d])
                                     ).then_inc(seg_loaded[q], 16)
                    sp.dma_start(tmb[pb, q].rearrange("p n i j -> p (n i j)"),
                                 tm[:, bass.ds(n0, QBLK)].rearrange("h n m -> h (n m)").unsqueeze(1).to_broadcast([H, VG, QBLK * C * C])
                                 ).then_inc(seg_loaded[q], 16)
                    sp.dma_start(vb[pb, q].rearrange("p t w -> p (t w)"),
                                 vg[:, :, bass.ds(t0, QT)].rearrange("h g t w -> h g (t w)")).then_inc(seg_loaded[q], 16)

            def store_u(s, q):
                for b in range(B):
                    t0 = s * SEG + (b * L + q * QT)
                    sp.dma_start(ug[:, :, bass.ds(t0, QT)].rearrange("h g t w -> h g (t w)"),
                                 ub[64 * b:64 * b + 64, q].rearrange("p t w -> p (t w)")).then_inc(u_stored[q], 16)

            def output_rows(u):
                for q in range(4):
                    sp.wait_ge(u_stored[q], u * (16 * B) + 16 * B)
                sp.wait_ge(moe_done, u + 1)
                for b in range(B):
                    t0 = u * SEG + b * L
                    pb = slice(64 * b, 64 * b + 64)
                    for g in range(VG):
                        sp.dma_start(uR[pb, g].rearrange("p t w -> p (t w)"),
                                     ug[:, g, bass.ds(t0, SEG)].rearrange("h (r t) w -> h r (t w)", r=4)).then_inc(r_loaded, 16)
                    sp.dma_start(vR[pb].rearrange("p t e -> p (t e)"),
                                 vh[:, bass.ds(t0, SEG)].rearrange("h (r t) e -> h r (t e)", r=4)).then_inc(r_loaded, 16)
                    sp.dma_start(w1R[pb],
                                 w1[:, bass.ds(t0, SEG)].rearrange("h (r t) -> h r t", r=4)).then_inc(r_loaded, 16)
                sp.wait_ge(y_ready, u + 1)
                for b in range(B):
                    for r in range(4):
                        t0 = u * SEG + (b * L + r * SR)
                        sp.dma_start(yd[bass.ds(t0, SR)].rearrange("t (h e) -> h t e", h=H),
                                     yR[64 * b + r:64 * b + 64:4]).then_inc(y_stored, 16)
                sp.wait_ge(y_stored, u * (64 * B) + 64 * B)
                for b in range(B):
                    sp.dma_start(Y[:, 2 * b:2 * b + 2],
                                 yd[bass.ds(u * SEG + b * L, SEG)].rearrange("(j p) c -> p j c", p=P)).then_inc(y_loaded, 16)

            def store_operands(u):
                sp.wait_ge(v_kept, u + 1)
                sp.wait_ge(low_done, u + 1)
                for b in range(B):
                    for a, dst in enumerate((xp, qp)):
                        for m in range(3):
                            sp.dma_start(dst[m, b].rearrange("(k p) t -> p k t", p=P)[:, :, bass.ds(u * SEG, SEG)],
                                         part[:, a, m, :, b * SEG:(b + 1) * SEG]).then_inc(d_stored, 16)
                    sp.dma_start(vx[b * H:(b + 1) * H, :, bass.ds(u * (GT // B), GT // B)].rearrange("h p k e -> p h (k e)"),
                                 vst[:, :, b * (GT // B):(b + 1) * (GT // B)].rearrange("p h k e -> p h (k e)")).then_inc(d_stored, 16)

            def after_segment(s):
                for q in range(4):
                    sp.wait_ge(quarter_done, s * 4 + (q - 3))
                    store_u(s - 1, q)
                    load_quarter(s, q)
                output_rows(s - 1)

            for q in range(4):
                load_quarter(0, q)
            for dst, src in ((gam, W["gamma"]), (bet, W["beta"]), (gbias, W["bias"])):
                sp.dma_start(dst[:], src.to_broadcast([P, src.shape[1]])).then_inc(w_loaded, 16)
            sp.dma_start(low[:].rearrange("p i j -> p (i j)"), W["low"].to_broadcast([P, NE * NE])).then_inc(w_loaded, 16)
            sp.dma_start(gw[:], W["gwT"].rearrange("(k p) e -> p k e", p=P)).then_inc(w_loaded, 16)
            for k in range(KC):
                sp.dma_start(wg[:, k], W["wgT"][k * P:(k + 1) * P]).then_inc(w_loaded, 16)
                sp.dma_start(wu[:, k], W["wuT"][k * P:(k + 1) * P]).then_inc(w_loaded, 16)
            sp.dma_start(wd[:], W["wdT"]).then_inc(w_loaded, 16)
            sp.dma_start(wv[:], W["wvT"].rearrange("(k p) n -> p k n", p=P)).then_inc(w_loaded, 16)
            sp.dma_start(wa[:], W["wa"].rearrange("(k p) n -> p k n", p=P)).then_inc(w_loaded, 16)
            sp.dma_start(vbias[:], W["wv_b"]).then_inc(w_loaded, 16)
            after_segment(1)
            with sp.Fori(2, NSEG) as s:
                after_segment(s)
                store_operands(s - 2)
            for q in range(4):
                sp.wait_ge(quarter_done, NSEG * 4 - 3 + q)
                store_u(NSEG - 1, q)
            output_rows(NSEG - 1)
            store_operands(NSEG - 2)
            store_operands(NSEG - 1)
            sp.wait_ge(d_stored, NSEG * D_SHARE + D_SHARE)

        @block.vector
        def _(dve):
            v = nc.vector
            ch = Chain(dve, chain)
            S3 = S[:].rearrange("p (w k) -> p w k", w=VW)
            s33 = s3[:].rearrange("p (w k) -> p w k", w=VW)

            behind = [0, 0]

            def halves(op):
                for h in range(2):
                    if behind[h]:
                        dve.wait_ge(chain, behind[h])
                    op(slice(h * VW // 2, (h + 1) * VW // 2)).then_inc(chain, 1)
                    ch.n += 1
                    behind[h] = ch.n

            def block_step(s, q, i):
                t = slice(C * i, C * i + C)
                u = ub[:, q, t]
                HW = VW // 2
                halves(lambda w: v.tensor_tensor(t1[:, :, w], kdb[:, q, t].unsqueeze(2).to_broadcast([P, C, HW, d]),
                                                 S3[:, w].unsqueeze(1).to_broadcast([P, C, HW, d]), ALU.mult))
                halves(lambda w: v.tensor_reduce(pr[:, :, w], t1[:, :, w], AX.X, ALU.add))
                halves(lambda w: v.tensor_tensor(rr[:, :, w], vb[:, q, t, w], pr[:, :, w], ALU.subtract))
                halves(lambda w: v.tensor_tensor(t2[:, :, w], tmb[:, q, i].unsqueeze(2).to_broadcast([P, C, HW, C]),
                                                 rr[:, :, w].rearrange("p j w -> p w j").unsqueeze(1).to_broadcast([P, C, HW, C]), ALU.mult))
                halves(lambda w: v.tensor_reduce(u[:, :, w], t2[:, :, w], AX.X, ALU.add))
                halves(lambda w: v.tensor_tensor(t3[:, w], ktb[:, q, t].rearrange("p i k -> p k i").unsqueeze(1).to_broadcast([P, HW, d, C]),
                                                 u[:, :, w].rearrange("p i w -> p w i").unsqueeze(2).to_broadcast([P, HW, d, C]), ALU.mult))
                halves(lambda w: v.tensor_reduce(s33[:, w], t3[:, w], AX.X, ALU.add))
                halves(lambda w: v.scalar_tensor_tensor(S3[:, w], S3[:, w], lam_c[:], s33[:, w], ALU.mult, ALU.add))
                if i == QBLK - 1:
                    dve.wait_ge(chain, ch.n)
                    dve.sem_inc(quarter_done, 1)
                    behind[:] = [0, 0]

            def stats(src, i):
                for j in range(GT):
                    last = v.bn_stats(st[:, j], src(j))
                ch.link(last)
                for j in range(GT):
                    last = v.bn_aggr(mv[:, j], st[:, j])
                ch.link(last)
                ch.link(v.tensor_scalar(ve[i][:], mv[:, :, 1], EPS, None, ALU.add))
                v.tensor_scalar(mneg[i][:], mv[:, :, 0], -1.0, None, ALU.mult)
                ch.link(v.tensor_scalar(ti[:], ve[i][:].bitcast(I32), 1, None, ALU.arith_shift_right))
                v.tensor_scalar(tj[i][:], ti[:], -1.0, MAGIC, ALU.mult, ALU.add).then_inc(started[i], 1)

            def ranks(x, n, out):
                eq, gt = ceq[:, :, 0:n, 0:n], cgt[:, :, 0:n, 0:n]
                xj = x.unsqueeze(2).to_broadcast([P, GT, n, n])
                xi = x.unsqueeze(3).to_broadcast([P, GT, n, n])
                ch.link(v.tensor_tensor(eq, xj, xi, ALU.is_equal))
                ch.link(v.tensor_tensor(eq, eq, low[:, 0:n, 0:n].unsqueeze(1).to_broadcast([P, GT, n, n]), ALU.mult))
                ch.link(v.tensor_tensor(gt, xj, xi, ALU.is_gt))
                ch.link(v.tensor_tensor(gt, gt, eq, ALU.add))
                ch.link(v.tensor_reduce(rank[:, :, 0:n], gt, AX.X, ALU.add))
                ch.link(v.tensor_scalar(out, rank[:, :, 0:n], 1.5, None, ALU.is_lt))

            def gate():
                ch.link(v.tensor_scalar(e1[:], ez[:], 1.0, None, ALU.add))
                ch.link(v.reciprocal(sco[:], e1[:]))
                ch.link(v.tensor_tensor(sfc[:], sco[:], gbias[:].unsqueeze(1).to_broadcast([P, GT, NE]), ALU.add))
                ch.link(v.tensor_tensor(gs[:], sfc[:, :, 0::2], sfc[:, :, 1::2], ALU.add))
                ranks(gs[:], NGRP, gsel[:])
                ch.link(v.tensor_tensor(tmpc[:].rearrange("p t (g m) -> p t g m", m=2), sfc[:].rearrange("p t (g m) -> p t g m", m=2),
                                        gsel[:].unsqueeze(3).to_broadcast([P, GT, NGRP, 2]), ALU.mult))
                ranks(tmpc[:], NE, sel[:])
                ch.link(v.tensor_tensor(sel[:], sel[:], sco[:], ALU.mult))
                ch.link(v.tensor_reduce(wsum[:], sel[:], AX.X, ALU.add))
                ch.link(v.tensor_scalar(wsum[:], wsum[:], 1e-20, None, ALU.add))
                ch.link(v.reciprocal(wsum[:], wsum[:]))
                v.tensor_tensor(wt[:], sel[:], wsum[:].unsqueeze(2).to_broadcast([P, GT, NE]), ALU.mult).then_inc(weights, 1)

            def slot(u, n):
                if n == 0:
                    dve.wait_ge(y_loaded, u * (16 * B) + 16 * B)
                    stats(lambda j: Y[:, j], 0)
                if n == 1:
                    dve.wait_ge(x1_done, u + 1)
                    stats(lambda j: X4[:, j // 2, bass.ds(2 * u + j % 2, 1)].rearrange("p a c -> p (a c)"), 1)
                if n == 2:
                    dve.wait_ge(exp_done, u + 1)
                    gate()
                if n == 3:
                    dve.wait_ge(down_done, u * NE + NE)
                    xs = X4[:, :, bass.ds(2 * u, 2)]
                    v.tensor_tensor(xs, xs, psY[:].rearrange("p (b t) c -> p b t c", b=B), ALU.add).then_inc(moe_done, 1)
                    dve.wait_ge(moe_done, u + 2)
                    dve.sem_inc(x2_seen, 1)
                    stats(lambda j: X4[:, j // 2, bass.ds(2 * u + j % 2, 1)].rearrange("p a c -> p (a c)"), 2)

            def segment(s, slots):
                for q in range(4):
                    dve.wait_ge(seg_loaded[q], s * SEG_LOADS + SEG_LOADS)
                    if slots:
                        dve.wait_ge(u_stored[q], s * (16 * B))
                    for i in range(QBLK):
                        block_step(s, q, i)
                        n = q * QBLK + i
                        if slots and n in SLOTS:
                            slot(s - 1, SLOTS.index(n))

            SLOTS = [7, 12, 17, 30]
            ch.link(v.memset(ones[:], 1.0))
            dve.sem_inc(moe_done, 1)
            ch.link(v.memset(S[:], 0.0))
            segment(0, False)
            with dve.Fori(1, NSEG) as s:
                dve.wait_ge(w_loaded, WLOADS)
                ch.clear()
                segment(s, True)
            dve.wait_ge(w_loaded, WLOADS)
            ch.clear()
            for n in range(4):
                slot(NSEG - 1, n)

        def loops(eng, body):
            with eng.Fori(0, NSEG) as u:
                body(u)

        @block.gpsimd
        def _(pool):
            g_ = nc.gpsimd
            ch = Chain(pool, pchain)
            ch.link(g_.memset(vst[:], 0.0))
            g_.memset(vst[:, :, :, d:d + 1], 1.0).then_inc(staged, 1)
            ch.clear()
            pool.wait_ge(w_loaded, WLOADS)

            def steps(u, i, signal):
                pool.wait_ge(started[i], u + 1)
                r = tj[i][:].bitcast(F32)
                for _ in range(3):
                    ch.link(g_.tensor_tensor(tt[:], r, r, ALU.mult))
                    ch.link(g_.tensor_tensor(tt[:], tt[:], ve[i][:], ALU.mult))
                    ch.link(g_.tensor_scalar(tt[:], tt[:], -0.5, 1.5, ALU.mult, ALU.add))
                    ch.link(g_.tensor_tensor(rs[i][:], tt[:], r, ALU.mult))
                    r = rs[i][:]
                g_.tensor_tensor(nm[i][:], mneg[i][:], rs[i][:], ALU.mult).then_inc(signal, 1)

            def operands(u):
                for i, whole in enumerate((xnT, qf)):
                    pool.wait_ge(high, u * 2 + (i + 1))
                    g_.tensor_tensor(rest[:, i], whole[:], part[:, i, 0], ALU.subtract).then_inc(rested, 1)
                for i in range(2):
                    pool.wait_ge(mid, u * 2 + (i + 1))
                    last = g_.tensor_tensor(part[:, i, 2], rest[:, i], part[:, i, 1], ALU.subtract)
                last.then_inc(low_done, 1)

            def group(u):
                pool.wait_ge(r_loaded, u * (16 * 12) + 16 * 12)
                ch.link(g_.tensor_tensor(tO[:].rearrange("p t (g w) -> p g t w", g=VG), uR[:],
                                         w1R[:].unsqueeze(1).unsqueeze(3).to_broadcast([P, VG, SR, VW]), ALU.mult))
                pool.wait_ge(v_doubled, u + 1)
                g_.tensor_tensor(yR[:], vR[:], tO[:], ALU.subtract).then_inc(y_ready, 1)
                xs = X4[:, :, bass.ds(2 * u, 2)]
                ch.link(g_.tensor_tensor(xs, xs, bet[:].unsqueeze(1).unsqueeze(1).to_broadcast([P, B, GT // B, D]), ALU.add))
                steps(u, 0, stats1)
                pool.wait_ge(normed1, u + 1)
                ch.link(g_.tensor_tensor(Y[:], Y[:], gam[:].unsqueeze(1).to_broadcast([P, GT, D]), ALU.mult))
                g_.tensor_tensor(xs, xs, Y[:].rearrange("p (b t) c -> p b t c", b=B), ALU.add).then_inc(x1_done, 1)
                steps(u, 1, stats2)
                for e in range(NE):
                    pool.wait_ge(wb_kept, u * NE + (e + 1))
                    ch.link(g_.tensor_tensor(sg[:, e % 2], sg[:, e % 2], wb[:, e % 2], ALU.mult))
                    if e >= 2:
                        pool.wait_ge(down_done, u * NE + (e - 1))
                    g_.tensor_tensor(hh[:, e % 2], sg[:, e % 2], uu[:, e % 2], ALU.mult).then_inc(h_done, 1)
                steps(u, 2, stats3)
                operands(u)
                ch.clear()

            loops(pool, group)

        @block.scalar
        def _(act):
            a = nc.scalar
            act.sem_inc(d_stored, D_SHARE)
            act.wait_ge(staged, 1)

            def operands(u):
                act.wait_ge(stats3, u + 1)
                act.sem_inc(stats3_seen, 1)
                for j in range(GT):
                    xj = X4[:, j // 2, bass.ds(2 * u + j % 2, 1)].rearrange("p a c -> p (a c)")
                    last = a.activation(xn[:, j], xj, ACT.Identity, bias=nm[2][:, j:j + 1], scale=rs[2][:, j:j + 1])
                last.then_inc(normed3, 1)
                act.wait_ge(turned3, u + 1)
                a.activation(xnT[:], psT[:], ACT.Copy).then_inc(turned3_kept, 1)
                act.wait_ge(d_stored, u * D_SHARE + D_SHARE)
                a.activation(part[:, 0, 0], psT[:], ACT.Copy).then_inc(high, 1)
                act.wait_ge(q_done, u + 1)
                a.activation(qf[:], psGU[:], ACT.Copy)
                a.activation(part[:, 1, 0], psGU[:], ACT.Copy).then_inc(high, 1)
                for i in range(2):
                    act.wait_ge(rested, u * 2 + (i + 1))
                    a.activation(part[:, i, 1], rest[:, i], ACT.Copy).then_inc(mid, 1)
                act.wait_ge(v_done, u + 1)
                a.activation(vst[:, :, :, 0:d].rearrange("p h t e -> p t h e"),
                             psB[:].rearrange("p a (j h e) -> p (a j) h e", h=H, e=d), ACT.Copy).then_inc(v_kept, 1)

            def group(u):
                act.wait_ge(r_loaded, u * (16 * 12) + 16 * 12)
                a.activation(vR[:], vR[:], ACT.Copy, scale=2.0).then_inc(v_doubled, 1)
                act.wait_ge(stats1, u + 1)
                for j in range(GT):
                    last = a.activation(Y[:, j], Y[:, j], ACT.Identity, bias=nm[0][:, j:j + 1], scale=rs[0][:, j:j + 1])
                last.then_inc(normed1, 1)
                act.wait_ge(stats2, u + 1)
                for j in range(GT):
                    xj = X4[:, j // 2, bass.ds(2 * u + j % 2, 1)].rearrange("p a c -> p (a c)")
                    last = a.activation(xn[:, j], xj, ACT.Identity, bias=nm[1][:, j:j + 1], scale=rs[1][:, j:j + 1])
                last.then_inc(normed2, 1)
                act.wait_ge(turned, u + 1)
                a.activation(xnT[:], psT[:], ACT.Copy).then_inc(turned_kept, 1)
                act.wait_ge(logits, u + 1)
                a.activation(ez[:], psT[:, 0, 0:GT * NE].rearrange("p (t e) -> p t e", e=NE), ACT.Exp, scale=-1.0).then_inc(exp_done, 1)
                for e in range(NE):
                    act.wait_ge(gu_done, u * NE + (e + 1))
                    if e >= 2:
                        act.wait_ge(h_done, u * NE + (e - 1))
                    a.activation(sg[:, e % 2], psGU[:, 0], ACT.Silu)
                    a.activation(uu[:, e % 2], psGU[:, 1], ACT.Copy).then_inc(gu_kept, 1)
                    act.wait_ge(wb_done, u * NE + (e + 1))
                    a.activation(wb[:, e % 2], psB[:, e % 2], ACT.Copy).then_inc(wb_kept, 1)
                operands(u)

            loops(act, group)

        @block.tensor
        def _(pe):
            t = nc.tensor
            pe.wait_ge(w_loaded, WLOADS)
            psV = psB[:].rearrange("p a (j c) -> p (a j) c", c=D)

            def operands(u):
                pe.wait_ge(normed3, u + 1)
                for k in range(KC):
                    for j in range(GT):
                        last = t.transpose(psT[:, k, j * P:(j + 1) * P], xn[:, j, k * P:(k + 1) * P], ident[:])
                last.then_inc(turned3, 1)
                pe.wait_ge(turned3_kept, u + 1)
                for k in range(KC):
                    last = t.matmul(psGU[:, k], wa[:, k], xnT[:, k], start=True, stop=True)
                last.then_inc(q_done, 1)
                for j in range(GT):
                    for k in range(KC):
                        t.matmul(psV[:, j], xnT[:, k, j * P:(j + 1) * P], wv[:, k], start=(k == 0), stop=False)
                    last = t.matmul(psV[:, j], ones[:], vbias[:], start=False, stop=True)
                last.then_inc(v_done, 1)

            def group(u):
                pe.wait_ge(normed2, u + 1)
                pe.wait_ge(moe_done, u + 1)
                for k in range(KC):
                    for j in range(GT):
                        last = t.transpose(psT[:, k, j * P:(j + 1) * P], xn[:, j, k * P:(k + 1) * P], ident[:])
                last.then_inc(turned, 1)
                pe.wait_ge(turned_kept, u + 1)
                for j in range(GT):
                    for k in range(KC):
                        last = t.matmul(psT[:, 0, j * NE:(j + 1) * NE], xnT[:, k, j * P:(j + 1) * P], gw[:, k],
                                        start=(k == 0), stop=(k == KC - 1))
                last.then_inc(logits, 1)

                def gate_up(e):
                    if e >= 1:
                        pe.wait_ge(gu_kept, u * NE + e)
                    for i, w in enumerate((wg, wu)):
                        for k in range(KC):
                            last = t.matmul(psGU[:, i], w[:, k, e], xnT[:, k], start=(k == 0), stop=(k == KC - 1))
                    last.then_inc(gu_done, 1)

                def spread(e):
                    if e == 0:
                        pe.wait_ge(weights, u + 1)
                    if e >= 2:
                        pe.wait_ge(wb_kept, u * NE + (e - 1))
                    for j in range(GT):
                        last = t.matmul(psB[:, e % 2, j * P:(j + 1) * P], wt[:, j, e:e + 1].to_broadcast([P, P]), ident[:],
                                        start=True, stop=True)
                    last.then_inc(wb_done, 1)

                def down(e):
                    pe.wait_ge(h_done, u * NE + (e + 1))
                    for j in range(GT):
                        last = t.matmul(psY[:, j], hh[:, e % 2, j * P:(j + 1) * P], wd[:, e],
                                        start=(e == 0 and j % 2 == 0), stop=(e == NE - 1), skip_group_check=True)
                    last.then_inc(down_done, 1)

                for e in range(NE):
                    gate_up(e)
                    spread(e)
                    if e >= 1:
                        down(e - 1)
                down(NE - 1)
                operands(u)

            loops(pe, group)


NH = B * H
KR = 6 * d
SPLIT_Q = (0, 0, 0, 1, 1, 2)
SPLIT_X = (0, 1, 2, 0, 1, 0)
RING = 4
KT = L // P
QC = 512
NQC = L // QC
MB = 3
LEAD = 8


def phase_e(nc, T, W, xp, qp, vx):
    ident, O2 = T["ident"], T["O2"]
    with ExitStack() as c:
        sb = lambda n, s, dt=F32: c.enter_context(nc.sbuf_tensor("e_" + n, s, dt))
        ps = lambda n, s: c.enter_context(nc.psum_tensor("e_" + n, s, F32))
        sem = lambda n: c.enter_context(nc.semaphore("e_" + n))
        wi = sb("wi", [P, 3, KC * HID], I32)
        XS = [sb(f"XS{i}", [P, L], BF16) for i in range(RING)]
        QS = [sb(f"QS{i}", [P, L], BF16) for i in range(RING)]
        Vh = [sb(f"Vh{i}", [P, KT, 32]) for i in range(2)]
        Pt = [sb(f"Pt{i}", [P, L]) for i in range(2)]
        oT = [sb(f"oT{i}", [P, QC]) for i in range(2)]
        mx = [sb(f"mx{i}", [P, KT, NQC]) for i in range(2)]
        one = sb("one", [P, KT]); mneg = sb("mneg", [P, KT]); mr = sb("mr", [P, KT]); M3 = sb("M3", [P, 3, 32], BF16)
        MT = [sb(f"MT{i}", [P, 3, 32], BF16) for i in range(2)]
        rden = sb("rden", [P, NQC, NQC])
        psS = [ps(f"psS{i}", [P, 2, QC]) for i in range(2)]
        psM = [ps(f"psM{i}", [P, QC]) for i in range(MB)]
        psO = ps("psO", [P, QC])
        stacks = sem("stacks"); v_loaded = sem("v_loaded"); ones = sem("ones")
        max_ready = sem("max_ready"); max_used = sem("max_used"); m_ready = sem("m_ready"); m_loaded = sem("m_loaded")
        wi_loaded = sem("wi_loaded"); m_whole = sem("m_whole"); m_split = sem("m_split"); pchain = sem("pchain")
        scores = sem("scores"); exp_done = sem("exp_done"); av_done = sem("av_done")
        o_kept = sem("o_kept"); o_turned = sem("o_turned"); normed = sem("normed"); chain = sem("chain")
        block = c.enter_context(nc.Block())
        SHARE = 16 * 12
        MT_OF = KT * NQC
        TURN_KT = 1
        TURN_AT = (TURN_KT + LEAD + 1) * NQC

        def place(c):
            return c if c < TURN_AT else c + 1

        def heads(body):
            def run(eng):
                body(0, 0)
                with eng.Fori(0, NH // RING - 1) as i:
                    for k in range(RING):
                        body(i * RING + (1 + k), (1 + k) % RING)
                for n in range(NH - RING + 1, NH):
                    body(n, n % RING)
            return run

        def is_there(n):
            return not isinstance(n, int) or 0 <= n < NH

        @block.sync
        def _(sp):
            def load_stacks(n, r):
                for row, (mq, mk) in enumerate(zip(SPLIT_Q, SPLIT_X)):
                    rows = slice(row * d, row * d + d)
                    sp.dma_start(QS[r % RING][rows], qp[mq].rearrange("b c t -> (b c) t")[bass.ds(n * d, d)]).then_inc(stacks, 16)
                    sp.dma_start(XS[r % RING][rows], xp[mk].rearrange("b c t -> (b c) t")[bass.ds(n * d, d)]).then_inc(stacks, 16)

            def load_values(n, r):
                sp.dma_start(Vh[r % 2][:].rearrange("p k e -> p (k e)"),
                             vx[bass.ds(n, 1)].rearrange("n p k e -> (n p) (k e)")).then_inc(v_loaded, 16)

            def load_max(n, r):
                sp.wait_ge(ones, 1)
                sp.wait_ge(m_ready, n + 1)
                for m in range(3):
                    for q4 in range(4):
                        dst = QS[r % RING][KR + m:KR + m + 1].rearrange("p (t q c) -> p q t c", q=4, c=32)[:, q4]
                        sp.dma_start(dst, MT[r % 2][32 * q4:32 * q4 + KT, m]).then_inc(m_loaded, 16)

            load_stacks(0, 0)
            sp.wait_ge(stacks, SHARE)
            load_stacks(1, 1)
            load_values(0, 0)
            load_max(0, 0)
            for i, (src, k) in enumerate(((W["fgT"], KC), (W["fuT"], KC), (W["fdT"], HC))):
                sp.dma_start(wi[:, i].rearrange("p (k n) -> p k n", k=k), src.rearrange("(k p) n -> p k n", p=P)).then_inc(wi_loaded, 16)

            def head(n, r):
                if not isinstance(n, int) or n > 0:
                    sp.wait_ge(av_done, n * KT)
                if is_there(n + 2):
                    sp.wait_ge(stacks, n * SHARE + 2 * SHARE)
                    load_stacks(n + 2, r + 2)
                if is_there(n + 1):
                    sp.wait_ge(v_loaded, n * 16 + 16)
                    load_values(n + 1, r + 1)
                    load_max(n + 1, r + 1)

            heads(head)(sp)

        @block.vector
        def _(dve):
            v = nc.vector
            ch = Chain(dve, chain)
            v.memset(M3[:], 0.0)
            v.memset(one[:], 1.0)
            for i in range(RING):
                v.memset(QS[i][KR:P], 0.0)
                last = v.memset(XS[i][KR:P], 0.0)
            ch.link(last)
            for i in range(RING):
                last = v.memset(XS[i][KR:KR + 3], 1.0)
            last.then_inc(ones, 1)

            def tile_max(n, r, t):
                for q in range(NQC):
                    dve.wait_ge(max_ready, n * MT_OF + (t * NQC + q + 1))
                    v.reduce_max(mx[r % 2][:, t, q:q + 1], psM[place(t * NQC + q) % MB][:], AX.X).then_inc(max_used, 1)
                if t == KT - 1:
                    dve.wait_ge(max_used, n * MT_OF + MT_OF)
                    if is_there(n - 1):
                        dve.wait_ge(m_split, n)
                    v.tensor_reduce(mneg[:], mx[r % 2][:], AX.X, ALU.max, negate=True).then_inc(m_whole, 1)

            def turn_max(n, r):
                dve.wait_ge(m_split, n + 1)
                if not isinstance(n, int) or n >= 2:
                    dve.wait_ge(m_loaded, n * SHARE - SHARE)
                v.transpose(MT[r % 2][:].rearrange("p m c -> p (m c)"), M3[:].rearrange("p m c -> p (m c)")).then_inc(m_ready, 1)

            def norm(n):
                dve.wait_ge(o_turned, n + 1)
                x = psM[TURN_AT % MB][:].rearrange("p (c j e) -> p j c e", c=NQC, e=32)
                ch.link(v.reciprocal(rden[:], x[:, :, :, d]))
                o = O2[:, bass.ds(n, 1)].rearrange("p a (j c) e -> p (a j) c e", j=NQC)
                v.tensor_tensor(o, x[:, :, :, 0:d], rden[:].unsqueeze(3).to_broadcast([P, NQC, NQC, d]), ALU.mult).then_inc(normed, 1)
                dve.wait_ge(normed, n + 1)

            for t in range(KT):
                tile_max(0, 0, t)
            for t in range(LEAD):
                tile_max(1, 1, t)
                if t == 0:
                    turn_max(0, 0)
            ch.clear()

            def head(n, r):
                for kt in range(KT):
                    ahead, t = 1 + (kt + LEAD) // KT, (kt + LEAD) % KT
                    if is_there(n + ahead):
                        tile_max(n + ahead, r + ahead, t)
                    if t == 0 and is_there(n + 1):
                        turn_max(n + 1, r + 1)
                    if kt == TURN_KT and is_there(n - 1):
                        norm(n - 1)
                ch.clear()

            heads(head)(dve)
            norm(NH - 1)

        @block.gpsimd
        def _(pool):
            g_ = nc.gpsimd
            ch = Chain(pool, pchain)
            pool.wait_ge(ones, 1)

            def convert_weights():
                pool.wait_ge(wi_loaded, 48)
                for i, w in enumerate((T["wg"], T["wu"], T["wd"])):
                    g_.tensor_copy(w[:].rearrange("p k n -> p (k n)"), wi[:, i])

            def head(n, r):
                pool.wait_ge(m_whole, n + 1)
                if is_there(n - 1):
                    pool.wait_ge(m_ready, n)
                ch.link(g_.tensor_tensor(M3[:, 0, 0:KT], mneg[:], one[:], ALU.mult))
                ch.link(g_.tensor_tensor(mr[:], mneg[:], M3[:, 0, 0:KT], ALU.subtract))
                ch.link(g_.tensor_tensor(M3[:, 1, 0:KT], mr[:], one[:], ALU.mult))
                g_.tensor_tensor(M3[:, 2, 0:KT], mr[:], M3[:, 1, 0:KT], ALU.subtract).then_inc(m_split, 1)
                ch.clear()
                if isinstance(n, int) and n == 0:
                    convert_weights()

            heads(head)(pool)

        @block.scalar
        def _(act):
            a = nc.scalar

            def keep_output(n, r):
                act.wait_ge(av_done, n * KT + KT)
                a.activation(oT[r % 2][:], psO[:], ACT.Copy).then_inc(o_kept, 1)

            def head(n, r):
                for kt in range(KT):
                    if not isinstance(n, int) or n * KT + kt >= 2:
                        act.wait_ge(av_done, n * KT + (kt - 1))
                    for half in range(2):
                        act.wait_ge(scores, n * (2 * KT) + (2 * kt + half + 1))
                        a.activation(Pt[kt % 2][:, half * 2 * QC:(half + 1) * 2 * QC], psS[half][:].rearrange("p a c -> p (a c)"),
                                     ACT.Exp, scale=float(d) ** -0.5).then_inc(exp_done, 1)
                    if kt == 0 and is_there(n - 1):
                        keep_output(n - 1, r + 1)

            heads(head)(act)
            keep_output(NH - 1, NH - 1)

        @block.tensor
        def _(pe):
            t_ = nc.tensor

            def for_max(n, r, t, q):
                if t == 0 and q == 0:
                    pe.wait_ge(stacks, n * SHARE + SHARE)
                at = place(t * NQC + q)
                if at - MB == TURN_AT:
                    if not isinstance(n, int) or n >= 2:
                        pe.wait_ge(normed, n - 1)
                elif at >= MB:
                    pe.wait_ge(max_used, n * MT_OF + (at - MB if at - MB < TURN_AT else at - MB - 1) + 1)
                elif is_there(n - 1):
                    past = [p for p in range(MT_OF + 1) if p % MB == at][-1]
                    pe.wait_ge(max_used, n * MT_OF + (past - MT_OF))
                t_.matmul(psM[at % MB][:], QS[r % RING][0:KR, t * P:(t + 1) * P], XS[r % RING][0:KR, q * QC:(q + 1) * QC],
                          start=True, stop=True).then_inc(max_ready, 1)

            def for_exp(n, r, kt, half, wait):
                if wait is not None:
                    pe.wait_ge(exp_done, wait)
                for q in range(2):
                    q0 = (half * 2 + q) * QC
                    last = t_.matmul(psS[half][:, q], XS[r % RING][:, kt * P:(kt + 1) * P], QS[r % RING][:, q0:q0 + QC],
                                     start=True, stop=True)
                last.then_inc(scores, 1)

            def times_values(n, r, kt):
                if kt == 0:
                    pe.wait_ge(v_loaded, n * 16 + 16)
                    if is_there(n - 1):
                        pe.wait_ge(o_kept, n)
                for j in range(NQC):
                    last = t_.matmul(psO[32 * j:32 * j + 32], Vh[r % 2][:, kt], Pt[kt % 2][:, j * QC:(j + 1) * QC],
                                     start=(kt == 0), stop=(kt == KT - 1))
                last.then_inc(av_done, 1)

            def turn_output(n, r):
                pe.wait_ge(o_kept, n + 1)
                if isinstance(n, int) and n >= NH - 2:
                    pe.wait_ge(max_used, NH * MT_OF)
                else:
                    pe.wait_ge(max_used, n * MT_OF + (2 * MT_OF + TURN_AT - MB + 1))
                for cc in range(NQC):
                    last = t_.transpose(psM[TURN_AT % MB][:, cc * P:(cc + 1) * P], oT[r % 2][:, cc * P:(cc + 1) * P], ident[:])
                last.then_inc(o_turned, 1)

            for t in range(KT):
                for q in range(NQC):
                    for_max(0, 0, t, q)
            for t in range(LEAD):
                for q in range(NQC):
                    for_max(1, 1, t, q)
            pe.wait_ge(ones, 1)
            pe.wait_ge(m_loaded, SHARE)
            for half in range(2):
                for_exp(0, 0, 0, half, None)

            def head(n, r):
                for kt in range(KT):
                    k = n * (2 * KT) + 2 * kt
                    ahead, t = 1 + (kt + LEAD) // KT, (kt + LEAD) % KT
                    nn, nr, nk = (n, r, kt + 1) if kt < KT - 1 else (n + 1, r + 1, 0)
                    if kt == KT - 1 and is_there(nn):
                        pe.wait_ge(m_loaded, n * SHARE + 2 * SHARE)
                    for half in range(2):
                        if is_there(nn):
                            for_exp(nn, nr, nk, half, k + (half + 1))
                        if is_there(n + ahead):
                            for_max(n + ahead, r + ahead, t, half)
                    if is_there(n + ahead):
                        for_max(n + ahead, r + ahead, t, 2)
                    if not is_there(nn):
                        pe.wait_ge(exp_done, k + 2)
                    times_values(n, r, kt)
                    if is_there(n + ahead):
                        for_max(n + ahead, r + ahead, t, 3)
                    if kt == TURN_KT and is_there(n - 1):
                        turn_output(n - 1, r + 1)

            heads(head)(pe)
            pe.wait_ge(normed, NH - 1)
            turn_output(NH - 1, NH - 1)


def phase_f(nc, T, W, out):
    X, ident, O2, wg, wu, wd = T["X"], T["ident"], T["O2"], T["wg"], T["wu"], T["wd"]
    with ExitStack() as c:
        sb = lambda n, s, dt=F32: c.enter_context(nc.sbuf_tensor("f_" + n, s, dt))
        ps = lambda n, s: c.enter_context(nc.psum_tensor("f_" + n, s, F32))
        sem = lambda n: c.enter_context(nc.semaphore("f_" + n))
        ow = sb("ow", [P, KC, D]); obias = sb("obias", [P, D])
        ot = sb("ot", [P, GT, D]); otT = sb("otT", [P, KC, GTOK]); xn = sb("xn", [P, GT, D])
        xh = sb("xh", [P, 2, KC, GTOK], F32R)
        st = sb("st", [P, GT, 6]); mv = sb("mv", [P, GT, 2])
        ve = sb("ve", [P, GT]); ti = sb("ti", [P, GT], I32); tj = sb("tj", [P, GT], I32); tt = sb("tt", [P, GT])
        rs = sb("rs", [P, GT]); nm = sb("nm", [P, GT])
        sg = sb("sg", [P, 2, GTOK]); hf = sb("hf", [P, 2, GTOK]); hp = sb("hp", [P, 2, 2, GTOK], F32R)
        yo = sb("yo", [P, GT, D])
        psT = ps("psT", [P, KC, GTOK]); psY = ps("psY", [P, GT, D])
        psG = [ps(f"psG{i}", [P, GTOK]) for i in range(2)]; psU = [ps(f"psU{i}", [P, GTOK]) for i in range(2)]
        psP = psT[:].rearrange("p k (j c) -> p (k j) c", c=D)
        w_loaded = sem("w_loaded"); chain = sem("chain")
        gathered = sem("gathered"); turned_o = sem("turned_o"); kept_o = sem("kept_o"); biased = sem("biased"); projected = sem("projected")
        stats = sem("stats"); normed = sem("normed"); turned = sem("turned"); high = sem("high"); low = sem("low")
        g_done = sem("g_done"); silu_done = sem("silu_done"); h_done = sem("h_done"); hh_done = sem("hh_done"); hl_done = sem("hl_done")
        down_done = sem("down_done"); y_done = sem("y_done"); stored = sem("stored")
        block = c.enter_context(nc.Block())
        GB = NG // B

        def groups(eng, first, step):
            o2 = lambda b, i: O2[:, b * H:(b + 1) * H, bass.ds(i * GT, GT), :]
            first(0, o2(0, 0))
            for b in range(B):
                with eng.Fori(0, GB - 1) as i:
                    step(i + b * GB, (i + (b * GB + 1), o2(b, i + 1)))
                step(b * GB + GB - 1, ((b + 1) * GB, o2(b + 1, 0)) if b < B - 1 else None)

        @block.sync
        def _(sp):
            sp.dma_start(ow[:], W["owT"].rearrange("(k p) n -> p k n", p=P)).then_inc(w_loaded, 16)
            sp.dma_start(obias[:], W["out_b"].to_broadcast([P, D])).then_inc(w_loaded, 16)
            with sp.Fori(0, NG) as g:
                sp.wait_ge(y_done, g + 2)
                sp.dma_start(out[bass.ds(g * GTOK, GTOK)].rearrange("(j p) c -> p j c", p=P), yo[:]).then_inc(stored, 16)
            sp.wait_ge(stored, NG * 16 + 16)

        @block.gpsimd
        def _(pool):
            pool.wait_ge(w_loaded, 32)
            with pool.Fori(0, NG) as g:
                xs = X[:, bass.ds(g * GT, GT)]
                nc.gpsimd.tensor_tensor(xs, xs, obias[:].unsqueeze(1).to_broadcast([P, GT, D]), ALU.add).then_inc(biased, 1)

        @block.scalar
        def _(act):
            a = nc.scalar

            def gather(g, o2):
                a.activation(ot[:].rearrange("p t (h e) -> p t h e", h=H), o2.rearrange("p h t e -> p t h e"), ACT.Copy).then_inc(gathered, 1)

            def keep(g):
                act.wait_ge(turned_o, g + 1)
                a.activation(otT[:], psT[:], ACT.Copy).then_inc(kept_o, 1)

            def norm(g):
                act.wait_ge(stats, g + 1)
                for j in range(GT):
                    last = a.activation(xn[:, j], X[:, bass.ds(g * GT + j, 1)].rearrange("p a c -> p (a c)"), ACT.Identity,
                                        bias=nm[:, j:j + 1], scale=rs[:, j:j + 1])
                last.then_inc(normed, 1)

            def round_high(g):
                act.wait_ge(turned, g + 1)
                a.activation(xh[:, 0], psT[:], ACT.Copy).then_inc(high, 1)

            def first(g, o2):
                gather(g, o2)
                keep(g)
                norm(g)
                round_high(g)

            def step(g, after):
                for m in range(HC):
                    act.wait_ge(g_done, g * HC + (m + 1))
                    a.activation(sg[:, m % 2], psG[m % 2][:], ACT.Silu, scale=FSCALE).then_inc(silu_done, 1)
                    if after and m == HC - 1:
                        round_high(after[0])
                    act.wait_ge(h_done, g * HC + (m + 3))
                    act.wait_ge(down_done, g * HC + (m + 1))
                    a.activation(hp[:, m % 2, 0], hf[:, m % 2], ACT.Copy).then_inc(hh_done, 1)
                    if after and m == 0:
                        gather(*after)
                    if after and m == 1:
                        keep(after[0])
                    if after and m == 3:
                        norm(after[0])

            groups(act, first, step)

        @block.vector
        def _(dve):
            v = nc.vector
            ch = Chain(dve, chain)
            dve.sem_inc(stored, 16)
            dve.sem_inc(y_done, 1)
            dve.sem_inc(h_done, 2)

            def residual(g):
                xs = X[:, bass.ds(g * GT, GT)]
                dve.wait_ge(biased, g + 1)
                dve.wait_ge(projected, g + 1)
                ch.link(v.tensor_tensor(xs, xs, psP, ALU.add))
                for j in range(GT):
                    last = v.bn_stats(st[:, j], X[:, bass.ds(g * GT + j, 1)].rearrange("p a c -> p (a c)"))
                return last

            def moments(g, after_stats):
                ch.link(after_stats)
                for j in range(GT):
                    last = v.bn_aggr(mv[:, j], st[:, j])
                ch.link(last)
                rstd(v, ch, mv[:], ve[:], ti[:], tj[:], tt[:], rs[:], nm[:]).then_inc(stats, 1)

            def round_low(g):
                dve.wait_ge(high, g + 1)
                v.tensor_tensor(xh[:, 1], psT[:], xh[:, 0], ALU.subtract).then_inc(low, 1)

            def first(g, o2):
                moments(g, residual(g))
                round_low(g)
                ch.clear()

            def step(g, after):
                for m in range(HC):
                    dve.wait_ge(silu_done, g * HC + (m + 1))
                    v.tensor_tensor(hf[:, m % 2], psU[m % 2][:], sg[:, m % 2], ALU.mult).then_inc(h_done, 1)
                    if after and m == HC - 1:
                        round_low(after[0])
                    dve.wait_ge(hh_done, g * HC + (m + 1))
                    v.tensor_tensor(hp[:, m % 2, 1], hf[:, m % 2], hp[:, m % 2, 0], ALU.subtract).then_inc(hl_done, 1)
                    if after and m == 2:
                        moments(after[0], residual(after[0]))
                dve.wait_ge(down_done, g * HC + (HC + 2))
                dve.wait_ge(stored, g * 16 + 16)
                v.scalar_tensor_tensor(yo[:].rearrange("p t c -> p (t c)"), psY[:].rearrange("p t c -> p (t c)"), FSCALE * FSCALE,
                                       X[:, bass.ds(g * GT, GT)].rearrange("p t c -> p (t c)"), ALU.mult, ALU.add).then_inc(y_done, 1)
                ch.clear()

            groups(dve, first, step)

        @block.tensor
        def _(pe):
            t = nc.tensor
            pe.wait_ge(w_loaded, 32)
            pe.sem_inc(down_done, 2)

            def turn(src, signal):
                for k in range(KC):
                    for j in range(GT):
                        last = t.transpose(psT[:, k, j * P:(j + 1) * P], src[:, j, k * P:(k + 1) * P], ident[:])
                last.then_inc(signal, 1)

            def turn_output(g):
                pe.wait_ge(gathered, g + 1)
                turn(ot, turned_o)

            def project(g):
                pe.wait_ge(kept_o, g + 1)
                for j in range(GT):
                    for k in range(KC):
                        last = t.matmul(psP[:, j], otT[:, k, j * P:(j + 1) * P], ow[:, k], start=(k == 0), stop=(k == KC - 1))
                last.then_inc(projected, 1)

            def turn_normed(g):
                pe.wait_ge(normed, g + 1)
                turn(xn, turned)

            def first(g, o2):
                turn_output(g)
                project(g)
                turn_normed(g)

            def step(g, after):
                def up(m):
                    pe.wait_ge(h_done, g * HC + (m + 1))
                    for w, o in ((wg, psG[m % 2]), (wu, psU[m % 2])):
                        n = 0
                        for k in range(KC):
                            for part in range(2):
                                last = t.matmul(o[:], w[:, k, m * P:(m + 1) * P], xh[:, part, k], start=(n == 0), stop=(n == 2 * KC - 1))
                                n += 1
                    last.then_inc(g_done, 1)

                def down(m):
                    pe.wait_ge(hl_done, g * HC + (m + 1))
                    if m == 0:
                        pe.wait_ge(y_done, g + 1)
                    for j in range(GT):
                        for part in range(2):
                            last = t.matmul(psY[:, j], hp[:, m % 2, part, j * P:(j + 1) * P], wd[:, m],
                                            start=(m == 0 and j % 2 == 0 and part == 0), stop=(m == HC - 1 and part == 1),
                                            skip_group_check=True)
                    last.then_inc(down_done, 1)

                pe.wait_ge(low, g + 1)
                for m in range(HC):
                    up(m)
                    if after and m == HC - 1:
                        turn_normed(after[0])
                    if m >= 1:
                        down(m - 1)
                    if after and m == 1:
                        turn_output(after[0])
                    if after and m == 2:
                        project(after[0])
                down(HC - 1)

            groups(pe, first, step)


def build(nc, a, out):
    scratch = lambda n, s, dt=F32: nc.dram_tensor(n, s, dt, kind="Internal").ap()
    with ExitStack() as c:
        sb = lambda n, s, dt=F32: c.enter_context(nc.sbuf_tensor(n, s, dt))
        T = {"ident_in": a["ident"]}
        T["X"] = sb("X", [P, NT, D])
        T["ident"] = sb("ident", [P, P])
        T["lam_c"] = sb("lam_c", [P, 1])
        kh = scratch("kh", (H, BL, d)); vh = scratch("vh", (H, BL, d))
        kd = scratch("kd", (H, BL, d)); kt = scratch("kt", (H, BL, d))
        tm = scratch("tm", (H, BL // C, C * C)); vg = scratch("vg", (H, VG, BL, VW)); w1 = scratch("w1", (H, BL))
        ug = scratch("ug", (H, VG, BL, VW)); yd = scratch("yd", (BL, D))
        xp = scratch("xp", (3, B, D, L), BF16); qp = scratch("qp", (3, B, D, L), BF16); vx = scratch("vx", (NH, P, KT, 32))
        phase_a(nc, T, a["x"], a["wT"], kh, vh)
        phase_b(nc, T, a["eta"], a["lam_logit"], kh, vh, kd, kt, tm, vg, w1)
        phase_c(nc, T, a, kd, kt, tm, vg, vh, w1, ug, yd, xp, qp, vx)
        T["O2"] = sb("O2", [P, NH, KT, d])
        T["wg"] = sb("wg", [P, KC, HID], F32R); T["wu"] = sb("wu", [P, KC, HID], F32R); T["wd"] = sb("wd", [P, HC, D], F32R)
        phase_e(nc, T, a, xp, qp, vx)
        phase_f(nc, T, a, out)


def laid_out(i):
    wa = np.zeros((D, P), np.float32)
    for h in range(H):
        hh = h % (P // d)
        wa[h * d:(h + 1) * d, hh * d:(hh + 1) * d] = i["L1_attn_w_att_val"][h]
    return {
        "x": i["L0_attn_x"].reshape(BL, D),
        "wT": i["L0_attn_W"].T,
        "gamma": i["L0_attn_ln_gamma"].reshape(1, D),
        "beta": i["L0_attn_ln_beta"].reshape(1, D),
        "eta": i["L0_attn_eta"].reshape(1, 1),
        "lam_logit": i["L0_attn_lam_logit"].reshape(1, 1),
        "gwT": i["L0_ffn_gate_weight"].T,
        "bias": i["L0_ffn_e_score_correction_bias"].reshape(1, NE),
        "wgT": i["L0_ffn_gate_proj"].transpose(2, 0, 1),
        "wuT": i["L0_ffn_up_proj"].transpose(2, 0, 1),
        "wdT": i["L0_ffn_down_proj"].transpose(2, 0, 1),
        "wa": wa,
        "wvT": i["L1_attn_wv_w"].T,
        "wv_b": i["L1_attn_wv_b"].reshape(1, D),
        "owT": i["L1_attn_out_w"].T,
        "out_b": i["L1_attn_out_b"].reshape(1, D),
        "fgT": i["L1_ffn_w_gate"].T,
        "fuT": i["L1_ffn_w_up"].T,
        "fdT": i["L1_ffn_w_down"].T,
        "ident": np.eye(P, dtype=np.float32),
        "low": np.tril(np.ones((NE, NE), np.float32), -1).reshape(1, NE * NE),
    }


def kernel(**inputs):
    import concourse.bacc as _bacc
    from concourse.bass_utils import run_bass_kernel_spmd as _run

    nc = _bacc.Bacc("TRN2", target_bir_lowering=False, num_devices=1)
    arrays = {f"in_{n}": np.ascontiguousarray(v) for n, v in laid_out({n: np.asarray(v) for n, v in inputs.items()}).items()}
    args = {n[3:]: nc.dram_tensor(n, v.shape, mybir.dt.from_np(v.dtype), kind="ExternalInput").ap() for n, v in arrays.items()}
    out = nc.dram_tensor("out", (BL, D), F32, kind="ExternalOutput").ap()
    build(nc, args, out)
    r = _run(nc, [arrays], core_ids=[0])
    return r.results[0]["out"].reshape(B, L, D)
```
